# Optimizing a Trainium2 kernel written in Bass

```python
import numpy as np
import jax
import jax.numpy as jnp

def _softmax(x, axis=-1):
    return jax.nn.softmax(x, axis=axis)

def _gelu(x):
    return jax.nn.gelu(x, approximate=True)

def _silu(x):
    return jax.nn.silu(x)

def _sigmoid(x):
    return jax.nn.sigmoid(x)

def _layernorm(x, axis=-1, eps=1e-05):
    m = jnp.mean(x, axis=axis, keepdims=True)
    v = jnp.var(x, axis=axis, keepdims=True)
    return (x - m) / jnp.sqrt(v + eps)

def _scatter_add(tgt, idx, src, axis=0):
    return tgt.at[idx].add(src)

def _segment_sum(src, seg, n):
    return jax.ops.segment_sum(src, seg, n)
kernel_name = 'mk_recurrent_d1_jaxref_r8_dae844'

def setup_inputs(seed: int=0):
    np.random.seed(seed)
    _w = jnp.asarray

    def _L0_attn_setup():
        import jax, jax.numpy as jnp
        import numpy as np
        D_MODEL = 128
        D_STATE = 128
        D_CONV = 4
        EXPAND = 2
        HEADDIM = 64
        D_INNER = D_MODEL * EXPAND
        NHEADS = D_INNER // HEADDIM
        CONV_DIM = D_INNER + 2 * D_STATE
        D_IN_PROJ = 2 * D_INNER + 2 * D_STATE + NHEADS
        POOL = 50
        SDIM = 64
        HEAD_DIM_RET = SDIM // 4
        TAU1 = 0.5
        TAU2 = 0.3
        HID = D_MODEL // 4
        B = 4
        T = 256
        EPS = 1e-05

        def _rmsnorm(x, w):
            return x * jax.lax.rsqrt(jnp.mean(x * x, axis=-1, keepdims=True) + EPS) * w

        def _mamba2(x, in_w, conv_w, conv_b, dt_bias, A_log, D_param, gnorm_w, out_w):
            Bn, Tn, _ = x.shape
            zxbcdt = x @ in_w.T
            z = zxbcdt[..., :D_INNER]
            xBC = zxbcdt[..., D_INNER:D_INNER + CONV_DIM]
            dt = zxbcdt[..., D_INNER + CONV_DIM:]
            xp = jnp.pad(jnp.transpose(xBC, (0, 2, 1)), ((0, 0), (0, 0), (D_CONV - 1, 0)))
            conv = jax.lax.conv_general_dilated(xp, conv_w[:, None, :], (1,), 'VALID', dimension_numbers=('NCH', 'OIH', 'NCH'), feature_group_count=CONV_DIM)
            xBC = jax.nn.silu(jnp.transpose(conv, (0, 2, 1)) + conv_b)
            xs = xBC[..., :D_INNER].reshape(Bn, Tn, NHEADS, HEADDIM)
            Bm = xBC[..., D_INNER:D_INNER + D_STATE]
            Cm = xBC[..., D_INNER + D_STATE:]
            dt = jax.nn.softplus(dt + dt_bias)
            A = -jnp.exp(A_log)
            dA = jnp.exp(dt * A)
            dtx = dt[..., None] * xs

            def step(h, inp):
                dA_t, dtx_t, B_t, C_t = inp
                h = h * dA_t[:, :, None, None] + dtx_t[..., None] * B_t[:, None, None, :]
                y = jnp.einsum('bhpn,bn->bhp', h, C_t)
                return (h, y)
            tm = lambda a: jnp.moveaxis(a, 1, 0)
            h0 = jnp.zeros((Bn, NHEADS, HEADDIM, D_STATE), x.dtype)
            _, ys = jax.lax.scan(step, h0, (tm(dA), tm(dtx), tm(Bm), tm(Cm)))
            y = jnp.moveaxis(ys, 0, 1) + D_param[None, None, :, None] * xs
            y = y.reshape(Bn, Tn, D_INNER)
            y = _rmsnorm(y * jax.nn.silu(z), gnorm_w)
            return y @ out_w.T

        def _update_memory(tokens, imp, summ_w, pool, prio, counts):
            Bn, Tn, Dm = tokens.shape
            S = min(Tn, POOL)
            order = jnp.argsort(-imp, axis=1)[:, :S]
            s_imp = jnp.take_along_axis(imp, order, axis=1)
            s_tok = jnp.take_along_axis(tokens, order[..., None], axis=1)
            s_sum = s_tok @ summ_w.T
            s_mask = s_imp > TAU1
            ar = jnp.arange(Bn)

            def body(carry, inp):
                pool, prio, counts = carry
                hi, si, ss = inp
                add = hi & (counts < POOL)
                idx = jnp.minimum(counts, POOL - 1)
                pool = pool.at[ar, idx].set(jnp.where(add[:, None], ss, pool[ar, idx]))
                prio = prio.at[ar, idx].set(jnp.where(add, si, prio[ar, idx]))
                counts = counts + add.astype(counts.dtype)
                repl = hi & (counts >= POOL)
                mi = jnp.argmin(prio, axis=1)
                should = repl & (si > prio[ar, mi])
                pool = pool.at[ar, mi].set(jnp.where(should[:, None], ss, pool[ar, mi]))
                prio = prio.at[ar, mi].set(jnp.where(should, si, prio[ar, mi]))
                return ((pool, prio, counts), None)
            xs = (jnp.moveaxis(s_mask, 1, 0), jnp.moveaxis(s_imp, 1, 0), jnp.moveaxis(s_sum, 1, 0))
            (pool, prio, counts), _ = jax.lax.scan(body, (pool, prio, counts), xs)
            return (pool, prio, counts)
        key = jax.random.key(seed)
        ks = jax.random.split(key, 16)

        def w(k, shape, fan_in):
            return jax.random.normal(k, shape, dtype=jnp.float32) / np.float32(np.sqrt(fan_in))
        inp = {}
        inp['x'] = jax.random.normal(ks[0], (B, T, D_MODEL), dtype=jnp.float32)
        inp['norm_w'] = jnp.ones((D_MODEL,), jnp.float32)
        inp['in_w'] = w(ks[1], (D_IN_PROJ, D_MODEL), D_MODEL)
        inp['conv_w'] = w(ks[2], (CONV_DIM, D_CONV), D_CONV)
        inp['conv_b'] = jnp.zeros((CONV_DIM,), jnp.float32)
        inp['dt_bias'] = jnp.log(jnp.expm1(jax.random.uniform(ks[3], (NHEADS,), minval=0.001, maxval=0.1))).astype(jnp.float32)
        inp['A_log'] = jnp.log(jax.random.uniform(ks[4], (NHEADS,), minval=1.0, maxval=16.0)).astype(jnp.float32)
        inp['D_param'] = jnp.ones((NHEADS,), jnp.float32)
        inp['gnorm_w'] = jnp.ones((D_INNER,), jnp.float32)
        inp['out_w'] = w(ks[5], (D_MODEL, D_INNER), D_INNER)
        inp['scorer_w1'] = w(ks[6], (HID, D_MODEL), D_MODEL)
        inp['scorer_w2'] = w(ks[7], (1, HID), HID)
        inp['summ_w'] = w(ks[8], (SDIM, D_MODEL), D_MODEL)
        inp['q_w'] = w(ks[9], (SDIM, D_MODEL), D_MODEL)
        inp['k_w'] = w(ks[10], (SDIM, SDIM), SDIM)
        inp['v_w'] = w(ks[11], (D_MODEL, SDIM), SDIM)
        inp['gate_w'] = w(ks[12], (D_MODEL, 2 * D_MODEL), 2 * D_MODEL)
        return inp
    _L0_attn_in = _L0_attn_setup()

    def _L0_ffn_setup():
        import jax, jax.numpy as jnp
        import numpy as np
        import math
        D_IN = 128
        FEATURES = (512, 512, 128)
        BATCH, SEQ = (8, 256)

        def _conn_dense(kernel_bool, x):
            w = jnp.where(kernel_bool, jnp.float32(1.0), jnp.float32(-1.0))
            return x @ w
        key = jax.random.key(seed)
        kx, kk0, kk1, kk2 = jax.random.split(key, 4)
        x = jax.random.normal(kx, (BATCH, SEQ, D_IN), dtype=jnp.float32)
        k0 = jax.random.randint(kk0, (2 * D_IN, FEATURES[0]), 0, 2).astype(jnp.bool_)
        k1 = jax.random.randint(kk1, (FEATURES[0], FEATURES[1]), 0, 2).astype(jnp.bool_)
        k2 = jax.random.randint(kk2, (FEATURES[1], FEATURES[2]), 0, 2).astype(jnp.bool_)
        s0 = jnp.asarray(1.0 / math.sqrt(2 * D_IN), dtype=jnp.float32)
        s1 = jnp.asarray(1.0 / math.sqrt(FEATURES[0]), dtype=jnp.float32)
        s2 = jnp.asarray(1.0 / math.sqrt(FEATURES[1]), dtype=jnp.float32)
        return {'x': x, 'k0': k0, 'k1': k1, 'k2': k2, 's0': s0, 's1': s1, 's2': s2}
    _L0_ffn_in = _L0_ffn_setup()
    _d = {'L0_attn_x': _L0_attn_in['x'], 'L0_attn_norm_w': _L0_attn_in['norm_w'], 'L0_attn_in_w': _L0_attn_in['in_w'], 'L0_attn_conv_w': _L0_attn_in['conv_w'], 'L0_attn_conv_b': _L0_attn_in['conv_b'], 'L0_attn_dt_bias': _L0_attn_in['dt_bias'], 'L0_attn_A_log': _L0_attn_in['A_log'], 'L0_attn_D_param': _L0_attn_in['D_param'], 'L0_attn_gnorm_w': _L0_attn_in['gnorm_w'], 'L0_attn_out_w': _L0_attn_in['out_w'], 'L0_attn_scorer_w1': _L0_attn_in['scorer_w1'], 'L0_attn_scorer_w2': _L0_attn_in['scorer_w2'], 'L0_attn_summ_w': _L0_attn_in['summ_w'], 'L0_attn_q_w': _L0_attn_in['q_w'], 'L0_attn_k_w': _L0_attn_in['k_w'], 'L0_attn_v_w': _L0_attn_in['v_w'], 'L0_attn_gate_w': _L0_attn_in['gate_w'], 'L0_ffn_k0': _L0_ffn_in['k0'], 'L0_ffn_k1': _L0_ffn_in['k1'], 'L0_ffn_k2': _L0_ffn_in['k2'], 'L0_ffn_s0': _L0_ffn_in['s0'], 'L0_ffn_s1': _L0_ffn_in['s1'], 'L0_ffn_s2': _L0_ffn_in['s2']}
    _x0 = _d['L0_attn_x']
    _d['L0_attn_x'] = jax.random.normal(jax.random.fold_in(jax.random.key(seed), 1), (16, 256, 128), dtype=_x0.dtype)
    del _x0
    return _d

def reference(L0_attn_x, L0_attn_norm_w, L0_attn_in_w, L0_attn_conv_w, L0_attn_conv_b, L0_attn_dt_bias, L0_attn_A_log, L0_attn_D_param, L0_attn_gnorm_w, L0_attn_out_w, L0_attn_scorer_w1, L0_attn_scorer_w2, L0_attn_summ_w, L0_attn_q_w, L0_attn_k_w, L0_attn_v_w, L0_attn_gate_w, L0_ffn_k0, L0_ffn_k1, L0_ffn_k2, L0_ffn_s0, L0_ffn_s1, L0_ffn_s2):

    def _L0_attn_ref(x, norm_w, in_w, conv_w, conv_b, dt_bias, A_log, D_param, gnorm_w, out_w, scorer_w1, scorer_w2, summ_w, q_w, k_w, v_w, gate_w):
        import jax, jax.numpy as jnp
        import numpy as np
        D_MODEL = 128
        D_STATE = 128
        D_CONV = 4
        EXPAND = 2
        HEADDIM = 64
        D_INNER = D_MODEL * EXPAND
        NHEADS = D_INNER // HEADDIM
        CONV_DIM = D_INNER + 2 * D_STATE
        D_IN_PROJ = 2 * D_INNER + 2 * D_STATE + NHEADS
        POOL = 50
        SDIM = 64
        HEAD_DIM_RET = SDIM // 4
        TAU1 = 0.5
        TAU2 = 0.3
        HID = D_MODEL // 4
        B = 4
        T = 256
        EPS = 1e-05

        def _rmsnorm(x, w):
            return x * jax.lax.rsqrt(jnp.mean(x * x, axis=-1, keepdims=True) + EPS) * w

        def _mamba2(x, in_w, conv_w, conv_b, dt_bias, A_log, D_param, gnorm_w, out_w):
            Bn, Tn, _ = x.shape
            zxbcdt = x @ in_w.T
            z = zxbcdt[..., :D_INNER]
            xBC = zxbcdt[..., D_INNER:D_INNER + CONV_DIM]
            dt = zxbcdt[..., D_INNER + CONV_DIM:]
            xp = jnp.pad(jnp.transpose(xBC, (0, 2, 1)), ((0, 0), (0, 0), (D_CONV - 1, 0)))
            conv = jax.lax.conv_general_dilated(xp, conv_w[:, None, :], (1,), 'VALID', dimension_numbers=('NCH', 'OIH', 'NCH'), feature_group_count=CONV_DIM)
            xBC = jax.nn.silu(jnp.transpose(conv, (0, 2, 1)) + conv_b)
            xs = xBC[..., :D_INNER].reshape(Bn, Tn, NHEADS, HEADDIM)
            Bm = xBC[..., D_INNER:D_INNER + D_STATE]
            Cm = xBC[..., D_INNER + D_STATE:]
            dt = jax.nn.softplus(dt + dt_bias)
            A = -jnp.exp(A_log)
            dA = jnp.exp(dt * A)
            dtx = dt[..., None] * xs

            def step(h, inp):
                dA_t, dtx_t, B_t, C_t = inp
                h = h * dA_t[:, :, None, None] + dtx_t[..., None] * B_t[:, None, None, :]
                y = jnp.einsum('bhpn,bn->bhp', h, C_t)
                return (h, y)
            tm = lambda a: jnp.moveaxis(a, 1, 0)
            h0 = jnp.zeros((Bn, NHEADS, HEADDIM, D_STATE), x.dtype)
            _, ys = jax.lax.scan(step, h0, (tm(dA), tm(dtx), tm(Bm), tm(Cm)))
            y = jnp.moveaxis(ys, 0, 1) + D_param[None, None, :, None] * xs
            y = y.reshape(Bn, Tn, D_INNER)
            y = _rmsnorm(y * jax.nn.silu(z), gnorm_w)
            return y @ out_w.T

        def _update_memory(tokens, imp, summ_w, pool, prio, counts):
            Bn, Tn, Dm = tokens.shape
            S = min(Tn, POOL)
            order = jnp.argsort(-imp, axis=1)[:, :S]
            s_imp = jnp.take_along_axis(imp, order, axis=1)
            s_tok = jnp.take_along_axis(tokens, order[..., None], axis=1)
            s_sum = s_tok @ summ_w.T
            s_mask = s_imp > TAU1
            ar = jnp.arange(Bn)

            def body(carry, inp):
                pool, prio, counts = carry
                hi, si, ss = inp
                add = hi & (counts < POOL)
                idx = jnp.minimum(counts, POOL - 1)
                pool = pool.at[ar, idx].set(jnp.where(add[:, None], ss, pool[ar, idx]))
                prio = prio.at[ar, idx].set(jnp.where(add, si, prio[ar, idx]))
                counts = counts + add.astype(counts.dtype)
                repl = hi & (counts >= POOL)
                mi = jnp.argmin(prio, axis=1)
                should = repl & (si > prio[ar, mi])
                pool = pool.at[ar, mi].set(jnp.where(should[:, None], ss, pool[ar, mi]))
                prio = prio.at[ar, mi].set(jnp.where(should, si, prio[ar, mi]))
                return ((pool, prio, counts), None)
            xs = (jnp.moveaxis(s_mask, 1, 0), jnp.moveaxis(s_imp, 1, 0), jnp.moveaxis(s_sum, 1, 0))
            (pool, prio, counts), _ = jax.lax.scan(body, (pool, prio, counts), xs)
            return (pool, prio, counts)
        residual = x
        xn = _rmsnorm(x, norm_w)
        y = _mamba2(xn, in_w, conv_w, conv_b, dt_bias, A_log, D_param, gnorm_w, out_w)
        h = jax.nn.relu(y @ scorer_w1.T)
        scores = jax.nn.sigmoid((h @ scorer_w2.T)[..., 0])
        Bn = x.shape[0]
        pool = jnp.zeros((Bn, POOL, SDIM), x.dtype)
        prio = jnp.zeros((Bn, POOL), x.dtype)
        counts = jnp.zeros((Bn,), jnp.int32)
        pool, prio, counts = _update_memory(y, scores, summ_w, pool, prio, counts)
        mean_score = jnp.mean(scores, axis=1)
        retrieve_mask = (mean_score > TAU2) & (counts > 0)
        memory_mask = jnp.arange(POOL)[None, :] < counts[:, None]
        q = y @ q_w.T
        k = pool @ k_w.T
        v = pool @ v_w.T
        scale = np.float32(1.0 / np.sqrt(HEAD_DIM_RET))
        logits = jnp.einsum('btd,bpd->btp', q, k) * scale
        logits = jnp.where(memory_mask[:, None, :], logits, jnp.float32(-1000000000.0))
        attn = jax.nn.softmax(logits, axis=-1)
        retrieved = jnp.einsum('btp,bpd->btd', attn, v)
        gate = jax.nn.sigmoid(jnp.concatenate([y, retrieved], axis=-1) @ gate_w.T)
        y = y + gate * retrieved * retrieve_mask[:, None, None].astype(y.dtype)
        return residual + y

    def _L0_ffn_ref(x, k0, k1, k2, s0, s1, s2):
        import jax, jax.numpy as jnp
        import numpy as np
        import math
        D_IN = 128
        FEATURES = (512, 512, 128)
        BATCH, SEQ = (8, 256)

        def _conn_dense(kernel_bool, x):
            w = jnp.where(kernel_bool, jnp.float32(1.0), jnp.float32(-1.0))
            return x @ w
        h = jnp.concatenate([x, -x], axis=-1)
        h = s0 * _conn_dense(k0, h)
        h = jax.nn.relu(h) * 2
        h = s1 * _conn_dense(k1, h)
        h = jax.nn.relu(h) * 2
        h = s2 * _conn_dense(k2, h)
        return h
    x = L0_attn_x
    xn = _layernorm(x, axis=-1)
    s = _L0_attn_ref(xn, L0_attn_norm_w, L0_attn_in_w, L0_attn_conv_w, L0_attn_conv_b, L0_attn_dt_bias, L0_attn_A_log, L0_attn_D_param, L0_attn_gnorm_w, L0_attn_out_w, L0_attn_scorer_w1, L0_attn_scorer_w2, L0_attn_summ_w, L0_attn_q_w, L0_attn_k_w, L0_attn_v_w, L0_attn_gate_w)
    g = _silu(_L0_ffn_ref(xn, L0_ffn_k0, L0_ffn_k1, L0_ffn_k2, L0_ffn_s0, L0_ffn_s1, L0_ffn_s2))
    x = x + s * g
    return x

_drawn_inputs = setup_inputs


def setup_inputs(seed=0):
    import zlib

    import numpy as np

    out = dict(_drawn_inputs(seed))
    spreads = {'L0_attn_norm_w': (1.0, 0.2),
     'L0_attn_conv_b': (0.0, 0.1),
     'L0_attn_D_param': (1.0, 0.2),
     'L0_attn_gnorm_w': (1.0, 0.2)}
    factors = {}
    for name, (base, spread) in spreads.items():
        noise = np.random.default_rng([zlib.crc32(name.encode()), seed]).standard_normal(out[name].shape)
        drawn = base * np.exp(spread * noise) if base else spread * noise
        out[name] = jnp.asarray(drawn.astype(out[name].dtype))
    for name, factor in factors.items():
        out[name] = (out[name] * factor).astype(out[name].dtype)
    return out
```

```python
import concourse.bass as bass
from concourse import mybir
from contextlib import ExitStack

P = 128
NB, T, D = 16, 256, 128
TJ = T // P
HEADS, HD, NSTATE = 4, 64, 128
DI = HEADS * HD
CONV = DI + 2 * NSTATE
CB = CONV // P
TAPS = 4
PAD = TAPS - 1
NIN = 2 * DI + 2 * NSTATE + HEADS
POOL, SDIM, HID = 50, 64, 32
FF = 512
FB = FF // P
EPS = 1e-5
WS = 64.0
H2S = 16.0
SATURATED = 16.635532
ATANH_TERMS = 8
NEG = -1.0e30
NUMS = {"-1/2": -0.5, "1/2": 0.5, "eps": EPS, "-1": -1.0, "1": 1.0, "2": 2.0, "1/8": 0.125, "1/DI": 1.0 / DI,
        "rms eps": EPS * (2 * WS) ** 2, **{f"atanh{i}": 2.0 / (2 * i + 1) for i in range(ATANH_TERMS)}}


def layer_kernel(nc, x, norm_w, in_w, conv_w, conv_b, dt_bias, A_log, D_param, gnorm_w, out_w,
                 scorer_w1, scorer_w2, summ_w, q_w, k_w, v_w, gate_w, k0, k1, k2, s0, s1, s2, out):
    f32, f16, bf16, u8 = mybir.dt.float32, mybir.dt.float16, mybir.dt.bfloat16, mybir.dt.uint8
    ALU = mybir.AluOpType
    ACT = mybir.ActivationFunctionType
    AX = mybir.AxisListType.X

    x_v = x.rearrange("b (j p) d -> b p j d", p=P)
    out_v = out.rearrange("b (j p) d -> b p j d", p=P)

    importance = nc.dram_tensor("importance", (NB, T), f32, kind="Internal").ap()

    ctx = ExitStack()
    with ctx:
        def sb(name, shape, dt=f32):
            return ctx.enter_context(nc.sbuf_tensor(name, shape, dt))

        def sem(name):
            return ctx.enter_context(nc.semaphore(name))

        inw_ld = sb("inw_ld", [P, 6, D])
        dtw_ld = sb("dtw_ld", [HEADS, D])
        outw_ld = sb("outw_ld", [P, DI])
        sw1_ld = sb("sw1_ld", [HID, D])
        gatew_ld = sb("gatew_ld", [P, 2 * D])
        kw_ld = sb("kw_ld", [SDIM, SDIM])
        vw_ld = sb("vw_ld", [P, SDIM])
        summ_sb = sb("summ_sb", [SDIM, D])
        qw_sb = sb("qw_sb", [SDIM, D])
        sw2_ld = sb("sw2_ld", [HID, 1])
        sw2_bc = sb("sw2_bc", [HID, P])
        k0_ld = sb("k0_ld", [P, 2, FF], u8)
        k1_ld = sb("k1_ld", [P, FB, FF], u8)
        k2_ld = sb("k2_ld", [P, FB, D], u8)
        nw_col = sb("nw_col", [P, 1])
        gw_col = sb("gw_col", [P, TJ])
        cw_ld = sb("cw_ld", [P, CB, TAPS])
        cb_sb = sb("cb_sb", [P, CB])
        dtb_bc = sb("dtb_bc", [P, HEADS])
        alog_bc = sb("alog_bc", [P, HEADS])
        dpar_bc = sb("dpar_bc", [P, HEADS])
        s_bc = sb("s_bc", [P, 3])
        ident = sb("ident", [P, P])
        ident_bf = sb("ident_bf", [P, P], bf16)
        ones32 = sb("ones32", [P, P])
        ones3 = sb("ones3", [3, P], bf16)
        upto = sb("upto", [P, T])
        mask = sb("mask", [P, HEADS, P], bf16)
        minus_head = sb("minus_head", [3 * HEADS, HEADS, P], bf16)
        slots = sb("slots", [P, POOL])
        nums = sb("nums", [P, len(NUMS)])
        wt32 = sb("wt32", [P, NIN])
        wt_hi = sb("wt_hi", [P, NIN], f16)
        wt_lo = sb("wt_lo", [P, NIN], f16)
        out_wT = sb("out_wT", [P, TJ, D])
        sw1T = sb("sw1T", [P, HID])
        gate1T = sb("gate1T", [P, D])
        gate2T = sb("gate2T", [P, D])
        kwT = sb("kwT", [SDIM, SDIM])
        vwT = sb("vwT", [SDIM, D])
        kp_sb = sb("kp_sb", [SDIM, D])
        wv_sb = sb("wv_sb", [P, D])
        wmT = sb("wmT", [P, D])
        wvv = sb("wvv", [P, 2 * D])
        k0_16 = sb("k0_16", [P, FF], f16)
        k0_d = sb("k0_d", [P, FF])
        k1_16 = sb("k1_16", [P, FB, FF], f16)
        k2_16 = sb("k2_16", [P, FB, D], f16)
        cw = sb("cw", [P, CB, TAPS])
        negA = sb("negA", [P, HEADS])
        aexp = sb("aexp", [P, HEADS])
        dhalf = sb("dhalf", [P, DI])
        sgn = sb("sgn", [P, 3])
        sneg = sb("sneg", [P, 3])
        sabs = sb("sabs", [P, 3])
        sprod = sb("sprod", [P, 1])
        fhalf = sb("fhalf", [P, 2])
        c1 = sb("c1", [P, 1])
        c2 = sb("c2", [P, 1])
        xall = sb("xall", [P, NB, TJ, D])
        yall = sb("yall", [P, NB, TJ, D])
        yTall = sb("yTall", [P, NB, T])
        gall = sb("gall", [P, NB, TJ, D])
        norms = sb("norms", [P, NB, 3, TJ])
        row = sb("row", [1, T])
        st6 = sb("st6", [P, TJ, 6])
        mv = sb("mv", [P, TJ, 2])
        lt = sb("lt", [P, 8, TJ])
        lnw = sb("lnw", [P, 3, TJ])
        xn = sb("xn", [P, TJ, D])
        xT_hi = sb("xT_hi", [P, T], f16)
        xT_lo = sb("xT_lo", [P, T], f16)
        raw = sb("raw", [P, TJ, HEADS])
        sp = sb("sp", [P, 9, TJ * HEADS])
        dt8 = sb("dt8", [P, TJ * HEADS])
        a_sb = sb("a_sb", [P, TJ * HEADS])
        craw = sb("craw", [HEADS, T])
        cres = sb("cres", [HEADS, T])
        parts = sb("parts", [HEADS, 3, T], bf16)
        cum_t = sb("cum_t", [3, HEADS, T], bf16)
        cum_s = sb("cum_s", [3 * HEADS, T], bf16)
        pre = sb("pre", [P, CB, PAD + T])
        acc = sb("acc", [P, CB, T])
        cth = sb("cth", [P, CB, T])
        xbc = sb("xbc", [P, CB, T])
        zth = sb("zth", [P, TJ, DI])
        zg = sb("zg", [P, TJ, DI])
        xtok = sb("xtok", [P, TJ, DI])
        dtx = sb("dtx", [P, TJ, DI])
        xD = sb("xD", [P, TJ, DI])
        decay = sb("decay", [P, 3, HEADS, P])
        mix = sb("mix", [P, 3, HEADS, P])
        ysum = sb("ysum", [P, TJ, DI])
        yg = sb("yg", [P, TJ, DI])
        sq = sb("sq", [P, TJ, DI])
        ss = sb("ss", [P, 2])
        rt = sb("rt", [P, 2])
        rstd = sb("rstd", [P, 2])
        ygT = sb("ygT", [P, TJ, T])
        ybuf = sb("ybuf", [P, TJ, D])
        yTbuf = sb("yTbuf", [P, T])
        hsc = sb("hsc", [HID, T])
        h1_hi = sb("h1_hi", [P, FB, T], f16)
        h1_lo = sb("h1_lo", [P, FB, T], f16)
        h2_hi = sb("h2_hi", [P, FB, T], f16)
        h2_lo = sb("h2_lo", [P, FB, T], f16)
        gth = sb("gth", [P, TJ, D])
        gth1 = sb("gth1", [P, TJ, D])
        keys = sb("keys", [NB, T])
        logit = sb("logit", [NB, T])
        work = sb("work", [NB, 2, T])
        top8 = sb("top8", [NB, 7, 8])
        gt = sb("gt", [NB, T])
        eq = sb("eq", [NB, T])
        eqc = sb("eqc", [NB, T])
        ok = sb("ok", [NB, T])
        sel = sb("sel", [NB, T])
        selc = sb("selc", [NB, T])
        slot = sb("slot", [NB, T])
        zero16 = sb("zero16", [NB, T])
        th16 = sb("th16", [NB, T])
        col = sb("col", [NB, 8])
        diag2 = sb("diag2", [NB, 2, NB])
        slotT = sb("slotT", [P, TJ, NB])
        cnt_rm = sb("cnt_rm", [P, 2, NB])
        yin = sb("yin", [P, 2, TJ, D])
        yTin = sb("yTin", [P, 2, T])
        onehot = sb("onehot", [P, TJ, POOL])
        pbias = sb("pbias", [P, POOL])
        sT = sb("sT", [P, POOL])
        m_sb = sb("m_sb", [P, POOL])
        vv = sb("vv", [POOL, 2 * D])
        lm = sb("lm", [P, TJ, POOL])
        ls = sb("ls", [P, TJ, POOL])
        ex = sb("ex", [P, TJ, POOL])
        at = sb("at", [P, TJ, POOL])
        mx = sb("mx", [P, TJ])
        sm = sb("sm", [P, TJ])
        rec = sb("rec", [P, TJ])
        atT = sb("atT", [POOL, T])
        gate = sb("gate", [P, TJ, D])
        base = sb("base", [P, 3, TJ, D])
        fin = sb("fin", [P, 3, TJ, D])
        obuf = sb("obuf", [P, 2, TJ, D])

        bank = [ctx.enter_context(nc.psum_tensor(f"bank{i}", [P, 512], f32)) for i in range(8)]
        F = [bank[0], bank[1]]
        pA = bank[2]
        pB = bank[3]
        pG = bank[4]
        pS = bank[5]
        pDT = pS[:, 0:TJ * HEADS]
        pY = bank[6]
        pO, pYT = bank[7][:, 0:256], bank[7][:, 256:512]

        S = {n: sem(n) for n in (
            "weights_in", "consts", "w_T", "w_ev", "w_split", "w_mlp", "w_small", "w_dve",
            "w_exp", "pads",
            "stats", "mv_ready", "ln_step", "norm_ready", "norm_kept", "dt8_ready", "xn_ready", "xT_done", "xT_hi_ready",
            "xT_lo_ready", "dt_done", "raw_ready", "sp_step", "abs_ready", "u_ready", "den_ready",
            "rden_ready", "a_ready", "cum_done", "craw_ready", "parts_step", "parts_ready",
            "rows_in", "proj_done", "pre_ready", "conv_step", "cth_ready", "xbc_ready", "z_done",
            "zth_ready", "zg_ready", "xtok_done", "xtok_ready", "x_scaled", "g_done", "seg_done",
            "decay_ready", "mix_ready", "y_done", "ysum_ready", "yg_ready", "ss_ready",
            "rstd_step", "rstd_ready", "ygT_done", "ygT_ready", "yo_done", "y_ready", "yT_done",
            "yT_ready", "h_done", "h_ready", "row_done", "row_ready", "y_saved", "yT_saved",
            "l1_done", "h1_hi_ready", "h1_lo_ready", "l2_done", "h2_hi_ready", "h2_lo_ready",
            "l3_done", "gth_ready", "gth1_ready", "g_ready",
            "keys_in", "row_saved", "sel_step", "slots_done", "th16_ready", "slotT_done", "slotT_ready",
            "onehot_ready", "bias_ready", "s_done", "sT_ready", "m_done", "m_ready", "vv_done",
            "vv_ready", "lg_done", "lm_ready", "max_ready", "ls_ready", "ex_ready", "sum_ready",
            "rec_ready", "at_ready", "atT_done", "atT_ready", "rg_done", "gate_ready",
            "base_step", "fin_step", "out_ready")}
        x_in = [sem("x_in0"), sem("x_in1")]
        y_in = [sem("y_in0"), sem("y_in1")]
        yT_in = [sem("yT_in0"), sem("yT_in1")]
        out_done = [sem("out_done0"), sem("out_done1")]

        ctx.enter_context(nc.allow_non_contiguous_dma(reason="columns of small weights"))
        block = ctx.enter_context(nc.Block())

        def num(name, p, *free):
            c = list(NUMS).index(name)
            a = nums[0:p, c:c + 1]
            for _ in free[1:]:
                a = a.unsqueeze(2)
            return a.broadcast_to([p, *free])

        def steps(eng, step):
            step(0, 0, 0, False)
            step(1, 1, 0, False)
            with eng.Fori(1, NB // 2 - 1) as i:
                step(2 * i, 0, i, False)
                step(2 * i + 1, 1, i, False)
            step(NB - 2, 0, NB // 2 - 1, False)
            step(NB - 1, 1, NB // 2 - 1, True)

        N_W = 22
        N_JOBS = 14
        LN_STEPS, SP_STEPS, PART_STEPS = 10, 2 + 1 + 2 * (ATANH_TERMS - 1) + 1, 2

        @block.sync
        def _(sp_eng):
            def w(dst, src):
                sp_eng.dma_start(dst, src).then_inc(S["weights_in"], 16)

            def load_x(n, par):
                sp_eng.dma_start(xall[:, bass.ds(n, 1), :, :], x_v[bass.ds(n, 1)].rearrange("b p j d -> p b j d")).then_inc(x_in[par], 16)

            sp_eng.dma_start(xall[:, 0:1, :, :], x_v[0:1].rearrange("b p j d -> p b j d")).then_inc(x_in[0], 16)
            w(inw_ld[:, :, :], in_w[0:6 * P, :].rearrange("(c p) d -> p c d", p=P))
            w(dtw_ld[:, :], in_w[6 * P:NIN, :])
            w(outw_ld[:, :], out_w[:, :])
            w(sw1_ld[:, :], scorer_w1[:, :])
            w(gatew_ld[:, :], gate_w[:, :])
            w(kw_ld[:, :], k_w[:, :])
            w(vw_ld[:, :], v_w[:, :])
            w(summ_sb[:, :], summ_w[:, :])
            w(qw_sb[:, :], q_w[:, :])
            w(sw2_ld[:, :], scorer_w2.rearrange("a h -> h a"))
            w(k0_ld[:, :, :], k0.rearrange("(a p) n -> p a n", p=P))
            w(k1_ld[:, :, :], k1.rearrange("(a p) n -> p a n", p=P))
            w(k2_ld[:, :, :], k2.rearrange("(a p) n -> p a n", p=P))
            w(nw_col[:, :], norm_w.rearrange("(p a) -> p a", a=1))
            w(gw_col[:, :], gnorm_w.rearrange("(a p) -> p a", p=P))
            w(cw_ld[:, :, :], conv_w.rearrange("(a p) k -> p a k", p=P))
            w(cb_sb[:, :], conv_b.rearrange("(a p) -> p a", p=P))
            w(dtb_bc[:, :], dt_bias.partition_broadcast(P))
            w(alog_bc[:, :], A_log.partition_broadcast(P))
            w(dpar_bc[:, :], D_param.partition_broadcast(P))
            w(s_bc[:, 0:1], s0.partition_broadcast(P))
            w(s_bc[:, 1:2], s1.partition_broadcast(P))
            w(s_bc[:, 2:3], s2.partition_broadcast(P))
            sp_eng.dma_start(xall[:, 1:2, :, :], x_v[1:2].rearrange("b p j d -> p b j d")).then_inc(x_in[1], 16)

            def relayout(n):
                sp_eng.wait_ge(S["parts_ready"], n + 1)
                for q in range(3):
                    sp_eng.dma_start(cum_t[q:q + 1, :, :], parts[:, q, :]).then_inc(S["rows_in"], 16)
                    sp_eng.dma_start(cum_s[HEADS * q:HEADS * (q + 1), :], parts[:, q, :]).then_inc(S["rows_in"], 16)

            def save_y(b):
                sp_eng.wait_ge(S["y_ready"], 2 * b + 2)
                sp_eng.dma_start(yall[:, bass.ds(b, 1), :, :], ybuf[:, :, :].unsqueeze(1)).then_inc(S["y_saved"], 16)

            relayout(0)

            def step(b, par, half, last):
                if isinstance(b, int):
                    if b + 2 < NB:
                        sp_eng.wait_ge(x_in[par], 16 * (half + 1))
                        load_x(b + 2, par)
                else:
                    sp_eng.wait_ge(x_in[par], 16 * (half + 1))
                    load_x(b + 2, par)
                save_y(b)
                if not last:
                    relayout(b + 1)

            steps(sp_eng, step)

            sp_eng.wait_ge(S["row_saved"], 16 * NB)
            sp_eng.dma_start(logit[:, :], importance[:, :]).then_inc(S["keys_in"], 16)

            def load_y(n, par):
                sp_eng.dma_start(yin[:, par, :, :], yall[:, bass.ds(n, 1), :, :].squeeze(1)).then_inc(y_in[par], 16)
                sp_eng.dma_start(yTin[:, par, :], yTall[:, bass.ds(n, 1), :].squeeze(1)).then_inc(yT_in[par], 16)

            sp_eng.wait_ge(S["y_saved"], 16 * NB)
            sp_eng.wait_ge(S["yT_saved"], 16 * NB)
            load_y(0, 0)
            load_y(1, 1)

            def step2(b, par, half, last):
                sp_eng.wait_ge(S["out_ready"], b + 1)
                if not isinstance(b, int) or b + 2 < NB:
                    load_y(b + 2, par)
                if not isinstance(b, int) or b > 1:
                    sp_eng.wait_ge(out_done[par], 16 * half)
                sp_eng.dma_start(out_v[bass.ds(b, 1)].rearrange("b p j d -> p b j d"), obuf[:, par, :, :].unsqueeze(1)).then_inc(out_done[par], 16)

            steps(sp_eng, step2)
            for par in range(2):
                sp_eng.wait_ge(out_done[par], 16 * NB // 2)

        @block.tensor
        def _(pe):
            mm = nc.tensor.matmul

            pe.wait_ge(S["consts"], 1)
            pe.wait_ge(S["weights_in"], 16 * (N_W + 1))
            jobs = [(inw_ld[:, c, :], P) for c in range(6)] + [(dtw_ld[:, :], HEADS)] \
                + [(outw_ld[:, k * P:(k + 1) * P], P) for k in range(2)] + [(sw1_ld[:, :], HID)] \
                + [(gatew_ld[:, k * D:(k + 1) * D], P) for k in range(2)] + [(kw_ld[:, :], SDIM), (vw_ld[:, :], P)]
            for t, (src, rows) in enumerate(jobs):
                if t >= 8:
                    pe.wait_ge(S["w_ev"], t - 7)
                cols = src.shape[1]
                nc.tensor.transpose(bank[t % 8][0:cols, 0:rows], src, ident[0:rows, 0:rows]).then_inc(S["w_T"], 1)
            pe.wait_ge(S["w_ev"], N_JOBS)
            mm(bank[0][0:SDIM, 0:D], kwT[:, :], summ_sb[:, :], start=True, stop=True).then_inc(S["w_T"], 1)
            mm(bank[1][:, 0:D], summ_sb[:, :], vwT[:, :], start=True, stop=True).then_inc(S["w_T"], 1)
            mm(bank[2][:, 0:D], vwT[:, :], summ_sb[:, :], start=True, stop=True).then_inc(S["w_T"], 1)
            pe.wait_ge(S["w_ev"], N_JOBS + 3)
            mm(bank[3][:, 0:D], kp_sb[:, :], qw_sb[:, :], start=True, stop=True).then_inc(S["w_T"], 1)
            mm(bank[4][:, 0:D], wv_sb[:, :], gate2T[:, :], start=True, stop=True).then_inc(S["w_T"], 1)

            def norm_T(n):
                pe.wait_ge(S["xn_ready"], TJ * (n + 1))
                pe.wait_ge(S["zg_ready"], n)
                for j in range(TJ):
                    nc.tensor.transpose(pA[:, j * P:(j + 1) * P], xn[:, j, :], ident[:, :]).then_inc(S["xT_done"], 1)

            def dt_proj(n):
                pe.wait_ge(S["xT_hi_ready"], n + 1)
                pe.wait_ge(S["xT_lo_ready"], n + 1)
                pe.wait_ge(S["decay_ready"], 3 * n)
                for j in range(TJ):
                    o = pDT[:, j * HEADS:(j + 1) * HEADS]
                    t = slice(j * P, (j + 1) * P)
                    mm(o, xT_hi[:, t], wt_hi[:, 6 * P:NIN], start=True, stop=False)
                    mm(o, xT_hi[:, t], wt_lo[:, 6 * P:NIN], start=False, stop=False)
                    mm(o, xT_lo[:, t], wt_hi[:, 6 * P:NIN], start=False, stop=True).then_inc(S["dt_done"], 1)

            def conv_proj(n, half):
                dst = pB if half else pA
                for i in range(2):
                    c = DI + (2 * half + i) * P
                    o = dst[:, i * T:(i + 1) * T]
                    mm(o, wt_hi[:, c:c + P], xT_hi[:, :], start=True, stop=False)
                    mm(o, wt_hi[:, c:c + P], xT_lo[:, :], start=False, stop=False)
                    mm(o, wt_lo[:, c:c + P], xT_hi[:, :], start=False, stop=True).then_inc(S["proj_done"], 1)

            def z_proj(n):
                pe.wait_ge(S["pre_ready"], 6 * n + 3)
                for j in range(TJ):
                    o = pA[:, j * DI:(j + 1) * DI]
                    t = slice(j * P, (j + 1) * P)
                    mm(o, xT_hi[:, t], wt_hi[:, 0:DI], start=True, stop=False)
                    mm(o, xT_hi[:, t], wt_lo[:, 0:DI], start=False, stop=False)
                    mm(o, xT_lo[:, t], wt_hi[:, 0:DI], start=False, stop=True).then_inc(S["z_done"], 1)

            def cum(n):
                pe.wait_ge(S["a_ready"], n + 1)
                pe.wait_ge(S["row_ready"], n)
                mm(pY[0:HEADS, 0:T], a_sb[:, 0:HEADS], upto[:, :], start=True, stop=False)
                mm(pY[0:HEADS, P:T], a_sb[:, HEADS:2 * HEADS], upto[:, 0:P], start=False, stop=True).then_inc(S["cum_done"], 1)

            def x_by_token(b):
                pe.wait_ge(S["xbc_ready"], 2 * b + 1)
                pe.wait_ge(S["ygT_ready"], b)
                for j in range(TJ):
                    for k in range(2):
                        nc.tensor.transpose(pB[:, j * DI + k * P:j * DI + (k + 1) * P], xbc[:, k, j * P:(j + 1) * P],
                                            ident[:, :]).then_inc(S["xtok_done"], 1)

            def scores(b):
                pe.wait_ge(S["xbc_ready"], 2 * b + 2)
                pe.wait_ge(S["mix_ready"], 3 * b)
                mm(pG[:, 0:T], xbc[:, 2, 0:P], xbc[:, 3, :], start=True, stop=True).then_inc(S["g_done"], 1)
                mm(pG[:, T:T + P], xbc[:, 2, P:T], xbc[:, 3, P:T], start=True, stop=True).then_inc(S["g_done"], 1)

            def segment(b, k):
                s, t = ((0, 0), (0, 1), (1, 1))[k]
                if k == 0:
                    pe.wait_ge(S["rows_in"], 96 * (b + 1))
                    pe.wait_ge(S["raw_ready"], b + 1)
                pe.wait_ge(S["decay_ready"], 3 * b + k)
                o = pS[:, :].rearrange("p (h t) -> p h t", h=HEADS)
                mm(o, ones3[:, :], cum_t[:, :, t * P:(t + 1) * P], start=True, stop=False)
                last = mm(o, cum_s[:, s * P:(s + 1) * P], minus_head[:, :, :], start=False, stop=s != t)
                if s == t:
                    last = mm(o, ident_bf[:, :], mask[:, :, :], start=False, stop=True)
                last.then_inc(S["seg_done"], 1)

            def recur(b):
                pe.wait_ge(S["mix_ready"], 3 * b + 3)
                pe.wait_ge(S["x_scaled"], 2 * b + 1)
                pe.wait_ge(S["craw_ready"], 2 * b + 2)
                for h in range(HEADS):
                    c = slice(h * HD, (h + 1) * HD)
                    mm(pY[:, c], mix[:, 0, h, :], dtx[:, 0, c], start=True, stop=True)
                for h in range(HEADS):
                    c = slice(h * HD, (h + 1) * HD)
                    o = pY[:, DI + h * HD:DI + (h + 1) * HD]
                    mm(o, mix[:, 1, h, :], dtx[:, 0, c], start=True, stop=False)
                    last = mm(o, mix[:, 2, h, :], dtx[:, 1, c], start=False, stop=True)
                last.then_inc(S["y_done"], 1)

            def gated_T(b):
                pe.wait_ge(S["yg_ready"], b + 1)
                for k in range(2):
                    for j in range(TJ):
                        nc.tensor.transpose(pB[:, k * T + j * P:k * T + (j + 1) * P], yg[:, j, k * P:(k + 1) * P],
                                            ident[:, :]).then_inc(S["ygT_done"], 1)

            def out_proj(b):
                pe.wait_ge(S["ygT_ready"], b + 1)
                pe.wait_ge(S["yT_ready"], b)
                for j in range(TJ):
                    o = pO[:, j * D:(j + 1) * D]
                    mm(o, ygT[:, 0, j * P:(j + 1) * P], out_wT[:, 0, :], start=True, stop=False)
                    mm(o, ygT[:, 1, j * P:(j + 1) * P], out_wT[:, 1, :], start=False, stop=True).then_inc(S["yo_done"], 1)

            def y_T(b):
                pe.wait_ge(S["y_ready"], 2 * b + 2)
                for j in range(TJ):
                    nc.tensor.transpose(pYT[:, j * P:(j + 1) * P], ybuf[:, j, :], ident[:, :]).then_inc(S["yT_done"], 1)

            def scorer(b):
                pe.wait_ge(S["yT_ready"], b + 1)
                pe.wait_ge(S["ysum_ready"], b + 1)
                mm(pY[0:HID, 0:T], sw1T[:, :], yTbuf[:, :], start=True, stop=True).then_inc(S["h_done"], 1)
                pe.wait_ge(S["h_ready"], b + 1)
                mm(pY[:, T:2 * T], sw2_bc[:, :], hsc[:, :], start=True, stop=True).then_inc(S["row_done"], 1)

            def layer1(b, half):
                if half == 0:
                    pe.wait_ge(S["xT_hi_ready"], b + 1)
                    pe.wait_ge(S["xT_lo_ready"], b + 1)
                    pe.wait_ge(S["g_ready"], 2 * b)
                else:
                    pe.wait_ge(S["h2_hi_ready"], 2 * b)
                    pe.wait_ge(S["h2_lo_ready"], 2 * b)
                for i in range(2):
                    m = 2 * half + i
                    o = F[half][:, i * T:(i + 1) * T]
                    mm(o, k0_16[:, m * P:(m + 1) * P], xT_hi[:, :], start=True, stop=False)
                    last = mm(o, k0_16[:, m * P:(m + 1) * P], xT_lo[:, :], start=False, stop=True)
                last.then_inc(S["l1_done"], 1)

            def layer2(b, half):
                if half == 0:
                    pe.wait_ge(S["h1_hi_ready"], 2 * b + 2)
                    pe.wait_ge(S["h1_lo_ready"], 2 * b + 2)
                for i in range(2):
                    m = 2 * half + i
                    o = F[half][:, i * T:(i + 1) * T]
                    for k in range(FB):
                        mm(o, k1_16[:, k, m * P:(m + 1) * P], h1_hi[:, k, :], start=k == 0, stop=False)
                        last = mm(o, k1_16[:, k, m * P:(m + 1) * P], h1_lo[:, k, :], start=False, stop=k == FB - 1)
                last.then_inc(S["l2_done"], 1)

            def layer3(b):
                pe.wait_ge(S["h2_hi_ready"], 2 * b + 2)
                pe.wait_ge(S["h2_lo_ready"], 2 * b + 2)
                for j in range(TJ):
                    o = F[0][:, j * D:(j + 1) * D]
                    t = slice(j * P, (j + 1) * P)
                    for k in range(FB):
                        mm(o, h2_hi[:, k, t], k2_16[:, k, :], start=k == 0, stop=False)
                        last = mm(o, h2_lo[:, k, t], k2_16[:, k, :], start=False, stop=k == FB - 1)
                last.then_inc(S["l3_done"], 1)

            pe.wait_ge(S["w_ev"], N_JOBS + 5)
            pe.wait_ge(S["w_split"], 2)
            pe.wait_ge(S["w_mlp"], 4)
            pe.wait_ge(S["consts"], 7)
            norm_T(0)
            dt_proj(0)
            conv_proj(0, 0)
            conv_proj(0, 1)
            z_proj(0)
            cum(0)

            def step(b, par, half, last):
                x_by_token(b)
                scores(b)
                layer1(b, 0)
                layer1(b, 1)
                segment(b, 0)
                if not last:
                    norm_T(b + 1)
                layer2(b, 0)
                segment(b, 1)
                layer2(b, 1)
                segment(b, 2)
                if not last:
                    dt_proj(b + 1)
                    conv_proj(b + 1, 0)
                recur(b)
                if not last:
                    pe.wait_ge(S["xtok_ready"], b + 1)
                    conv_proj(b + 1, 1)
                layer3(b)
                if not last:
                    z_proj(b + 1)
                    pe.wait_ge(S["pre_ready"], 6 * b + 12)
                gated_T(b)
                out_proj(b)
                y_T(b)
                scorer(b)
                if not last:
                    cum(b + 1)

            steps(pe, step)

            pe.wait_ge(S["slots_done"], 1)
            for j in range(TJ):
                nc.tensor.transpose(bank[0][:, j * NB:(j + 1) * NB], slot[:, j * P:(j + 1) * P], ident[0:NB, 0:NB]).then_inc(S["slotT_done"], 1)
            mm(bank[1][:, 0:2 * NB], ones32[0:NB, :], diag2[:, :, :], start=True, stop=True).then_inc(S["slotT_done"], 1)
            pe.wait_ge(S["slotT_ready"], 2)

            def gather(n, par, half):
                pe.wait_ge(S["onehot_ready"], n + 1)
                pe.wait_ge(y_in[par], 16 * (half + 1))
                pe.wait_ge(S["sT_ready"], n)
                for j in range(TJ):
                    last = mm(bank[0][:, 0:POOL], yin[:, par, j, :], onehot[:, j, :], start=j == 0, stop=j == TJ - 1)
                last.then_inc(S["s_done"], 1)

            def pool_vectors(n):
                pe.wait_ge(S["sT_ready"], n + 1)
                pe.wait_ge(S["m_ready"], n)
                mm(bank[1][:, 0:POOL], wmT[:, :], sT[:, :], start=True, stop=True).then_inc(S["m_done"], 1)
                pe.wait_ge(S["vv_ready"], n)
                mm(bank[2][0:POOL, 0:2 * D], sT[:, :], wvv[:, :], start=True, stop=True).then_inc(S["vv_done"], 1)

            def logits(n, par, half):
                pe.wait_ge(S["m_ready"], n + 1)
                pe.wait_ge(yT_in[par], 16 * (half + 1))
                pe.wait_ge(S["lm_ready"], n)
                for j in range(TJ):
                    last = mm(bank[3][:, j * 64:j * 64 + POOL], yTin[:, par, j * P:(j + 1) * P], m_sb[:, :], start=True, stop=True)
                last.then_inc(S["lg_done"], 1)

            def attend(b, par):
                pe.wait_ge(S["at_ready"], b + 1)
                pe.wait_ge(S["atT_ready"], b)
                for j in range(TJ):
                    last = mm(bank[4][0:POOL, j * P:(j + 1) * P], at[:, j, :], ident[:, :], start=True, stop=True)
                last.then_inc(S["atT_done"], 1)
                pe.wait_ge(S["atT_ready"], b + 1)
                pe.wait_ge(S["vv_ready"], b + 1)
                pe.wait_ge(S["fin_step"], 3 * b)
                for j in range(TJ):
                    o = bank[5][:, j * 2 * D:(j + 1) * 2 * D]
                    mm(o, atT[:, j * P:(j + 1) * P], vv[:, :], start=True, stop=False)
                    last = mm(o[:, D:2 * D], yTin[:, par, j * P:(j + 1) * P], gate1T[:, :], start=False, stop=True)
                last.then_inc(S["rg_done"], 1)

            gather(0, 0, 0)
            pool_vectors(0)
            logits(0, 0, 0)

            def step2(b, par, half, last):
                if not last:
                    gather(b + 1, 1 - par, half + par)
                attend(b, par)
                if not last:
                    pool_vectors(b + 1)
                    logits(b + 1, 1 - par, half + par)

            steps(pe, step2)

        @block.scalar
        def _(act):
            go = nc.scalar.activation
            act.wait_ge(S["weights_in"], 16 * (N_W + 1))
            go(aexp[:, :], alog_bc[:, :], ACT.Exp).then_inc(S["w_exp"], 1)
            act.wait_ge(S["w_ev"], 7)
            go(wt_hi[:, :], wt32[:, :], ACT.Copy).then_inc(S["w_split"], 1)

            def xT_high(n):
                act.wait_ge(S["xT_done"], TJ * (n + 1))
                act.wait_ge(S["l1_done"], 2 * n)
                act.wait_ge(S["z_done"], TJ * n)
                go(xT_hi[:, :], pA[:, 0:T], ACT.Copy).then_inc(S["xT_hi_ready"], 1)

            def exp_dt(n):
                act.wait_ge(S["abs_ready"], 2 * n + 2)
                go(sp[:, 2, :], sp[:, 1, :], ACT.Exp).then_inc(S["u_ready"], 1)

            def conv_start(n, half):
                src = pB if half else pA
                act.wait_ge(S["proj_done"], 4 * n + 2 * half + 2)
                act.wait_ge(S["xbc_ready"], 2 * n)
                go(pre[:, 2 * half:2 * half + 2, PAD:], src[:, :].rearrange("p (c t) -> p c t", c=2), ACT.Copy).then_inc(S["pre_ready"], 1)
                for i in range(2):
                    c = 2 * half + i
                    go(acc[:, c, :], src[:, i * T:(i + 1) * T], ACT.Identity, bias=cb_sb[:, c:c + 1],
                       scale=cw[:, c, TAPS - 1:TAPS]).then_inc(S["pre_ready"], 1)

            def conv_tanh(n, half):
                act.wait_ge(S["conv_step"], 12 * n + 6 * half + 6)
                act.wait_ge(S["xbc_ready"], 2 * n)
                go(cth[:, 2 * half:2 * half + 2, :], acc[:, 2 * half:2 * half + 2, :], ACT.Tanh, scale=0.5).then_inc(S["cth_ready"], 1)

            def z_tanh(n):
                act.wait_ge(S["z_done"], TJ * (n + 1))
                act.wait_ge(S["zg_ready"], n)
                go(zth[:, :, :], pA[:, :].rearrange("p (j c) -> p j c", j=TJ), ACT.Tanh, scale=0.5 / WS).then_inc(S["zth_ready"], 1)

            def cum_out(n):
                act.wait_ge(S["cum_done"], n + 1)
                act.wait_ge(S["rows_in"], 96 * n)
                act.wait_ge(S["parts_ready"], n)
                go(parts[:, 0, :], pY[0:HEADS, 0:T], ACT.Copy).then_inc(S["craw_ready"], 1)
                go(craw[:, :], pY[0:HEADS, 0:T], ACT.Copy).then_inc(S["craw_ready"], 1)

            def hidden_high(b, layer, half):
                done, ready = (("l1_done", "h1_hi_ready"), ("l2_done", "h2_hi_ready"))[layer]
                act.wait_ge(S[done], 2 * b + half + 1)
                if half == 0:
                    if layer == 0:
                        act.wait_ge(S["l2_done"], 2 * b)
                    else:
                        act.wait_ge(S["l3_done"], b)
                dst = (h1_hi, h2_hi)[layer]
                go(dst[:, 2 * half:2 * half + 2, :], F[half][:, :].rearrange("p (c t) -> p c t", c=2), ACT.Relu).then_inc(S[ready], 1)

            def decay_exp(b, k):
                act.wait_ge(S["seg_done"], 3 * b + k + 1)
                if k == 0:
                    act.wait_ge(S["mix_ready"], 3 * b)
                go(decay[:, k, :, :], pS[:, :].rearrange("p (h t) -> p h t", h=HEADS), ACT.Exp).then_inc(S["decay_ready"], 1)

            def x_out(b):
                act.wait_ge(S["xtok_done"], 4 * b + 4)
                act.wait_ge(S["x_scaled"], 2 * b)
                go(xtok[:, :, :], pB[:, :].rearrange("p (j c) -> p j c", j=TJ), ACT.Copy).then_inc(S["xtok_ready"], 1)

            def mlp_tanh(b):
                act.wait_ge(S["l3_done"], b + 1)
                act.wait_ge(S["gth1_ready"], b)
                for j in range(TJ):
                    go(gth[:, j, :], F[0][:, j * D:(j + 1) * D], ACT.Tanh,
                       scale=norms[:, bass.ds(b, 1), 2, j:j + 1].squeeze(1)).then_inc(S["gth_ready"], 1)

            def squares(b):
                act.wait_ge(S["yg_ready"], b + 1)
                act.wait_ge(S["rstd_step"], 2 * b)
                for j in range(TJ):
                    go(sq[:, j, :], yg[:, j, :], ACT.Square, accum_out=ss[:, j:j + 1]).then_inc(S["ss_ready"], 1)

            def gated_T_out(b):
                act.wait_ge(S["ygT_done"], 4 * b + 4)
                act.wait_ge(S["yo_done"], 2 * b)
                go(ygT[:, :, :], pB[:, :].rearrange("p (k t) -> p k t", k=2), ACT.Copy).then_inc(S["ygT_ready"], 1)

            def y_out(b):
                act.wait_ge(S["yo_done"], 2 * b + 2)
                act.wait_ge(S["rstd_ready"], b + 1)
                act.wait_ge(S["y_saved"], 16 * b)
                act.wait_ge(S["yT_done"], 2 * b)
                for j in range(TJ):
                    go(ybuf[:, j, :], pO[:, j * D:(j + 1) * D], ACT.Copy, scale=rstd[:, j:j + 1]).then_inc(S["y_ready"], 1)

            def y_T_out(b):
                act.wait_ge(S["yT_done"], 2 * b + 2)
                act.wait_ge(S["yT_saved"], 16 * b)
                act.wait_ge(S["h_done"], b)
                go(yTbuf[:, :], pYT, ACT.Copy).then_inc(S["yT_ready"], 1)

            def scorer_out(b):
                act.wait_ge(S["h_done"], b + 1)
                act.wait_ge(S["row_done"], b)
                go(hsc[:, :], pY[0:HID, 0:T], ACT.Relu).then_inc(S["h_ready"], 1)
                act.wait_ge(S["row_done"], b + 1)
                act.wait_ge(S["yT_ready"], b + 1)
                act.wait_ge(S["row_saved"], 16 * b)
                go(row[:, :], pY[0:1, T:2 * T], ACT.Copy).then_inc(S["row_ready"], 1)
                act.dma_start(yTall[:, bass.ds(b, 1), :], yTbuf[:, :].unsqueeze(1)).then_inc(S["yT_saved"], 16)
                act.wait_ge(S["row_ready"], b + 1)
                act.dma_start(importance[bass.ds(b, 1), :], row[:, :]).then_inc(S["row_saved"], 16)

            act.wait_ge(S["pads"], 1)
            act.wait_ge(S["w_dve"], 1)
            xT_high(0)
            exp_dt(0)
            conv_start(0, 0)
            conv_start(0, 1)
            conv_tanh(0, 0)
            conv_tanh(0, 1)
            z_tanh(0)
            cum_out(0)

            def step(b, par, half, last):
                x_out(b)
                hidden_high(b, 0, 0)
                hidden_high(b, 0, 1)
                decay_exp(b, 0)
                if not last:
                    xT_high(b + 1)
                hidden_high(b, 1, 0)
                decay_exp(b, 1)
                hidden_high(b, 1, 1)
                decay_exp(b, 2)
                if not last:
                    exp_dt(b + 1)
                    conv_start(b + 1, 0)
                    conv_start(b + 1, 1)
                mlp_tanh(b)
                squares(b)
                if not last:
                    z_tanh(b + 1)
                gated_T_out(b)
                if not last:
                    conv_tanh(b + 1, 0)
                y_out(b)
                y_T_out(b)
                if not last:
                    conv_tanh(b + 1, 1)
                scorer_out(b)
                if not last:
                    cum_out(b + 1)

            steps(act, step)

            act.wait_ge(S["keys_in"], 16)
            go(th16[:, :], logit[:, :], ACT.Tanh, scale=0.5, accum_out=col[:, 4:5]).then_inc(S["th16_ready"], 1)

            def pool_out(n):
                act.wait_ge(S["s_done"], n + 1)
                act.wait_ge(S["vv_done"], n)
                go(sT[:, :], bank[0][:, 0:POOL], ACT.Copy).then_inc(S["sT_ready"], 1)
                act.wait_ge(S["m_done"], n + 1)
                act.wait_ge(S["lg_done"], n)
                go(m_sb[:, :], bank[1][:, 0:POOL], ACT.Copy).then_inc(S["m_ready"], 1)
                act.wait_ge(S["vv_done"], n + 1)
                act.wait_ge(S["rg_done"], n)
                go(vv[:, :], bank[2][0:POOL, 0:2 * D], ACT.Copy).then_inc(S["vv_ready"], 1)

            def soft_exp(n):
                act.wait_ge(S["ls_ready"], n + 1)
                act.wait_ge(S["at_ready"], n)
                go(ex[:, :, :], ls[:, :, :], ACT.Exp, scale=0.25).then_inc(S["ex_ready"], 1)

            def attend_out(b):
                act.wait_ge(S["atT_done"], b + 1)
                act.wait_ge(S["rg_done"], b)
                go(atT[:, :], bank[4][0:POOL, 0:T], ACT.Copy).then_inc(S["atT_ready"], 1)
                act.wait_ge(S["rg_done"], b + 1)
                act.wait_ge(S["fin_step"], 3 * b)
                go(gate[:, :, :], bank[5][:, :].rearrange("p (j c) -> p j c", j=TJ)[:, :, D:2 * D], ACT.Tanh, scale=0.5).then_inc(S["gate_ready"], 1)

            pool_out(0)
            soft_exp(0)

            def step2(b, par, half, last):
                attend_out(b)
                if not last:
                    pool_out(b + 1)
                    soft_exp(b + 1)

            steps(act, step2)

        @block.vector
        def _(dve):
            v = nc.vector
            dve.wait_ge(S["weights_in"], 16 * (N_W + 1))
            v.tensor_scalar(sgn[:, :], s_bc[:, :], 0.0, None, ALU.is_gt).then_inc(S["w_small"], 1)
            v.tensor_scalar(sneg[:, :], s_bc[:, :], 0.0, None, ALU.is_lt).then_inc(S["w_small"], 1)
            dve.wait_ge(S["w_small"], 2)
            v.tensor_tensor(sgn[:, :], sgn[:, :], sneg[:, :], ALU.subtract).then_inc(S["w_small"], 1)
            dve.wait_ge(S["w_small"], 3)
            v.tensor_tensor(sabs[:, :], sgn[:, :], s_bc[:, :], ALU.mult).then_inc(S["w_small"], 1)
            v.tensor_scalar(c1[:, :], sgn[:, 1:2], 2.0 / H2S, None, ALU.mult).then_inc(S["w_small"], 1)
            v.tensor_scalar(c2[:, :], sgn[:, 1:2], -1.0 / H2S, None, ALU.mult).then_inc(S["w_small"], 1)
            dve.wait_ge(S["w_small"], 6)
            v.tensor_scalar(sprod[:, :], sabs[:, 0:1], sabs[:, 1:2], 4.0 * H2S, ALU.mult, ALU.mult).then_inc(S["w_small"], 1)
            dve.wait_ge(S["w_small"], 7)
            v.tensor_scalar(fhalf[:, :], s_bc[:, 2:3].broadcast_to([P, 2]), sprod[:, :], None, ALU.mult).then_inc(S["w_small"], 1)
            v.tensor_scalar(cw[:, :, :], cw_ld[:, :, :], 1.0 / WS, None, ALU.mult).then_inc(S["w_dve"], 1)
            v.tensor_scalar(dhalf[:, :].rearrange("p (h d) -> p h d", h=HEADS),
                            dpar_bc[:, :].unsqueeze(2).broadcast_to([P, HEADS, HD]), 0.5, None, ALU.mult).then_inc(S["w_small"], 1)
            v.tensor_copy(sw2_bc[:, :], sw2_ld[:, :].broadcast_to([HID, P])).then_inc(S["w_mlp"], 1)
            v.memset(pre[:, :, 0:PAD], 0.0).then_inc(S["pads"], 1)
            dve.wait_ge(S["w_exp"], 1)
            v.tensor_scalar(negA[:, :], aexp[:, :], -1.0, None, ALU.mult).then_inc(S["w_small"], 1)

            def out_of(t, dst, src, *scale):
                dve.wait_ge(S["w_T"], t + 1)
                if scale:
                    v.tensor_scalar(dst, src, scale[0], scale[1], ALU.mult, ALU.mult).then_inc(S["w_ev"], 1)
                else:
                    v.tensor_copy(dst, src).then_inc(S["w_ev"], 1)

            for t in range(6):
                out_of(t, wt32[:, t * P:(t + 1) * P], bank[t][:, 0:P], nw_col[:, :], WS)
            out_of(6, wt32[:, 6 * P:NIN], bank[6][:, 0:HEADS], nw_col[:, :], WS)
            out_of(7, out_wT[:, 0, :], bank[7][:, 0:P], gw_col[:, 0:1], 1.0)
            out_of(8, out_wT[:, 1, :], bank[0][:, 0:P], gw_col[:, 1:2], 1.0)
            out_of(9, sw1T[:, :], bank[1][:, 0:HID])
            out_of(10, gate1T[:, :], bank[2][:, 0:D])
            out_of(11, gate2T[:, :], bank[3][:, 0:D])
            out_of(12, kwT[:, :], bank[4][0:SDIM, 0:SDIM])
            out_of(13, vwT[:, :], bank[5][0:SDIM, 0:D])
            out_of(14, kp_sb[:, :], bank[0][0:SDIM, 0:D])
            out_of(15, wvv[:, 0:D], bank[1][:, 0:D])
            out_of(16, wv_sb[:, :], bank[2][:, 0:D])
            out_of(17, wmT[:, :], bank[3][:, 0:D])
            out_of(18, wvv[:, D:2 * D], bank[4][:, 0:D])
            dve.wait_ge(S["w_split"], 1)
            v.tensor_tensor(wt_lo[:, :], wt32[:, :], wt_hi[:, :], ALU.subtract).then_inc(S["w_split"], 1)
            v.tensor_tensor(k0_d[:, :], k0_ld[:, 0, :], k0_ld[:, 1, :], ALU.subtract).then_inc(S["w_small"], 1)
            dve.wait_ge(S["w_small"], 11)
            v.tensor_scalar(k0_16[:, :], k0_d[:, :], sgn[:, 0:1], None, ALU.mult).then_inc(S["w_mlp"], 1)
            v.tensor_scalar(k1_16[:, :, :], k1_ld[:, :, :], c1[:, :], c2[:, :], ALU.mult, ALU.add).then_inc(S["w_mlp"], 1)
            v.tensor_scalar(k2_16[:, :, :], k2_ld[:, :, :], 2.0, -1.0, ALU.mult, ALU.add).then_inc(S["w_mlp"], 1)

            def stats(n, par, half):
                dve.wait_ge(x_in[par], 16 * (half + 1))
                for j in range(TJ):
                    v.bn_stats(st6[:, j, :], xall[:, bass.ds(n, 1), j, :].squeeze(1)).then_inc(S["stats"], 1)

            def mean_var(n):
                for j in range(TJ):
                    v.bn_aggr(mv[:, j, :], st6[:, j, :]).then_inc(S["mv_ready"], 1)

            def normed(n):
                dve.wait_ge(S["norm_ready"], n + 1)
                dve.wait_ge(S["xT_done"], TJ * n)
                for j in range(TJ):
                    v.tensor_scalar(xn[:, j, :], xall[:, bass.ds(n, 1), j, :].squeeze(1), lt[:, 5, j:j + 1],
                                    lt[:, 6, j:j + 1], ALU.mult, ALU.add).then_inc(S["xn_ready"], 1)

            def xT_low(n):
                dve.wait_ge(S["xT_hi_ready"], n + 1)
                v.tensor_tensor(xT_lo[:, :], pA[:, 0:T], xT_hi[:, :], ALU.subtract).then_inc(S["xT_lo_ready"], 1)

            def dt_raw(n):
                dve.wait_ge(S["dt_done"], TJ * (n + 1))
                dve.wait_ge(S["sp_step"], SP_STEPS * n)
                dve.wait_ge(S["u_ready"], n)
                v.scalar_tensor_tensor(raw[:, :, :], pDT.rearrange("p (j h) -> p j h", j=TJ), 1.0 / WS,
                                       dtb_bc[:, :].unsqueeze(1).broadcast_to([P, TJ, HEADS]), ALU.mult, ALU.add).then_inc(S["raw_ready"], 1)
                r = raw[:, :, :].rearrange("p j h -> p (j h)")
                dve.wait_ge(S["raw_ready"], n + 1)
                v.tensor_scalar(sp[:, 0, :], r, 0.0, None, ALU.max).then_inc(S["abs_ready"], 1)
                v.scalar_tensor_tensor(sp[:, 1, :], r, -1.0, r, ALU.mult, ALU.min).then_inc(S["abs_ready"], 1)

            def dt_recip(n):
                dve.wait_ge(S["den_ready"], n + 1)
                v.reciprocal(sp[:, 4, :], sp[:, 3, :]).then_inc(S["rden_ready"], 1)

            def conv(n, half):
                dve.wait_ge(S["pre_ready"], 6 * n + 3 * half + 3)
                for k in range(PAD):
                    for i in range(2):
                        c = 2 * half + i
                        if k:
                            dve.wait_ge(S["conv_step"], 12 * n + 6 * half + 2 * k + i - 1)
                        v.scalar_tensor_tensor(acc[:, c, :], pre[:, c, k:k + T], cw[:, c, k:k + 1], acc[:, c, :],
                                               ALU.mult, ALU.add).then_inc(S["conv_step"], 1)

            def conv_silu(n, half):
                dve.wait_ge(S["cth_ready"], 2 * n + half + 1)
                if half == 0:
                    dve.wait_ge(S["xtok_done"], 4 * n)
                    dve.wait_ge(S["g_done"], 2 * n)
                c = slice(2 * half, 2 * half + 2)
                v.scalar_tensor_tensor(xbc[:, c, :], cth[:, c, :], 1.0, acc[:, c, :], ALU.add, ALU.mult).then_inc(S["xbc_ready"], 1)

            def z_gate(n):
                dve.wait_ge(S["zth_ready"], n + 1)
                v.scalar_tensor_tensor(zg[:, :, :], zth[:, :, :], 1.0, pA[:, :].rearrange("p (j c) -> p j c", j=TJ),
                                       ALU.add, ALU.mult).then_inc(S["zg_ready"], 1)

            def hidden_low(b, layer, half):
                hi, lo = ((h1_hi, h1_lo), (h2_hi, h2_lo))[layer]
                dve.wait_ge(S[("h1_hi_ready", "h2_hi_ready")[layer]], 2 * b + half + 1)
                c = slice(2 * half, 2 * half + 2)
                v.scalar_tensor_tensor(lo[:, c, :], F[half][:, :].rearrange("p (c t) -> p c t", c=2), 0.0, hi[:, c, :],
                                       ALU.max, ALU.subtract).then_inc(S[("h1_lo_ready", "h2_lo_ready")[layer]], 1)

            def mixing(b, k):
                dve.wait_ge(S["decay_ready"], 3 * b + k + 1)
                dve.wait_ge(S["g_done"], 2 * b + 2)
                if k == 0:
                    dve.wait_ge(S["y_done"], b)
                v.tensor_tensor(mix[:, k, :, :], decay[:, k, :, :],
                                pG[:, k * P:(k + 1) * P].unsqueeze(1).broadcast_to([P, HEADS, P]), ALU.mult).then_inc(S["mix_ready"], 1)

            def gated(b):
                dve.wait_ge(S["y_done"], b + 1)
                dve.wait_ge(S["x_scaled"], 2 * b + 2)
                v.tensor_tensor(ysum[:, :, :], pY[:, :].rearrange("p (j c) -> p j c", j=TJ), xD[:, :, :], ALU.add).then_inc(S["ysum_ready"], 1)
                dve.wait_ge(S["ysum_ready"], b + 1)
                dve.wait_ge(S["zg_ready"], b + 1)
                dve.wait_ge(S["ygT_done"], 4 * b)
                dve.wait_ge(S["ss_ready"], 2 * b)
                v.tensor_tensor(yg[:, :, :], ysum[:, :, :], zg[:, :, :], ALU.mult).then_inc(S["yg_ready"], 1)

            def mlp_out(b):
                dve.wait_ge(S["gth_ready"], 2 * b + 2)
                dve.wait_ge(S["g_ready"], 2 * b)
                v.tensor_scalar(gth1[:, :, :], gth[:, :, :], 1.0, None, ALU.add).then_inc(S["gth1_ready"], 1)
                dve.wait_ge(S["gth1_ready"], b + 1)
                for j in range(TJ):
                    v.scalar_tensor_tensor(gall[:, bass.ds(b, 1), j, :].squeeze(1), F[0][:, j * D:(j + 1) * D],
                                           norms[:, bass.ds(b, 1), 2, j:j + 1].squeeze(1), gth1[:, j, :],
                                           ALU.mult, ALU.mult).then_inc(S["g_ready"], 1)

            stats(0, 0, 0)
            dve.wait_ge(S["stats"], TJ)
            mean_var(0)
            normed(0)
            xT_low(0)
            dt_raw(0)
            conv(0, 0)
            dt_recip(0)
            conv(0, 1)
            conv_silu(0, 0)
            conv_silu(0, 1)
            z_gate(0)

            def step(b, par, half, last):
                if not last:
                    stats(b + 1, 1 - par, half + par)
                    dve.wait_ge(S["stats"], TJ * (b + 2))
                    dve.wait_ge(S["norm_kept"], 2 * b + 2)
                hidden_low(b, 0, 0)
                if not last:
                    mean_var(b + 1)
                hidden_low(b, 0, 1)
                if not last:
                    normed(b + 1)
                mixing(b, 0)
                if not last:
                    xT_low(b + 1)
                hidden_low(b, 1, 0)
                mixing(b, 1)
                hidden_low(b, 1, 1)
                mixing(b, 2)
                if not last:
                    dt_raw(b + 1)
                    conv(b + 1, 0)
                    dt_recip(b + 1)
                gated(b)
                if not last:
                    conv(b + 1, 1)
                mlp_out(b)
                if not last:
                    z_gate(b + 1)
                    conv_silu(b + 1, 0)
                    conv_silu(b + 1, 1)

            steps(dve, step)

            dve.wait_ge(S["keys_in"], 16)
            k = 0

            def link(ins):
                nonlocal k
                k += 1
                ins.then_inc(S["sel_step"], 1)
                dve.wait_ge(S["sel_step"], k)

            link(v.memset(zero16[:, :], 0.0))
            link(v.tensor_scalar(keys[:, :], logit[:, :], SATURATED, None, ALU.min))
            cur = keys[:, :]
            for r in range(7):
                link(v.max(top8[:, r, :], cur))
                if r < 6:
                    link(v.match_replace(work[:, r % 2, :], top8[:, r, :], cur, -3.0e38))
                    cur = work[:, r % 2, :]
            kth = top8[:, 6, 1:2]
            link(v.tensor_scalar(gt[:, :], keys[:, :], kth, None, ALU.is_gt))
            link(v.tensor_scalar(eq[:, :], keys[:, :], kth, None, ALU.is_equal))
            link(v.tensor_reduce(col[:, 0:1], gt[:, :], AX, ALU.add))
            link(v.tensor_scalar(col[:, 1:2], col[:, 0:1], -1.0, float(POOL), ALU.mult, ALU.add))
            link(v.tensor_tensor_scan(eqc[:, :], eq[:, :], zero16[:, :], 0.0, ALU.add, ALU.add))
            link(v.tensor_scalar(ok[:, :], eqc[:, :], col[:, 1:2], None, ALU.is_le))
            link(v.tensor_tensor(ok[:, :], ok[:, :], eq[:, :], ALU.mult))
            link(v.tensor_tensor(sel[:, :], ok[:, :], gt[:, :], ALU.add))
            link(v.scalar_tensor_tensor(sel[:, :], keys[:, :], 0.0, sel[:, :], ALU.is_gt, ALU.mult))
            link(v.tensor_tensor_scan(selc[:, :], sel[:, :], zero16[:, :], 0.0, ALU.add, ALU.add))
            link(v.tensor_tensor(slot[:, :], selc[:, :], sel[:, :], ALU.mult))
            dve.wait_ge(S["th16_ready"], 1)
            link(v.tensor_scalar(col[:, 2:3], col[:, 4:5], 0.5 / T, 0.5, ALU.mult, ALU.add))
            link(v.tensor_scalar(col[:, 3:4], col[:, 2:3], 0.3, 0.5, ALU.is_gt, ALU.mult))
            link(v.scalar_tensor_tensor(col[:, 5:6], selc[:, T - 1:T], 0.0, col[:, 3:4], ALU.is_gt, ALU.mult))
            link(v.tensor_scalar(diag2[:, 0, :], ident[0:NB, 0:NB], selc[:, T - 1:T], None, ALU.mult))
            v.tensor_scalar(diag2[:, 1, :], ident[0:NB, 0:NB], col[:, 5:6], None, ALU.mult).then_inc(S["slots_done"], 1)
            dve.wait_ge(S["slotT_done"], 3)
            v.tensor_copy(slotT[:, :, :], bank[0][:, 0:TJ * NB].rearrange("p (j b) -> p j b", j=TJ)).then_inc(S["slotT_ready"], 1)
            v.tensor_copy(cnt_rm[:, :, :], bank[1][:, 0:2 * NB].rearrange("p (a b) -> p a b", a=2)).then_inc(S["slotT_ready"], 1)
            dve.wait_ge(S["slotT_ready"], 2)

            def choose(n):
                dve.wait_ge(S["s_done"], n)
                v.tensor_tensor(onehot[:, :, :], slots[:, :].unsqueeze(1).broadcast_to([P, TJ, POOL]),
                                slotT[:, :, bass.ds(n, 1)].broadcast_to([P, TJ, POOL]), ALU.is_equal).then_inc(S["onehot_ready"], 1)
                v.tensor_scalar(pbias[:, :], slots[:, :], cnt_rm[:, 0, bass.ds(n, 1)], -4.0e9, ALU.is_gt, ALU.mult).then_inc(S["bias_ready"], 1)

            def softmax_in(n):
                dve.wait_ge(S["lg_done"], n + 1)
                dve.wait_ge(S["bias_ready"], n + 1)
                v.tensor_tensor(lm[:, :, :], bank[3][:, 0:2 * 64].rearrange("p (j c) -> p j c", j=TJ)[:, :, 0:POOL],
                                pbias[:, :].unsqueeze(1).broadcast_to([P, TJ, POOL]), ALU.add).then_inc(S["lm_ready"], 1)
                dve.wait_ge(S["lm_ready"], n + 1)
                v.tensor_reduce(mx[:, :], lm[:, :, :], AX, ALU.max).then_inc(S["max_ready"], 1)
                dve.wait_ge(S["max_ready"], n + 1)
                dve.wait_ge(S["ex_ready"], n)
                v.tensor_tensor(ls[:, :, :], lm[:, :, :], mx[:, :].unsqueeze(2).broadcast_to([P, TJ, POOL]), ALU.subtract).then_inc(S["ls_ready"], 1)

            def softmax_out(n):
                dve.wait_ge(S["ex_ready"], n + 1)
                v.tensor_reduce(sm[:, :], ex[:, :, :], AX, ALU.add).then_inc(S["sum_ready"], 1)
                dve.wait_ge(S["sum_ready"], n + 1)
                v.reciprocal(rec[:, :], sm[:, :]).then_inc(S["rec_ready"], 1)
                dve.wait_ge(S["rec_ready"], n + 1)
                dve.wait_ge(S["atT_done"], n)
                v.tensor_tensor(at[:, :, :], ex[:, :, :], rec[:, :].unsqueeze(2).broadcast_to([P, TJ, POOL]), ALU.mult).then_inc(S["at_ready"], 1)

            def finish(b, par, half):
                bb = bass.ds(b, 1)
                dve.wait_ge(S["gate_ready"], b + 1)
                v.scalar_tensor_tensor(fin[:, 0, :, :], gate[:, :, :], 1.0,
                                       bank[5][:, :].rearrange("p (j c) -> p j c", j=TJ)[:, :, 0:D], ALU.add, ALU.mult).then_inc(S["fin_step"], 1)
                dve.wait_ge(S["fin_step"], 3 * b + 1)
                dve.wait_ge(S["base_step"], 3 * b + 3)
                v.scalar_tensor_tensor(fin[:, 1, :, :], fin[:, 0, :, :], cnt_rm[:, 1, bb], base[:, 2, :, :], ALU.mult, ALU.add).then_inc(S["fin_step"], 1)
                dve.wait_ge(S["fin_step"], 3 * b + 2)
                v.tensor_tensor(fin[:, 2, :, :], fin[:, 1, :, :], gall[:, bb, :, :].squeeze(1), ALU.mult).then_inc(S["fin_step"], 1)
                dve.wait_ge(S["fin_step"], 3 * b + 3)
                dve.wait_ge(out_done[par], 16 * half)
                v.tensor_tensor(obuf[:, par, :, :], fin[:, 2, :, :], xall[:, bb, :, :].squeeze(1), ALU.add).then_inc(S["out_ready"], 1)

            choose(0)
            softmax_in(0)
            softmax_out(0)

            def step2(b, par, half, last):
                if not last:
                    choose(b + 1)
                finish(b, par, half)
                if not last:
                    softmax_in(b + 1)
                    softmax_out(b + 1)

            steps(dve, step2)

        @block.gpsimd
        def _(pool):
            g = nc.gpsimd
            g.memset(ident[:, :], 0.0).then_inc(S["ln_step"], 1)
            pool.wait_ge(S["ln_step"], 1)
            g.affine_select(out=ident[:, :], in_=ident[:, :], compare_op=ALU.not_equal, fill=1.0, base=0,
                            pattern=[[-1, P]], channel_multiplier=1).then_inc(S["consts"], 1)
            pool.wait_ge(S["consts"], 1)
            g.tensor_copy(ident_bf[:, :], ident[:, :]).then_inc(S["consts"], 1)
            g.memset(ones32[:, :], 1.0).then_inc(S["consts"], 1)
            g.memset(ones3[:, :], 1.0).then_inc(S["consts"], 1)
            g.memset(upto[:, :], 1.0).then_inc(S["ln_step"], 1)
            g.memset(mask[:, :, :], 0.0).then_inc(S["ln_step"], 1)
            g.memset(minus_head[:, :, :], 0.0).then_inc(S["ln_step"], 1)
            pool.wait_ge(S["ln_step"], 4)
            g.affine_select(out=upto[:, 0:P], in_=upto[:, 0:P], compare_op=ALU.is_ge, fill=0.0, base=0,
                            pattern=[[1, P]], channel_multiplier=-1).then_inc(S["consts"], 1)
            g.affine_select(out=mask[:, :, :], in_=mask[:, :, :], compare_op=ALU.is_ge, fill=NEG, base=0,
                            pattern=[[0, HEADS], [1, P]], channel_multiplier=-1).then_inc(S["consts"], 1)
            for q in range(3):
                ins = g.affine_select(out=minus_head[:, :, :], in_=minus_head[:, :, :], compare_op=ALU.not_equal, fill=-1.0,
                                      base=-HEADS * q, pattern=[[-1, HEADS], [0, P]], channel_multiplier=1)
                ins.then_inc(S["ln_step"], 1)
                pool.wait_ge(S["ln_step"], 5 + q)
            g.iota(slots[:, :], pattern=[[1, POOL]], base=1, channel_multiplier=0,
                   allow_small_or_imprecise_dtypes=True).then_inc(S["consts"], 1)
            for c, value in enumerate(NUMS.values()):
                g.memset(nums[:, c:c + 1], value).then_inc(S["ln_step"], 1)
            SETUP = 7 + len(NUMS)
            pool.wait_ge(S["ln_step"], SETUP)
            pool.wait_ge(S["w_small"], 10)

            def norm(n):
                k = 0

                def link(ins):
                    nonlocal k
                    k += 1
                    ins.then_inc(S["ln_step"], 1)
                    pool.wait_ge(S["ln_step"], LN_STEPS * n + (SETUP + k))

                pool.wait_ge(S["mv_ready"], TJ * (n + 1))
                pool.wait_ge(S["xn_ready"], TJ * n)
                mean, var = mv[:, :, 0], mv[:, :, 1]
                link(g.tensor_tensor(lt[:, 0, :], var, num("eps", P, TJ), ALU.add))
                link(g.tensor_tensor(lnw[:, 0, :], lt[:, 0, :], num("-1/2", P, TJ), ALU.pow))
                link(g.tensor_tensor(lt[:, 1, :], var, lnw[:, 0, :], ALU.mult))
                link(g.tensor_tensor(lt[:, 2, :], lt[:, 1, :], lnw[:, 0, :], ALU.mult))
                link(g.tensor_tensor(lt[:, 2, :], lt[:, 2, :], num("eps", P, TJ), ALU.add))
                link(g.tensor_tensor(lt[:, 3, :], lt[:, 2, :], num("-1/2", P, TJ), ALU.pow))
                link(g.tensor_tensor(lt[:, 5, :], lnw[:, 0, :], lt[:, 3, :], ALU.mult))
                link(g.tensor_tensor(lt[:, 7, :], mean, num("-1", P, TJ), ALU.mult))
                link(g.tensor_tensor(lnw[:, 1, :], lt[:, 7, :], lnw[:, 0, :], ALU.mult))
                g.tensor_tensor(lt[:, 6, :], lnw[:, 1, :], lt[:, 3, :], ALU.mult).then_inc(S["norm_ready"], 1)
                link(g.tensor_tensor(lt[:, 4, :], lt[:, 2, :], num("1/2", P, TJ), ALU.pow))
                g.tensor_tensor(lnw[:, 2, :], lt[:, 4, :], fhalf[:, :], ALU.mult).then_inc(S["norm_kept"], 1)
                pool.wait_ge(S["norm_kept"], 2 * n + 1)
                g.tensor_tensor(norms[:, bass.ds(n, 1), :, :].squeeze(1), lnw[:, :, :], num("1", P, 3, TJ), ALU.mult).then_inc(S["norm_kept"], 1)
                assert k == LN_STEPS

            def scale_x(b):
                pool.wait_ge(S["xtok_ready"], b + 1)
                pool.wait_ge(S["y_done"], b)
                g.tensor_tensor(dtx[:, :, :].rearrange("p j (h d) -> p (j h) d", h=HEADS),
                                xtok[:, :, :].rearrange("p j (h d) -> p (j h) d", h=HEADS),
                                dt8[:, :].unsqueeze(2).broadcast_to([P, TJ * HEADS, HD]), ALU.mult).then_inc(S["x_scaled"], 1)
                pool.wait_ge(S["ysum_ready"], b)
                g.tensor_tensor(xD[:, :, :], xtok[:, :, :], dhalf[:, :].unsqueeze(1).broadcast_to([P, TJ, DI]), ALU.mult).then_inc(S["x_scaled"], 1)

            def softplus(n):
                k = 0

                def link(ins):
                    nonlocal k
                    k += 1
                    ins.then_inc(S["sp_step"], 1)
                    pool.wait_ge(S["sp_step"], SP_STEPS * n + k)

                W = TJ * HEADS
                pool.wait_ge(S["u_ready"], n + 1)
                g.tensor_tensor(sp[:, 3, :], sp[:, 2, :], num("2", P, W), ALU.add).then_inc(S["den_ready"], 1)
                pool.wait_ge(S["rden_ready"], n + 1)
                link(g.tensor_tensor(sp[:, 5, :], sp[:, 2, :], sp[:, 4, :], ALU.mult))
                link(g.tensor_tensor(sp[:, 6, :], sp[:, 5, :], sp[:, 5, :], ALU.mult))
                link(g.tensor_tensor(sp[:, 7, :], sp[:, 6, :], num(f"atanh{ATANH_TERMS - 1}", P, W), ALU.mult))
                for t in range(ATANH_TERMS - 2, -1, -1):
                    link(g.tensor_tensor(sp[:, 7, :], sp[:, 7, :], num(f"atanh{t}", P, W), ALU.add))
                    link(g.tensor_tensor(sp[:, 7, :], sp[:, 7, :], sp[:, 6 if t else 5, :], ALU.mult))
                link(g.tensor_tensor(sp[:, 8, :], sp[:, 0, :], sp[:, 7, :], ALU.add))
                pool.wait_ge(S["cum_done"], n)
                g.tensor_tensor(a_sb[:, :].rearrange("p (j h) -> p j h", j=TJ), sp[:, 8, :].rearrange("p (j h) -> p j h", j=TJ),
                                negA[:, :].unsqueeze(1).broadcast_to([P, TJ, HEADS]), ALU.mult).then_inc(S["a_ready"], 1)
                g.tensor_tensor(dt8[:, :], sp[:, 8, :], num("1/8", P, W), ALU.mult).then_inc(S["dt8_ready"], 1)
                assert k == SP_STEPS

            def split_cum(n):
                pool.wait_ge(S["craw_ready"], 2 * n + 2)
                pool.wait_ge(S["rows_in"], 96 * n)
                g.tensor_tensor(cres[:, :], craw[:, :], parts[:, 0, :], ALU.subtract).then_inc(S["parts_step"], 1)
                pool.wait_ge(S["parts_step"], PART_STEPS * n + 1)
                g.tensor_tensor(parts[:, 1, :], cres[:, :], num("1", HEADS, T), ALU.mult).then_inc(S["parts_step"], 1)
                pool.wait_ge(S["seg_done"], 3 * n)
                pool.wait_ge(S["parts_step"], PART_STEPS * n + 2)
                g.tensor_tensor(parts[:, 2, :], cres[:, :], parts[:, 1, :], ALU.subtract).then_inc(S["parts_ready"], 1)

            def rms(b):
                pool.wait_ge(S["ss_ready"], 2 * b + 2)
                g.tensor_tensor(rt[:, :], ss[:, :], num("1/DI", P, TJ), ALU.mult).then_inc(S["rstd_step"], 1)
                pool.wait_ge(S["rstd_step"], 2 * b + 1)
                g.tensor_tensor(rt[:, :], rt[:, :], num("rms eps", P, TJ), ALU.add).then_inc(S["rstd_step"], 1)
                pool.wait_ge(S["rstd_step"], 2 * b + 2)
                pool.wait_ge(S["y_ready"], 2 * b)
                g.tensor_tensor(rstd[:, :], rt[:, :], num("-1/2", P, TJ), ALU.pow).then_inc(S["rstd_ready"], 1)

            norm(0)
            softplus(0)
            split_cum(0)

            def step(b, par, half, last):
                if not last:
                    norm(b + 1)
                pool.wait_ge(S["dt8_ready"], b + 1)
                scale_x(b)
                if not last:
                    softplus(b + 1)
                rms(b)
                if not last:
                    split_cum(b + 1)

            steps(pool, step)

            def base_sum(b, par, half):
                bb = bass.ds(b, 1)
                pool.wait_ge(y_in[par], 16 * (half + 1))
                pool.wait_ge(S["out_ready"], b)
                g.tensor_tensor(base[:, 0, :, :], xall[:, bb, :, :].squeeze(1),
                                norms[:, bb, 0, :].squeeze(1).unsqueeze(2).broadcast_to([P, TJ, D]), ALU.mult).then_inc(S["base_step"], 1)
                pool.wait_ge(S["base_step"], 3 * b + 1)
                g.tensor_tensor(base[:, 1, :, :], base[:, 0, :, :],
                                norms[:, bb, 1, :].squeeze(1).unsqueeze(2).broadcast_to([P, TJ, D]), ALU.add).then_inc(S["base_step"], 1)
                pool.wait_ge(S["base_step"], 3 * b + 2)
                g.tensor_tensor(base[:, 2, :, :], base[:, 1, :, :], yin[:, par, :, :], ALU.add).then_inc(S["base_step"], 1)

            steps(pool, lambda b, par, half, last: base_sum(b, par, half))


_INS = ['x', 'norm_w', 'in_w', 'conv_w', 'conv_b', 'dt_bias', 'A_log', 'D_param', 'gnorm_w', 'out_w',
        'scorer_w1', 'scorer_w2', 'summ_w', 'q_w', 'k_w', 'v_w', 'gate_w']
_FFN = ['k0', 'k1', 'k2', 's0', 's1', 's2']


def kernel(**inputs):
    import numpy as _np
    import concourse.bacc as _bacc
    from concourse import mybir as _mybir
    from concourse.bass_utils import run_bass_kernel_spmd as _run

    nc = _bacc.Bacc("TRN2", target_bir_lowering=False, num_devices=1)
    arrays, args = {}, []
    for name in [f"L0_attn_{n}" for n in _INS] + [f"L0_ffn_{n}" for n in _FFN]:
        a = _np.ascontiguousarray(inputs[name])
        if a.ndim == 0:
            a = a.reshape(1)
        arrays[f"in_{name}"] = a
        args.append(nc.dram_tensor(f"in_{name}", a.shape, _mybir.dt.from_np(a.dtype), kind="ExternalInput").ap())
    args.append(nc.dram_tensor("out_0", (NB, T, D), _mybir.dt.float32, kind="ExternalOutput").ap())
    layer_kernel(nc, *args)
    r = _run(nc, [arrays], core_ids=[0])
    return r.results[0]["out_0"]
```

```python
import concourse.bass as bass
from concourse import mybir
from contextlib import ExitStack

P = 128
NB, T, D = 16, 256, 128
TJ = T // P
HEADS, HD, NSTATE = 4, 64, 128
DI = HEADS * HD
CONV = DI + 2 * NSTATE
CB = CONV // P
TAPS = 4
PAD = TAPS - 1
NIN = 2 * DI + 2 * NSTATE + HEADS
POOL, SDIM, HID = 50, 64, 32
PAIR = 2
NG = NB // PAIR
FIN = 2 * PAIR + 1
FF = 512
FB = FF // P
EPS = 1e-5
WS = 64.0
H2S = 16.0
SATURATED = 16.635532
ATANH_TERMS = 8
NEG = -1.0e30
NUMS = {"-1/2": -0.5, "1/2": 0.5, "eps": EPS, "-1": -1.0, "1": 1.0, "2": 2.0, "1/8": 0.125, "1/DI": 1.0 / DI,
        "rms eps": EPS * (2 * WS) ** 2, **{f"atanh{i}": 2.0 / (2 * i + 1) for i in range(ATANH_TERMS)}}


def layer_kernel(nc, x, norm_w, in_w, conv_w, conv_b, dt_bias, A_log, D_param, gnorm_w, out_w,
                 scorer_w1, scorer_w2, summ_w, q_w, k_w, v_w, gate_w, k0, k1, k2, s0, s1, s2, out):
    f32, f16, bf16, u8 = mybir.dt.float32, mybir.dt.float16, mybir.dt.bfloat16, mybir.dt.uint8
    ALU = mybir.AluOpType
    ACT = mybir.ActivationFunctionType
    AX = mybir.AxisListType.X

    x_v = x.rearrange("b (j p) d -> b p j d", p=P)
    out_v = out.rearrange("b (j p) d -> b p j d", p=P)

    importance = nc.dram_tensor("importance", (NB, T), f32, kind="Internal").ap()

    ctx = ExitStack()
    with ctx:
        def sb(name, shape, dt=f32):
            return ctx.enter_context(nc.sbuf_tensor(name, shape, dt))

        def sem(name):
            return ctx.enter_context(nc.semaphore(name))

        inw_ld = sb("inw_ld", [P, 6, D])
        dtw_ld = sb("dtw_ld", [HEADS, D])
        outw_ld = sb("outw_ld", [P, DI])
        sw1_ld = sb("sw1_ld", [HID, D])
        gatew_ld = sb("gatew_ld", [P, 2 * D])
        kw_ld = sb("kw_ld", [SDIM, SDIM])
        vw_ld = sb("vw_ld", [P, SDIM])
        summ_sb = sb("summ_sb", [SDIM, D])
        qw_sb = sb("qw_sb", [SDIM, D])
        sw2_ld = sb("sw2_ld", [HID, 1])
        sw2_bc = sb("sw2_bc", [HID, P])
        k0_ld = sb("k0_ld", [P, 2, FF], u8)
        k1_ld = sb("k1_ld", [P, FB, FF], u8)
        k2_ld = sb("k2_ld", [P, FB, D], u8)
        nw_col = sb("nw_col", [P, 1])
        gw_col = sb("gw_col", [P, TJ])
        cw_ld = sb("cw_ld", [P, CB, TAPS])
        cb_sb = sb("cb_sb", [P, CB])
        dtb_bc = sb("dtb_bc", [P, HEADS])
        alog_bc = sb("alog_bc", [P, HEADS])
        dpar_bc = sb("dpar_bc", [P, HEADS])
        s_bc = sb("s_bc", [P, 3])
        ident = sb("ident", [P, P])
        ident_bf = sb("ident_bf", [P, P], bf16)
        ones32 = sb("ones32", [P, P])
        ones3 = sb("ones3", [3, P], bf16)
        upto = sb("upto", [P, T])
        mask = sb("mask", [P, HEADS, P], bf16)
        minus_head = sb("minus_head", [3 * HEADS, HEADS, P], bf16)
        slots = sb("slots", [P, POOL])
        nums = sb("nums", [P, len(NUMS)])
        wt32 = sb("wt32", [P, NIN])
        wt_hi = sb("wt_hi", [P, NIN], f16)
        wt_lo = sb("wt_lo", [P, NIN], f16)
        out_wT = sb("out_wT", [P, TJ, D])
        sw1T = sb("sw1T", [P, HID])
        gate1T = sb("gate1T", [P, D])
        gate2T = sb("gate2T", [P, D])
        kwT = sb("kwT", [SDIM, SDIM])
        vwT = sb("vwT", [SDIM, D])
        kp_sb = sb("kp_sb", [SDIM, D])
        wv_sb = sb("wv_sb", [P, D])
        wmT = sb("wmT", [P, D])
        wvv = sb("wvv", [P, 2 * D])
        k0_16 = sb("k0_16", [P, FF], f16)
        k0_d = sb("k0_d", [P, FF])
        k1_16 = sb("k1_16", [P, FB, FF], f16)
        k2_16 = sb("k2_16", [P, FB, D], f16)
        cw = sb("cw", [P, CB, TAPS])
        negA = sb("negA", [P, HEADS])
        aexp = sb("aexp", [P, HEADS])
        dhalf = sb("dhalf", [P, DI])
        sgn = sb("sgn", [P, 3])
        sneg = sb("sneg", [P, 3])
        sabs = sb("sabs", [P, 3])
        sprod = sb("sprod", [P, 1])
        fhalf = sb("fhalf", [P, 2])
        c1 = sb("c1", [P, 1])
        c2 = sb("c2", [P, 1])
        xall = sb("xall", [P, NB, TJ, D])
        yall = sb("yall", [P, NB, TJ, D])
        yTall = sb("yTall", [P, NB, T])
        gall = sb("gall", [P, NB, TJ, D])
        norms = sb("norms", [P, 3, NB, TJ])
        row = sb("row", [1, T])
        st6 = sb("st6", [P, TJ, 6])
        mv = sb("mv", [P, TJ, 2])
        lt = sb("lt", [P, 8, TJ])
        lnw = sb("lnw", [P, 3, TJ])
        xn = sb("xn", [P, TJ, D])
        xT_hi = sb("xT_hi", [P, 2, T], f16)
        xT_lo = sb("xT_lo", [P, 2, T], f16)
        raw = sb("raw", [P, TJ, HEADS])
        sp = sb("sp", [P, 9, TJ * HEADS])
        dt8 = sb("dt8", [P, TJ * HEADS])
        a_sb = sb("a_sb", [P, TJ * HEADS])
        craw = sb("craw", [HEADS, T])
        cres = sb("cres", [HEADS, T])
        parts = sb("parts", [HEADS, 3, T], bf16)
        cum_t = sb("cum_t", [3, HEADS, T], bf16)
        cum_s = sb("cum_s", [3 * HEADS, T], bf16)
        pre = sb("pre", [P, CB, PAD + T])
        acc = sb("acc", [P, CB, T])
        cth = sb("cth", [P, CB, T])
        xbc = sb("xbc", [P, CB, T])
        zth = sb("zth", [P, TJ, DI])
        zg = sb("zg", [P, TJ, DI])
        xtok = sb("xtok", [P, TJ, DI])
        dtx = sb("dtx", [P, TJ, DI])
        xD = sb("xD", [P, TJ, DI])
        decay = sb("decay", [P, 3, HEADS, P])
        mix = sb("mix", [P, 3, HEADS, P])
        ysum = sb("ysum", [P, TJ, DI])
        yg = sb("yg", [P, TJ, DI])
        ysq = sb("ysq", [P, TJ, DI], bf16)
        ss = sb("ss", [P, 2])
        rt = sb("rt", [P, 2])
        rstd = sb("rstd", [P, 2])
        ygT = sb("ygT", [P, TJ, T])
        ybuf = sb("ybuf", [P, TJ, D])
        yTbuf = sb("yTbuf", [P, T])
        hsc = sb("hsc", [HID, T])
        h1_hi = sb("h1_hi", [P, FB, T], f16)
        h1_lo = sb("h1_lo", [P, FB, T], f16)
        h2_hi = sb("h2_hi", [P, FB, T], f16)
        h2_lo = sb("h2_lo", [P, FB, T], f16)
        gth = sb("gth", [P, TJ, D])
        gth1 = sb("gth1", [P, TJ, D])
        keys = sb("keys", [NB, T])
        logit = sb("logit", [NB, T])
        work = sb("work", [NB, 2, T])
        top8 = sb("top8", [NB, 7, 8])
        gt = sb("gt", [NB, T])
        eq = sb("eq", [NB, T])
        eqc = sb("eqc", [NB, T])
        ok = sb("ok", [NB, T])
        sel = sb("sel", [NB, T])
        selc = sb("selc", [NB, T])
        slot = sb("slot", [NB, T])
        zero16 = sb("zero16", [NB, T])
        th16 = sb("th16", [NB, T])
        col = sb("col", [NB, 8])
        diag2 = sb("diag2", [NB, 2, NB])
        slotT = sb("slotT", [P, TJ, NB])
        cnt_rm = sb("cnt_rm", [P, 2, NB])
        yin = decay[:, 0:2, :, :].rearrange("p s (q j) d -> p s q j d", q=PAIR)
        yTin = mix[:, 0:2, :, :].rearrange("p s (q j) d -> p s q (j d)", q=PAIR)
        onehot = sb("onehot", [P, TJ, PAIR, POOL])
        pover = sb("pover", [P, PAIR, POOL])
        sT = sb("sT", [P, PAIR, POOL])
        m_sb = sb("m_sb", [P, PAIR, POOL])
        vv = zth[0:POOL, :, :]
        lm = sb("lm", [P, PAIR * TJ, POOL])
        ls = sb("ls", [P, PAIR * TJ, POOL])
        ex = sb("ex", [P, PAIR * TJ, POOL])
        at = sb("at", [P, PAIR * TJ, POOL])
        mx = sb("mx", [P, PAIR * TJ])
        sm = sb("sm", [P, PAIR * TJ])
        rec = sb("rec", [P, PAIR * TJ])
        atT = zg[0:POOL, :, :].rearrange("p j c -> p (j c)")
        gate = ysum[:, :, :].rearrange("p q (j d) -> p q j d", j=TJ)
        base = sb("base", [P, 3, PAIR, TJ, D])
        fin = sb("fin", [P, 3, PAIR, TJ, D])
        obuf = xbc[:, :, :].rearrange("p (s q) (j d) -> p s q j d", s=2, j=TJ)

        bank = [ctx.enter_context(nc.psum_tensor(f"bank{i}", [P, 512], f32)) for i in range(8)]
        F = [bank[0], bank[1]]
        pA = bank[2]
        pB = bank[3]
        pG = bank[4]
        pDT = pA[:, 0:TJ * HEADS]
        pY = bank[6]
        pS = [bank[5], pY, bank[5]]
        pO, pYT = bank[7][:, 0:256], bank[7][:, 256:512]

        S = {n: sem(n) for n in (
            "weights_in", "consts", "w_T", "w_ev", "w_split", "w_mlp", "w_small", "w_dve",
            "w_exp", "pads",
            "stats", "mv_ready", "ln_step", "norm_ready", "norm_kept", "dt8_ready", "xn_ready", "xT_done", "xT_hi_ready",
            "xT_lo_ready", "dt_done", "raw_ready", "sp_step", "abs_ready", "u_ready", "den_ready",
            "rden_ready", "a_ready", "cum_done", "craw_ready", "parts_step", "parts_ready",
            "rows_in", "proj_done", "pre_ready", "conv_step", "cth_ready", "xbc_ready", "z_done",
            "zth_ready", "zg_ready", "xtok_done", "xtok_ready", "x_scaled", "g_done", "seg_done",
            "decay_ready", "mix_ready", "y_done", "ysum_ready", "yg_ready", "ss_ready",
            "rstd_step", "rstd_ready", "ygT_done", "ygT_ready", "yo_done", "y_ready", "yT_done",
            "yT_ready", "h_done", "h_ready", "row_done", "row_ready", "y_saved", "yT_saved",
            "l1_done", "h1_hi_ready", "h1_lo_ready", "l2_done", "h2_hi_ready", "h2_lo_ready",
            "l3_done", "gth_ready", "gth1_ready", "g_ready",
            "keys_in", "row_saved", "sel_step", "slots_done", "th16_ready", "slotT_done", "slotT_ready",
            "onehot_ready", "choose_step", "lm_step", "bias_ready", "s_done", "sT_ready", "m_done", "m_ready", "vv_done",
            "vv_ready", "lg_done", "lm_ready", "max_ready", "ls_ready", "ex_ready", "sum_ready",
            "rec_ready", "at_ready", "atT_done", "atT_ready", "rg_done", "gate_ready",
            "base_step", "fin_step", "out_ready")}
        x_in = [sem("x_in0"), sem("x_in1")]
        y_in = [sem("y_in0"), sem("y_in1")]
        yT_in = [sem("yT_in0"), sem("yT_in1")]
        out_done = [sem("out_done0"), sem("out_done1")]

        ctx.enter_context(nc.allow_non_contiguous_dma(reason="columns of small weights"))
        block = ctx.enter_context(nc.Block())

        def num(name, p, *free):
            c = list(NUMS).index(name)
            a = nums[0:p, c:c + 1]
            for _ in free[1:]:
                a = a.unsqueeze(2)
            return a.broadcast_to([p, *free])

        def steps(eng, step, count=NB):
            step(0, 0, 0)
            step(1, 1, 0)
            with eng.Fori(1, count // 2 - 1) as i:
                step(2 * i, 0, i)
                step(2 * i + 1, 1, i)
            step(count - 2, 0, count // 2 - 1)
            step(count - 1, 1, count // 2 - 1)

        def has(b, ahead, count=NB):
            return not isinstance(b, int) or 0 <= b + ahead < count

        N_W = 22
        N_JOBS = 14
        LN_STEPS, SP_STEPS, PART_STEPS = 10, 2 + 1 + 2 * (ATANH_TERMS - 1) + 1, 2

        @block.sync
        def _(sp_eng):
            def w(dst, src):
                sp_eng.dma_start(dst, src).then_inc(S["weights_in"], 16)

            def load_x(n, par):
                sp_eng.dma_start(xall[:, bass.ds(n, 1), :, :], x_v[bass.ds(n, 1)].rearrange("b p j d -> p b j d")).then_inc(x_in[par], 16)

            sp_eng.dma_start(xall[:, 0:1, :, :], x_v[0:1].rearrange("b p j d -> p b j d")).then_inc(x_in[0], 16)
            w(inw_ld[:, :, :], in_w[0:6 * P, :].rearrange("(c p) d -> p c d", p=P))
            w(dtw_ld[:, :], in_w[6 * P:NIN, :])
            w(outw_ld[:, :], out_w[:, :])
            w(sw1_ld[:, :], scorer_w1[:, :])
            w(gatew_ld[:, :], gate_w[:, :])
            w(kw_ld[:, :], k_w[:, :])
            w(vw_ld[:, :], v_w[:, :])
            w(summ_sb[:, :], summ_w[:, :])
            w(qw_sb[:, :], q_w[:, :])
            w(sw2_ld[:, :], scorer_w2.rearrange("a h -> h a"))
            w(k0_ld[:, :, :], k0.rearrange("(a p) n -> p a n", p=P))
            w(k1_ld[:, :, :], k1.rearrange("(a p) n -> p a n", p=P))
            w(k2_ld[:, :, :], k2.rearrange("(a p) n -> p a n", p=P))
            w(nw_col[:, :], norm_w.rearrange("(p a) -> p a", a=1))
            w(gw_col[:, :], gnorm_w.rearrange("(a p) -> p a", p=P))
            w(cw_ld[:, :, :], conv_w.rearrange("(a p) k -> p a k", p=P))
            w(cb_sb[:, :], conv_b.rearrange("(a p) -> p a", p=P))
            w(dtb_bc[:, :], dt_bias.partition_broadcast(P))
            w(alog_bc[:, :], A_log.partition_broadcast(P))
            w(dpar_bc[:, :], D_param.partition_broadcast(P))
            w(s_bc[:, 0:1], s0.partition_broadcast(P))
            w(s_bc[:, 1:2], s1.partition_broadcast(P))
            w(s_bc[:, 2:3], s2.partition_broadcast(P))
            sp_eng.dma_start(xall[:, 1:2, :, :], x_v[1:2].rearrange("b p j d -> p b j d")).then_inc(x_in[1], 16)

            def relayout(n):
                sp_eng.wait_ge(S["parts_ready"], n + 1)
                for q in range(3):
                    sp_eng.dma_start(cum_t[q:q + 1, :, :], parts[:, q, :]).then_inc(S["rows_in"], 16)
                    sp_eng.dma_start(cum_s[HEADS * q:HEADS * (q + 1), :], parts[:, q, :]).then_inc(S["rows_in"], 16)

            def save_y(b):
                sp_eng.wait_ge(S["y_ready"], 2 * b + 2)
                sp_eng.dma_start(yall[:, bass.ds(b, 1), :, :], ybuf[:, :, :].unsqueeze(1)).then_inc(S["y_saved"], 16)

            for n in range(2, 4):
                sp_eng.wait_ge(x_in[n % 2], 16)
                load_x(n, n % 2)
            relayout(0)

            def step(b, par, half):
                if has(b, 4):
                    sp_eng.wait_ge(x_in[par], 16 * (half + 2))
                    load_x(b + 4, par)
                if has(b, -1):
                    save_y(b - 1)
                if has(b, 1):
                    relayout(b + 1)

            step(0, 0, 0)
            step(1, 1, 0)
            with sp_eng.Fori(1, NB // 2 - 2) as i:
                step(2 * i, 0, i)
                step(2 * i + 1, 1, i)
            for b in range(NB - 4, NB):
                step(b, b % 2, b // 2)
            save_y(NB - 1)

            sp_eng.wait_ge(S["row_saved"], 16 * NB)
            sp_eng.dma_start(logit[:, :], importance[:, :]).then_inc(S["keys_in"], 16)

            def load_y(n, par):
                pair = bass.ds(PAIR * n, PAIR)
                sp_eng.dma_start(yin[:, par, :, :, :], yall[:, pair, :, :]).then_inc(y_in[par], 16)
                sp_eng.dma_start(yTin[:, par, :, :], yTall[:, pair, :]).then_inc(yT_in[par], 16)

            sp_eng.wait_ge(S["y_saved"], 16 * NB)
            sp_eng.wait_ge(S["yT_saved"], 16 * NB)
            load_y(0, 0)
            load_y(1, 1)

            def step2(b, par, half):
                sp_eng.wait_ge(S["out_ready"], b + 1)
                if has(b, 2, NG):
                    load_y(b + 2, par)
                if has(b, -2, NG):
                    sp_eng.wait_ge(out_done[par], 16 * half)
                sp_eng.dma_start(out_v[bass.ds(PAIR * b, PAIR)].rearrange("b p j d -> p b j d"), obuf[:, par, :, :, :]).then_inc(out_done[par], 16)

            steps(sp_eng, step2, NG)
            for par in range(2):
                sp_eng.wait_ge(out_done[par], 16 * NG // 2)

        @block.tensor
        def _(pe):
            mm = nc.tensor.matmul

            pe.wait_ge(S["consts"], 1)
            pe.wait_ge(S["weights_in"], 16 * (N_W + 1))
            jobs = [(inw_ld[:, c, :], P) for c in range(6)] + [(dtw_ld[:, :], HEADS)] \
                + [(outw_ld[:, k * P:(k + 1) * P], P) for k in range(2)] + [(sw1_ld[:, :], HID)] \
                + [(gatew_ld[:, k * D:(k + 1) * D], P) for k in range(2)] + [(kw_ld[:, :], SDIM), (vw_ld[:, :], P)]
            for t, (src, rows) in enumerate(jobs):
                if t >= 8:
                    pe.wait_ge(S["w_ev"], t - 7)
                cols = src.shape[1]
                nc.tensor.transpose(bank[t % 8][0:cols, 0:rows], src, ident[0:rows, 0:rows]).then_inc(S["w_T"], 1)
            pe.wait_ge(S["w_ev"], N_JOBS)
            mm(bank[0][0:SDIM, 0:D], kwT[:, :], summ_sb[:, :], start=True, stop=True).then_inc(S["w_T"], 1)
            mm(bank[1][:, 0:D], summ_sb[:, :], vwT[:, :], start=True, stop=True).then_inc(S["w_T"], 1)
            mm(bank[2][:, 0:D], vwT[:, :], summ_sb[:, :], start=True, stop=True).then_inc(S["w_T"], 1)
            pe.wait_ge(S["w_ev"], N_JOBS + 3)
            mm(bank[3][:, 0:D], kp_sb[:, :], qw_sb[:, :], start=True, stop=True).then_inc(S["w_T"], 1)
            mm(bank[4][:, 0:D], wv_sb[:, :], gate2T[:, :], start=True, stop=True).then_inc(S["w_T"], 1)

            def norm_T(n):
                pe.wait_ge(S["xn_ready"], TJ * (n + 1))
                pe.wait_ge(S["zg_ready"], n)
                for j in range(TJ):
                    nc.tensor.transpose(pA[:, j * P:(j + 1) * P], xn[:, j, :], ident[:, :]).then_inc(S["xT_done"], 1)

            def dt_proj(n, par):
                pe.wait_ge(S["xT_hi_ready"], n + 1)
                pe.wait_ge(S["xT_lo_ready"], n + 1)
                for j in range(TJ):
                    o = pDT[:, j * HEADS:(j + 1) * HEADS]
                    t = slice(j * P, (j + 1) * P)
                    mm(o, xT_hi[:, par, t], wt_hi[:, 6 * P:NIN], start=True, stop=False)
                    mm(o, xT_hi[:, par, t], wt_lo[:, 6 * P:NIN], start=False, stop=False)
                    mm(o, xT_lo[:, par, t], wt_hi[:, 6 * P:NIN], start=False, stop=True).then_inc(S["dt_done"], 1)

            def conv_proj(n, par, half):
                dst = pB if half else pA
                if half == 0:
                    pe.wait_ge(S["raw_ready"], n + 1)
                for i in range(2):
                    c = DI + (2 * half + i) * P
                    o = dst[:, i * T:(i + 1) * T]
                    mm(o, wt_hi[:, c:c + P], xT_hi[:, par, :], start=True, stop=False)
                    mm(o, wt_hi[:, c:c + P], xT_lo[:, par, :], start=False, stop=False)
                    mm(o, wt_lo[:, c:c + P], xT_hi[:, par, :], start=False, stop=True).then_inc(S["proj_done"], 1)

            def z_proj(n, par):
                pe.wait_ge(S["pre_ready"], 6 * n + 3)
                for j in range(TJ):
                    o = pA[:, j * DI:(j + 1) * DI]
                    t = slice(j * P, (j + 1) * P)
                    mm(o, xT_hi[:, par, t], wt_hi[:, 0:DI], start=True, stop=False)
                    mm(o, xT_hi[:, par, t], wt_lo[:, 0:DI], start=False, stop=False)
                    mm(o, xT_lo[:, par, t], wt_hi[:, 0:DI], start=False, stop=True).then_inc(S["z_done"], 1)

            def cum(n):
                pe.wait_ge(S["a_ready"], n + 1)
                if has(n, -2):
                    pe.wait_ge(S["row_ready"], n - 1)
                elif has(n, -1):
                    pe.wait_ge(S["mix_ready"], 3 * n)
                mm(pG[0:HEADS, 0:T], a_sb[:, 0:HEADS], upto[:, :], start=True, stop=False)
                mm(pG[0:HEADS, P:T], a_sb[:, HEADS:2 * HEADS], upto[:, 0:P], start=False, stop=True).then_inc(S["cum_done"], 1)

            def x_by_token(b):
                pe.wait_ge(S["xbc_ready"], 2 * b + 1)
                pe.wait_ge(S["pre_ready"], 6 * b + 6)
                for j in range(TJ):
                    for k in range(2):
                        nc.tensor.transpose(pB[:, j * DI + k * P:j * DI + (k + 1) * P], xbc[:, k, j * P:(j + 1) * P],
                                            ident[:, :]).then_inc(S["xtok_done"], 1)

            def scores(b):
                pe.wait_ge(S["xbc_ready"], 2 * b + 2)
                pe.wait_ge(S["craw_ready"], 2 * b + 2)
                mm(pG[:, 0:T], xbc[:, 2, 0:P], xbc[:, 3, :], start=True, stop=True).then_inc(S["g_done"], 1)
                mm(pG[:, T:T + P], xbc[:, 2, P:T], xbc[:, 3, P:T], start=True, stop=True).then_inc(S["g_done"], 1)

            def segment(b, k):
                s, t = ((0, 0), (0, 1), (1, 1))[k]
                if k == 0:
                    pe.wait_ge(S["rows_in"], 96 * (b + 1))
                if k == 1:
                    pe.wait_ge(S["ysum_ready"], b)
                elif k == 2 or has(b, -1):
                    pe.wait_ge(S["decay_ready"], 3 * b + (1 if k else 0))
                o = pS[k][:, :].rearrange("p (h t) -> p h t", h=HEADS)
                mm(o, ones3[:, :], cum_t[:, :, t * P:(t + 1) * P], start=True, stop=False)
                last = mm(o, cum_s[:, s * P:(s + 1) * P], minus_head[:, :, :], start=False, stop=s != t)
                if s == t:
                    last = mm(o, ident_bf[:, :], mask[:, :, :], start=False, stop=True)
                last.then_inc(S["seg_done"], 1)

            def recur(b):
                pe.wait_ge(S["mix_ready"], 3 * b + 3)
                pe.wait_ge(S["x_scaled"], 2 * b + 1)
                for h in range(HEADS):
                    c = slice(h * HD, (h + 1) * HD)
                    mm(pY[:, c], mix[:, 0, h, :], dtx[:, 0, c], start=True, stop=True)
                for h in range(HEADS):
                    c = slice(h * HD, (h + 1) * HD)
                    o = pY[:, DI + h * HD:DI + (h + 1) * HD]
                    mm(o, mix[:, 1, h, :], dtx[:, 0, c], start=True, stop=False)
                    last = mm(o, mix[:, 2, h, :], dtx[:, 1, c], start=False, stop=True)
                last.then_inc(S["y_done"], 1)

            def gated_T(b):
                pe.wait_ge(S["yg_ready"], b + 1)
                for k in range(2):
                    for j in range(TJ):
                        nc.tensor.transpose(pB[:, k * T + j * P:k * T + (j + 1) * P], yg[:, j, k * P:(k + 1) * P],
                                            ident[:, :]).then_inc(S["ygT_done"], 1)

            def out_proj(b):
                pe.wait_ge(S["ygT_ready"], b + 1)
                pe.wait_ge(S["yT_ready"], b)
                for j in range(TJ):
                    o = pO[:, j * D:(j + 1) * D]
                    mm(o, ygT[:, 0, j * P:(j + 1) * P], out_wT[:, 0, :], start=True, stop=False)
                    mm(o, ygT[:, 1, j * P:(j + 1) * P], out_wT[:, 1, :], start=False, stop=True).then_inc(S["yo_done"], 1)

            def y_T(b):
                pe.wait_ge(S["y_ready"], 2 * b + 2)
                for j in range(TJ):
                    nc.tensor.transpose(pYT[:, j * P:(j + 1) * P], ybuf[:, j, :], ident[:, :]).then_inc(S["yT_done"], 1)

            def scorer(b):
                pe.wait_ge(S["yT_ready"], b + 1)
                pe.wait_ge(S["mix_ready"], 3 * b + (6 if has(b, 1) else 3))
                mm(pG[0:HID, 0:T], sw1T[:, :], yTbuf[:, :], start=True, stop=True).then_inc(S["h_done"], 1)

            def scorer_row(b):
                pe.wait_ge(S["h_ready"], b + 1)
                mm(pG[:, T:2 * T], sw2_bc[:, :], hsc[:, :], start=True, stop=True).then_inc(S["row_done"], 1)

            def layer1(b, par, half):
                if half == 0:
                    pe.wait_ge(S["xT_hi_ready"], b + 1)
                    pe.wait_ge(S["xT_lo_ready"], b + 1)
                    pe.wait_ge(S["g_ready"], 2 * b)
                else:
                    pe.wait_ge(S["h2_hi_ready"], 2 * b)
                    pe.wait_ge(S["h2_lo_ready"], 2 * b)
                for i in range(2):
                    m = 2 * half + i
                    o = F[half][:, i * T:(i + 1) * T]
                    mm(o, k0_16[:, m * P:(m + 1) * P], xT_hi[:, par, :], start=True, stop=False)
                    last = mm(o, k0_16[:, m * P:(m + 1) * P], xT_lo[:, par, :], start=False, stop=True)
                last.then_inc(S["l1_done"], 1)

            def layer2(b, half, quarters=(0, 1)):
                if half == 0 and 0 in quarters:
                    pe.wait_ge(S["h1_hi_ready"], 2 * b + 2)
                    pe.wait_ge(S["h1_lo_ready"], 2 * b + 2)
                for i in quarters:
                    m = 2 * half + i
                    o = F[half][:, i * T:(i + 1) * T]
                    for k in range(FB):
                        mm(o, k1_16[:, k, m * P:(m + 1) * P], h1_hi[:, k, :], start=k == 0, stop=False)
                        last = mm(o, k1_16[:, k, m * P:(m + 1) * P], h1_lo[:, k, :], start=False, stop=k == FB - 1)
                if 1 in quarters:
                    last.then_inc(S["l2_done"], 1)

            def layer3(b):
                pe.wait_ge(S["h2_hi_ready"], 2 * b + 2)
                pe.wait_ge(S["h2_lo_ready"], 2 * b + 2)
                for j in range(TJ):
                    o = F[0][:, j * D:(j + 1) * D]
                    t = slice(j * P, (j + 1) * P)
                    for k in range(FB):
                        mm(o, h2_hi[:, k, t], k2_16[:, k, :], start=k == 0, stop=False)
                        last = mm(o, h2_lo[:, k, t], k2_16[:, k, :], start=False, stop=k == FB - 1)
                last.then_inc(S["l3_done"], 1)

            pe.wait_ge(S["w_ev"], N_JOBS + 5)
            pe.wait_ge(S["w_split"], 2)
            pe.wait_ge(S["w_mlp"], 4)
            pe.wait_ge(S["consts"], 7)
            norm_T(0)
            dt_proj(0, 0)
            conv_proj(0, 0, 0)
            conv_proj(0, 0, 1)
            z_proj(0, 0)
            cum(0)

            def step(b, par, half):
                x_by_token(b)
                layer1(b, par, 0)
                layer1(b, par, 1)
                if has(b, 1):
                    norm_T(b + 1)
                scores(b)
                if has(b, -1):
                    pe.wait_ge(S["xtok_ready"], b + 1)
                    gated_T(b - 1)
                layer2(b, 0, (0,))
                if has(b, 1):
                    dt_proj(b + 1, 1 - par)
                layer2(b, 0, (1,))
                if has(b, 1):
                    conv_proj(b + 1, 1 - par, 0)
                segment(b, 0)
                if has(b, -1):
                    out_proj(b - 1)
                segment(b, 1)
                if has(b, 1):
                    pe.wait_ge(S["xtok_ready"], b + 1)
                    if has(b, -1):
                        pe.wait_ge(S["ygT_ready"], b)
                    conv_proj(b + 1, 1 - par, 1)
                layer2(b, 1, (0,))
                if has(b, -1):
                    y_T(b - 1)
                segment(b, 2)
                layer2(b, 1, (1,))
                if has(b, 1):
                    z_proj(b + 1, 1 - par)
                layer3(b)
                if has(b, -1):
                    scorer(b - 1)
                recur(b)
                if has(b, -1):
                    scorer_row(b - 1)
                if has(b, 1):
                    cum(b + 1)

            steps(pe, step)
            pe.wait_ge(S["xtok_ready"], NB)
            gated_T(NB - 1)
            out_proj(NB - 1)
            y_T(NB - 1)
            scorer(NB - 1)
            scorer_row(NB - 1)

            pe.wait_ge(S["slots_done"], 1)
            for j in range(TJ):
                nc.tensor.transpose(bank[0][:, j * NB:(j + 1) * NB], slot[:, j * P:(j + 1) * P], ident[0:NB, 0:NB]).then_inc(S["slotT_done"], 1)
            mm(bank[1][:, 0:2 * NB], ones32[0:NB, :], diag2[:, :, :], start=True, stop=True).then_inc(S["slotT_done"], 1)
            pe.wait_ge(S["slotT_ready"], 2)

            def gather(n, par, half):
                pe.wait_ge(S["onehot_ready"], n + 1)
                pe.wait_ge(y_in[par], 16 * (half + 1))
                pe.wait_ge(S["m_ready"], n)
                for q in range(PAIR):
                    for j in range(TJ):
                        last = mm(bank[0][:, q * POOL:(q + 1) * POOL], yin[:, par, q, j, :], onehot[:, j, q, :],
                                  start=j == 0, stop=j == TJ - 1)
                last.then_inc(S["s_done"], 1)

            def pool_vectors(n):
                pe.wait_ge(S["sT_ready"], n + 1)
                mm(bank[0][:, 256:256 + PAIR * POOL], wmT[:, :], sT[:, :, :], start=True, stop=True).then_inc(S["m_done"], 1)
                pe.wait_ge(S["vv_ready"], n)
                for q in range(PAIR):
                    last = mm(bank[1][0:POOL, q * 2 * D:(q + 1) * 2 * D], sT[:, q, :], wvv[:, :], start=True, stop=True)
                last.then_inc(S["vv_done"], 1)

            def logits(n, par, half):
                pe.wait_ge(S["m_ready"], n + 1)
                pe.wait_ge(yT_in[par], 16 * (half + 1))
                pe.wait_ge(S["lm_ready"], n)
                for q in range(PAIR):
                    for j in range(TJ):
                        c = (q * TJ + j) * POOL
                        last = mm(bank[2][:, c:c + POOL], yTin[:, par, q, j * P:(j + 1) * P], m_sb[:, q, :], start=True, stop=True)
                last.then_inc(S["lg_done"], 1)

            def attention_T(b):
                pe.wait_ge(S["at_ready"], b + 1)
                pe.wait_ge(S["atT_ready"], b)
                for q in range(PAIR):
                    for j in range(TJ):
                        c = (q * TJ + j) * P
                        last = mm(bank[3][0:POOL, c:c + P], at[:, q * TJ + j, :], ident[:, :], start=True, stop=True)
                last.then_inc(S["atT_done"], 1)

            def retrieve(b, par):
                pe.wait_ge(S["atT_ready"], b + 1)
                pe.wait_ge(S["vv_ready"], b + 1)
                if has(b, -1, NG):
                    pe.wait_ge(S["fin_step"], FIN * (b - 1))
                for q in range(PAIR):
                    for j in range(TJ):
                        o = bank[4 + 2 * par + q][:, j * 2 * D:(j + 1) * 2 * D]
                        mm(o, atT[:, (q * TJ + j) * P:(q * TJ + j + 1) * P], vv[:, q, :], start=True, stop=False)
                        last = mm(o[:, D:2 * D], yTin[:, par, q, j * P:(j + 1) * P], gate1T[:, :], start=False, stop=True)
                    last.then_inc(S["rg_done"], 1)

            gather(0, 0, 0)
            pool_vectors(0)
            logits(0, 0, 0)

            def step2(b, par, half):
                if has(b, 1, NG):
                    gather(b + 1, 1 - par, half + par)
                attention_T(b)
                retrieve(b, par)
                if has(b, 1, NG):
                    pool_vectors(b + 1)
                    logits(b + 1, 1 - par, half + par)

            steps(pe, step2, NG)

        @block.scalar
        def _(act):
            go = nc.scalar.activation
            act.wait_ge(S["weights_in"], 16 * (N_W + 1))
            go(aexp[:, :], alog_bc[:, :], ACT.Exp).then_inc(S["w_exp"], 1)
            act.wait_ge(S["w_ev"], 7)
            go(wt_hi[:, :], wt32[:, :], ACT.Copy).then_inc(S["w_split"], 1)

            def xT_high(n, par):
                act.wait_ge(S["xT_done"], TJ * (n + 1))
                if has(n, -2):
                    act.wait_ge(S["l1_done"], 2 * (n - 1))
                go(xT_hi[:, par, :], pA[:, 0:T], ACT.Copy).then_inc(S["xT_hi_ready"], 1)

            def exp_dt(n):
                act.wait_ge(S["abs_ready"], 2 * n + 2)
                go(sp[:, 2, :], sp[:, 1, :], ACT.Exp).then_inc(S["u_ready"], 1)

            def conv_start(n, half):
                src = pB if half else pA
                act.wait_ge(S["proj_done"], 4 * n + 2 * half + 2)
                act.wait_ge(S["xbc_ready"], 2 * n)
                go(pre[:, 2 * half:2 * half + 2, PAD:], src[:, :].rearrange("p (c t) -> p c t", c=2), ACT.Copy).then_inc(S["pre_ready"], 1)
                for i in range(2):
                    c = 2 * half + i
                    go(acc[:, c, :], src[:, i * T:(i + 1) * T], ACT.Identity, bias=cb_sb[:, c:c + 1],
                       scale=cw[:, c, TAPS - 1:TAPS]).then_inc(S["pre_ready"], 1)

            def conv_tanh(n, half):
                act.wait_ge(S["conv_step"], 12 * n + 6 * half + 6)
                act.wait_ge(S["xbc_ready"], 2 * n)
                go(cth[:, 2 * half:2 * half + 2, :], acc[:, 2 * half:2 * half + 2, :], ACT.Tanh, scale=0.5).then_inc(S["cth_ready"], 1)

            def z_tanh(n):
                act.wait_ge(S["z_done"], TJ * (n + 1))
                act.wait_ge(S["zg_ready"], n)
                go(zth[:, :, :], pA[:, :].rearrange("p (j c) -> p j c", j=TJ), ACT.Tanh, scale=0.5 / WS).then_inc(S["zth_ready"], 1)

            def cum_out(n):
                act.wait_ge(S["cum_done"], n + 1)
                act.wait_ge(S["rows_in"], 96 * n)
                act.wait_ge(S["parts_ready"], n)
                go(parts[:, 0, :], pG[0:HEADS, 0:T], ACT.Copy).then_inc(S["craw_ready"], 1)
                go(craw[:, :], pG[0:HEADS, 0:T], ACT.Copy).then_inc(S["craw_ready"], 1)

            def hidden_high(b, layer, half):
                done, ready = (("l1_done", "h1_hi_ready"), ("l2_done", "h2_hi_ready"))[layer]
                act.wait_ge(S[done], 2 * b + half + 1)
                if half == 0:
                    if layer == 0:
                        act.wait_ge(S["l2_done"], 2 * b)
                    else:
                        act.wait_ge(S["l3_done"], b)
                dst = (h1_hi, h2_hi)[layer]
                go(dst[:, 2 * half:2 * half + 2, :], F[half][:, :].rearrange("p (c t) -> p c t", c=2), ACT.Relu).then_inc(S[ready], 1)

            def decay_exp(b, k):
                act.wait_ge(S["seg_done"], 3 * b + k + 1)
                if k == 0:
                    act.wait_ge(S["mix_ready"], 3 * b)
                go(decay[:, k, :, :], pS[k][:, :].rearrange("p (h t) -> p h t", h=HEADS), ACT.Exp).then_inc(S["decay_ready"], 1)

            def x_out(b):
                act.wait_ge(S["xtok_done"], 4 * b + 4)
                act.wait_ge(S["x_scaled"], 2 * b)
                go(xtok[:, :, :], pB[:, :].rearrange("p (j c) -> p j c", j=TJ), ACT.Copy).then_inc(S["xtok_ready"], 1)

            def mlp_tanh(b):
                act.wait_ge(S["l3_done"], b + 1)
                act.wait_ge(S["gth1_ready"], b)
                for j in range(TJ):
                    go(gth[:, j, :], F[0][:, j * D:(j + 1) * D], ACT.Tanh,
                       scale=norms[:, 2, bass.ds(b, 1), j:j + 1].squeeze(1)).then_inc(S["gth_ready"], 1)

            def squares(b):
                act.wait_ge(S["yg_ready"], b + 1)
                act.wait_ge(S["rstd_step"], 2 * b)
                for j in range(TJ):
                    go(ysq[:, j, :], yg[:, j, :], ACT.Square, accum_out=ss[:, j:j + 1]).then_inc(S["ss_ready"], 1)

            def gated_T_out(b):
                act.wait_ge(S["ygT_done"], 4 * b + 4)
                act.wait_ge(S["yo_done"], 2 * b)
                go(ygT[:, :, :], pB[:, :].rearrange("p (k t) -> p k t", k=2), ACT.Copy).then_inc(S["ygT_ready"], 1)

            def y_out(b):
                act.wait_ge(S["yo_done"], 2 * b + 2)
                act.wait_ge(S["rstd_ready"], b + 1)
                act.wait_ge(S["y_saved"], 16 * b)
                act.wait_ge(S["yT_done"], 2 * b)
                for j in range(TJ):
                    go(ybuf[:, j, :], pO[:, j * D:(j + 1) * D], ACT.Copy, scale=rstd[:, j:j + 1]).then_inc(S["y_ready"], 1)

            def y_T_out(b):
                act.wait_ge(S["yT_done"], 2 * b + 2)
                act.wait_ge(S["yT_saved"], 16 * b)
                act.wait_ge(S["h_done"], b)
                go(yTbuf[:, :], pYT, ACT.Copy).then_inc(S["yT_ready"], 1)

            def scorer_out(b):
                act.wait_ge(S["h_done"], b + 1)
                act.wait_ge(S["row_done"], b)
                go(hsc[:, :], pG[0:HID, 0:T], ACT.Relu).then_inc(S["h_ready"], 1)

            def row_out(b):
                act.wait_ge(S["row_done"], b + 1)
                act.wait_ge(S["yT_ready"], b + 1)
                act.wait_ge(S["row_saved"], 16 * b)
                go(row[:, :], pG[0:1, T:2 * T], ACT.Copy).then_inc(S["row_ready"], 1)
                act.dma_start(yTall[:, bass.ds(b, 1), :], yTbuf[:, :].unsqueeze(1)).then_inc(S["yT_saved"], 16)
                act.wait_ge(S["row_ready"], b + 1)
                act.dma_start(importance[bass.ds(b, 1), :], row[:, :]).then_inc(S["row_saved"], 16)

            act.wait_ge(S["pads"], 1)
            act.wait_ge(S["w_dve"], 1)
            xT_high(0, 0)
            exp_dt(0)
            conv_start(0, 0)
            conv_start(0, 1)
            conv_tanh(0, 0)
            conv_tanh(0, 1)
            z_tanh(0)
            cum_out(0)

            def step(b, par, half):
                x_out(b)
                hidden_high(b, 0, 0)
                hidden_high(b, 0, 1)
                if has(b, 1):
                    xT_high(b + 1, 1 - par)
                if has(b, -1):
                    gated_T_out(b - 1)
                    squares(b - 1)
                if has(b, 1):
                    exp_dt(b + 1)
                hidden_high(b, 1, 0)
                if has(b, 1):
                    conv_start(b + 1, 0)
                decay_exp(b, 0)
                if has(b, -1):
                    y_out(b - 1)
                decay_exp(b, 1)
                if has(b, 1):
                    conv_start(b + 1, 1)
                if has(b, -1):
                    y_T_out(b - 1)
                decay_exp(b, 2)
                hidden_high(b, 1, 1)
                if has(b, 1):
                    z_tanh(b + 1)
                    conv_tanh(b + 1, 0)
                mlp_tanh(b)
                if has(b, -1):
                    scorer_out(b - 1)
                if has(b, 1):
                    conv_tanh(b + 1, 1)
                if has(b, -1):
                    row_out(b - 1)
                if has(b, 1):
                    cum_out(b + 1)

            steps(act, step)
            squares(NB - 1)
            gated_T_out(NB - 1)
            y_out(NB - 1)
            y_T_out(NB - 1)
            scorer_out(NB - 1)
            row_out(NB - 1)

            act.wait_ge(S["keys_in"], 16)
            go(th16[:, :], logit[:, :], ACT.Tanh, scale=0.5, accum_out=col[:, 4:5]).then_inc(S["th16_ready"], 1)

            def pool_out(n):
                act.wait_ge(S["s_done"], n + 1)
                act.wait_ge(S["vv_done"], n)
                go(sT[:, :, :], bank[0][:, 0:PAIR * POOL].rearrange("p (q c) -> p q c", q=PAIR), ACT.Copy).then_inc(S["sT_ready"], 1)
                act.wait_ge(S["m_done"], n + 1)
                act.wait_ge(S["lg_done"], n)
                go(m_sb[:, :, :], bank[0][:, 256:256 + PAIR * POOL].rearrange("p (q c) -> p q c", q=PAIR), ACT.Copy).then_inc(S["m_ready"], 1)
                act.wait_ge(S["vv_done"], n + 1)
                act.wait_ge(S["rg_done"], PAIR * n)
                go(vv[:, :, :], bank[1][0:POOL, :].rearrange("p (q c) -> p q c", q=PAIR), ACT.Copy).then_inc(S["vv_ready"], 1)

            def soft_exp(n):
                act.wait_ge(S["ls_ready"], n + 1)
                act.wait_ge(S["at_ready"], n)
                go(ex[:, :, :], ls[:, :, :], ACT.Exp, scale=0.25).then_inc(S["ex_ready"], 1)

            def attention_out(b):
                act.wait_ge(S["atT_done"], b + 1)
                act.wait_ge(S["rg_done"], PAIR * b)
                go(atT[:, :], bank[3][0:POOL, :], ACT.Copy).then_inc(S["atT_ready"], 1)

            def gate_tanh(b, par):
                for q in range(PAIR):
                    act.wait_ge(S["rg_done"], PAIR * b + q + 1)
                    if q == 0:
                        act.wait_ge(S["fin_step"], FIN * b)
                    go(gate[:, q, :, :], bank[4 + 2 * par + q][:, :].rearrange("p (j c) -> p j c", j=TJ)[:, :, D:2 * D],
                       ACT.Tanh, scale=0.5).then_inc(S["gate_ready"], 1)

            pool_out(0)
            soft_exp(0)

            def step2(b, par, half):
                attention_out(b)
                if has(b, 1, NG):
                    pool_out(b + 1)
                gate_tanh(b, par)
                if has(b, 1, NG):
                    soft_exp(b + 1)

            steps(act, step2, NG)

        @block.vector
        def _(dve):
            v = nc.vector
            dve.wait_ge(S["weights_in"], 16 * (N_W + 1))
            v.tensor_scalar(sgn[:, :], s_bc[:, :], 0.0, None, ALU.is_gt).then_inc(S["w_small"], 1)
            v.tensor_scalar(sneg[:, :], s_bc[:, :], 0.0, None, ALU.is_lt).then_inc(S["w_small"], 1)
            dve.wait_ge(S["w_small"], 2)
            v.tensor_tensor(sgn[:, :], sgn[:, :], sneg[:, :], ALU.subtract).then_inc(S["w_small"], 1)
            dve.wait_ge(S["w_small"], 3)
            v.tensor_tensor(sabs[:, :], sgn[:, :], s_bc[:, :], ALU.mult).then_inc(S["w_small"], 1)
            v.tensor_scalar(c1[:, :], sgn[:, 1:2], 2.0 / H2S, None, ALU.mult).then_inc(S["w_small"], 1)
            v.tensor_scalar(c2[:, :], sgn[:, 1:2], -1.0 / H2S, None, ALU.mult).then_inc(S["w_small"], 1)
            dve.wait_ge(S["w_small"], 6)
            v.tensor_scalar(sprod[:, :], sabs[:, 0:1], sabs[:, 1:2], 4.0 * H2S, ALU.mult, ALU.mult).then_inc(S["w_small"], 1)
            dve.wait_ge(S["w_small"], 7)
            v.tensor_scalar(fhalf[:, :], s_bc[:, 2:3].broadcast_to([P, 2]), sprod[:, :], None, ALU.mult).then_inc(S["w_small"], 1)
            v.tensor_scalar(cw[:, :, :], cw_ld[:, :, :], 1.0 / WS, None, ALU.mult).then_inc(S["w_dve"], 1)
            v.tensor_scalar(dhalf[:, :].rearrange("p (h d) -> p h d", h=HEADS),
                            dpar_bc[:, :].unsqueeze(2).broadcast_to([P, HEADS, HD]), 0.5, None, ALU.mult).then_inc(S["w_small"], 1)
            v.tensor_copy(sw2_bc[:, :], sw2_ld[:, :].broadcast_to([HID, P])).then_inc(S["w_mlp"], 1)
            v.memset(pre[:, :, 0:PAD], 0.0).then_inc(S["pads"], 1)
            dve.wait_ge(S["w_exp"], 1)
            v.tensor_scalar(negA[:, :], aexp[:, :], -1.0, None, ALU.mult).then_inc(S["w_small"], 1)

            def out_of(t, dst, src, *scale):
                dve.wait_ge(S["w_T"], t + 1)
                if scale:
                    v.tensor_scalar(dst, src, scale[0], scale[1], ALU.mult, ALU.mult).then_inc(S["w_ev"], 1)
                else:
                    v.tensor_copy(dst, src).then_inc(S["w_ev"], 1)

            for t in range(6):
                out_of(t, wt32[:, t * P:(t + 1) * P], bank[t][:, 0:P], nw_col[:, :], WS)
            out_of(6, wt32[:, 6 * P:NIN], bank[6][:, 0:HEADS], nw_col[:, :], WS)
            out_of(7, out_wT[:, 0, :], bank[7][:, 0:P], gw_col[:, 0:1], 1.0)
            out_of(8, out_wT[:, 1, :], bank[0][:, 0:P], gw_col[:, 1:2], 1.0)
            out_of(9, sw1T[:, :], bank[1][:, 0:HID])
            out_of(10, gate1T[:, :], bank[2][:, 0:D])
            out_of(11, gate2T[:, :], bank[3][:, 0:D])
            out_of(12, kwT[:, :], bank[4][0:SDIM, 0:SDIM])
            out_of(13, vwT[:, :], bank[5][0:SDIM, 0:D])
            out_of(14, kp_sb[:, :], bank[0][0:SDIM, 0:D])
            out_of(15, wvv[:, 0:D], bank[1][:, 0:D])
            out_of(16, wv_sb[:, :], bank[2][:, 0:D])
            out_of(17, wmT[:, :], bank[3][:, 0:D])
            out_of(18, wvv[:, D:2 * D], bank[4][:, 0:D])
            dve.wait_ge(S["w_split"], 1)
            v.tensor_tensor(wt_lo[:, :], wt32[:, :], wt_hi[:, :], ALU.subtract).then_inc(S["w_split"], 1)
            v.tensor_tensor(k0_d[:, :], k0_ld[:, 0, :], k0_ld[:, 1, :], ALU.subtract).then_inc(S["w_small"], 1)
            dve.wait_ge(S["w_small"], 11)
            v.tensor_scalar(k0_16[:, :], k0_d[:, :], sgn[:, 0:1], None, ALU.mult).then_inc(S["w_mlp"], 1)
            v.tensor_scalar(k1_16[:, :, :], k1_ld[:, :, :], c1[:, :], c2[:, :], ALU.mult, ALU.add).then_inc(S["w_mlp"], 1)
            v.tensor_scalar(k2_16[:, :, :], k2_ld[:, :, :], 2.0, -1.0, ALU.mult, ALU.add).then_inc(S["w_mlp"], 1)

            def stats(n, par, half):
                dve.wait_ge(x_in[par], 16 * (half + 1))
                for j in range(TJ):
                    v.bn_stats(st6[:, j, :], xall[:, bass.ds(n, 1), j, :].squeeze(1)).then_inc(S["stats"], 1)

            def mean_var(n):
                for j in range(TJ):
                    v.bn_aggr(mv[:, j, :], st6[:, j, :]).then_inc(S["mv_ready"], 1)

            def normed(n):
                dve.wait_ge(S["norm_ready"], n + 1)
                dve.wait_ge(S["xT_done"], TJ * n)
                for j in range(TJ):
                    v.tensor_scalar(xn[:, j, :], xall[:, bass.ds(n, 1), j, :].squeeze(1), lt[:, 5, j:j + 1],
                                    lt[:, 6, j:j + 1], ALU.mult, ALU.add).then_inc(S["xn_ready"], 1)

            def xT_low(n, par):
                dve.wait_ge(S["xT_hi_ready"], n + 1)
                v.tensor_tensor(xT_lo[:, par, :], pA[:, 0:T], xT_hi[:, par, :], ALU.subtract).then_inc(S["xT_lo_ready"], 1)

            def dt_raw(n):
                dve.wait_ge(S["dt_done"], TJ * (n + 1))
                dve.wait_ge(S["sp_step"], SP_STEPS * n)
                dve.wait_ge(S["u_ready"], n)
                v.scalar_tensor_tensor(raw[:, :, :], pDT.rearrange("p (j h) -> p j h", j=TJ), 1.0 / WS,
                                       dtb_bc[:, :].unsqueeze(1).broadcast_to([P, TJ, HEADS]), ALU.mult, ALU.add).then_inc(S["raw_ready"], 1)
                r = raw[:, :, :].rearrange("p j h -> p (j h)")
                dve.wait_ge(S["raw_ready"], n + 1)
                v.tensor_scalar(sp[:, 0, :], r, 0.0, None, ALU.max).then_inc(S["abs_ready"], 1)
                v.scalar_tensor_tensor(sp[:, 1, :], r, -1.0, r, ALU.mult, ALU.min).then_inc(S["abs_ready"], 1)

            def dt_recip(n):
                dve.wait_ge(S["den_ready"], n + 1)
                v.reciprocal(sp[:, 4, :], sp[:, 3, :]).then_inc(S["rden_ready"], 1)

            def conv(n, half):
                dve.wait_ge(S["pre_ready"], 6 * n + 3 * half + 3)
                for k in range(PAD):
                    for i in range(2):
                        c = 2 * half + i
                        if k:
                            dve.wait_ge(S["conv_step"], 12 * n + 6 * half + 2 * k + i - 1)
                        v.scalar_tensor_tensor(acc[:, c, :], pre[:, c, k:k + T], cw[:, c, k:k + 1], acc[:, c, :],
                                               ALU.mult, ALU.add).then_inc(S["conv_step"], 1)

            def conv_silu(n, half):
                dve.wait_ge(S["cth_ready"], 2 * n + half + 1)
                dve.wait_ge(S[("xtok_done", "g_done")[half]], (4, 2)[half] * n)
                c = slice(2 * half, 2 * half + 2)
                v.scalar_tensor_tensor(xbc[:, c, :], cth[:, c, :], 1.0, acc[:, c, :], ALU.add, ALU.mult).then_inc(S["xbc_ready"], 1)

            def z_gate(n):
                dve.wait_ge(S["zth_ready"], n + 1)
                dve.wait_ge(S["yg_ready"], n)
                v.scalar_tensor_tensor(zg[:, :, :], zth[:, :, :], 1.0, pA[:, :].rearrange("p (j c) -> p j c", j=TJ),
                                       ALU.add, ALU.mult).then_inc(S["zg_ready"], 1)

            def hidden_low(b, layer, half):
                hi, lo = ((h1_hi, h1_lo), (h2_hi, h2_lo))[layer]
                dve.wait_ge(S[("h1_hi_ready", "h2_hi_ready")[layer]], 2 * b + half + 1)
                c = slice(2 * half, 2 * half + 2)
                v.scalar_tensor_tensor(lo[:, c, :], F[half][:, :].rearrange("p (c t) -> p c t", c=2), 0.0, hi[:, c, :],
                                       ALU.max, ALU.subtract).then_inc(S[("h1_lo_ready", "h2_lo_ready")[layer]], 1)

            def mixing(b, k):
                dve.wait_ge(S["decay_ready"], 3 * b + k + 1)
                dve.wait_ge(S["g_done"], 2 * b + 2)
                if k == 0:
                    dve.wait_ge(S["y_done"], b)
                v.tensor_tensor(mix[:, k, :, :], decay[:, k, :, :],
                                pG[:, k * P:(k + 1) * P].unsqueeze(1).broadcast_to([P, HEADS, P]), ALU.mult).then_inc(S["mix_ready"], 1)

            def gated(b):
                dve.wait_ge(S["y_done"], b + 1)
                dve.wait_ge(S["x_scaled"], 2 * b + 2)
                v.tensor_tensor(ysum[:, :, :], pY[:, :].rearrange("p (j c) -> p j c", j=TJ), xD[:, :, :], ALU.add).then_inc(S["ysum_ready"], 1)
                dve.wait_ge(S["ysum_ready"], b + 1)
                dve.wait_ge(S["zg_ready"], b + 1)
                dve.wait_ge(S["ygT_done"], 4 * b)
                dve.wait_ge(S["ss_ready"], 2 * b)
                v.tensor_tensor(yg[:, :, :], ysum[:, :, :], zg[:, :, :], ALU.mult).then_inc(S["yg_ready"], 1)

            def mlp_out(b):
                dve.wait_ge(S["gth_ready"], 2 * b + 2)
                dve.wait_ge(S["g_ready"], 2 * b)
                v.tensor_scalar(gth1[:, :, :], gth[:, :, :], 1.0, None, ALU.add).then_inc(S["gth1_ready"], 1)
                dve.wait_ge(S["gth1_ready"], b + 1)
                for j in range(TJ):
                    v.scalar_tensor_tensor(gall[:, bass.ds(b, 1), j, :].squeeze(1), F[0][:, j * D:(j + 1) * D],
                                           norms[:, 2, bass.ds(b, 1), j:j + 1].squeeze(1), gth1[:, j, :],
                                           ALU.mult, ALU.mult).then_inc(S["g_ready"], 1)

            stats(0, 0, 0)
            dve.wait_ge(S["stats"], TJ)
            mean_var(0)
            normed(0)
            stats(1, 1, 0)
            dve.wait_ge(S["stats"], 2 * TJ)
            dve.wait_ge(S["norm_kept"], 2)
            mean_var(1)
            xT_low(0, 0)
            dt_raw(0)
            dt_recip(0)
            conv(0, 0)
            conv_silu(0, 0)
            conv(0, 1)
            z_gate(0)
            conv_silu(0, 1)
            normed(1)

            def step(b, par, half):
                hidden_low(b, 0, 0)
                hidden_low(b, 0, 1)
                if has(b, 1):
                    xT_low(b + 1, 1 - par)
                if has(b, 2):
                    stats(b + 2, par, half + 1)
                if has(b, 1):
                    dt_raw(b + 1)
                if has(b, 2):
                    dve.wait_ge(S["stats"], TJ * (b + 3))
                    dve.wait_ge(S["norm_kept"], 2 * b + 4)
                hidden_low(b, 1, 0)
                if has(b, 2):
                    mean_var(b + 2)
                if has(b, 1):
                    dt_recip(b + 1)
                mixing(b, 0)
                if has(b, 1):
                    conv(b + 1, 0)
                mixing(b, 1)
                mixing(b, 2)
                hidden_low(b, 1, 1)
                if has(b, 1):
                    conv(b + 1, 1)
                    conv_silu(b + 1, 0)
                gated(b)
                if has(b, 1):
                    conv_silu(b + 1, 1)
                    z_gate(b + 1)
                mlp_out(b)
                if has(b, 2):
                    normed(b + 2)

            steps(dve, step)

            dve.wait_ge(S["keys_in"], 16)
            k = 0

            def link(ins):
                nonlocal k
                k += 1
                ins.then_inc(S["sel_step"], 1)
                dve.wait_ge(S["sel_step"], k)

            link(v.memset(zero16[:, :], 0.0))
            link(v.tensor_scalar(keys[:, :], logit[:, :], SATURATED, None, ALU.min))
            cur = keys[:, :]
            for r in range(7):
                link(v.max(top8[:, r, :], cur))
                if r < 6:
                    link(v.match_replace(work[:, r % 2, :], top8[:, r, :], cur, -3.0e38))
                    cur = work[:, r % 2, :]
            kth = top8[:, 6, 1:2]
            link(v.tensor_scalar(gt[:, :], keys[:, :], kth, None, ALU.is_gt))
            link(v.tensor_scalar(eq[:, :], keys[:, :], kth, None, ALU.is_equal))
            link(v.tensor_reduce(col[:, 0:1], gt[:, :], AX, ALU.add))
            link(v.tensor_scalar(col[:, 1:2], col[:, 0:1], -1.0, float(POOL), ALU.mult, ALU.add))
            link(v.tensor_tensor_scan(eqc[:, :], eq[:, :], zero16[:, :], 0.0, ALU.add, ALU.add))
            link(v.tensor_scalar(ok[:, :], eqc[:, :], col[:, 1:2], None, ALU.is_le))
            link(v.tensor_tensor(ok[:, :], ok[:, :], eq[:, :], ALU.mult))
            link(v.tensor_tensor(sel[:, :], ok[:, :], gt[:, :], ALU.add))
            link(v.scalar_tensor_tensor(sel[:, :], keys[:, :], 0.0, sel[:, :], ALU.is_gt, ALU.mult))
            link(v.tensor_tensor_scan(selc[:, :], sel[:, :], zero16[:, :], 0.0, ALU.add, ALU.add))
            link(v.tensor_tensor(slot[:, :], selc[:, :], sel[:, :], ALU.mult))
            dve.wait_ge(S["th16_ready"], 1)
            link(v.tensor_scalar(col[:, 2:3], col[:, 4:5], 0.5 / T, 0.5, ALU.mult, ALU.add))
            link(v.tensor_scalar(col[:, 3:4], col[:, 2:3], 0.3, 0.5, ALU.is_gt, ALU.mult))
            link(v.scalar_tensor_tensor(col[:, 5:6], selc[:, T - 1:T], 0.0, col[:, 3:4], ALU.is_gt, ALU.mult))
            link(v.tensor_scalar(diag2[:, 0, :], ident[0:NB, 0:NB], selc[:, T - 1:T], None, ALU.mult))
            v.tensor_scalar(diag2[:, 1, :], ident[0:NB, 0:NB], col[:, 5:6], None, ALU.mult).then_inc(S["slots_done"], 1)
            dve.wait_ge(S["slotT_done"], 3)
            v.tensor_copy(slotT[:, :, :], bank[0][:, 0:TJ * NB].rearrange("p (j b) -> p j b", j=TJ)).then_inc(S["slotT_ready"], 1)
            v.tensor_copy(cnt_rm[:, :, :], bank[1][:, 0:2 * NB].rearrange("p (a b) -> p a b", a=2)).then_inc(S["slotT_ready"], 1)
            dve.wait_ge(S["slotT_ready"], 2)

            def choose(n):
                c = bass.ds(PAIR * n, PAIR)
                dve.wait_ge(S["s_done"], n)
                for j in range(TJ):
                    v.tensor_tensor(onehot[:, j, :, :], slots[:, :].unsqueeze(1).broadcast_to([P, PAIR, POOL]),
                                    slotT[:, j, c].unsqueeze(2).broadcast_to([P, PAIR, POOL]), ALU.is_equal)\
                        .then_inc(S[("choose_step", "onehot_ready")[j]], 1)
                v.tensor_tensor(pover[:, :, :], slots[:, :].unsqueeze(1).broadcast_to([P, PAIR, POOL]),
                                cnt_rm[:, 0, c].unsqueeze(2).broadcast_to([P, PAIR, POOL]), ALU.is_gt).then_inc(S["bias_ready"], 1)

            def softmax_in(n):
                dve.wait_ge(S["lg_done"], n + 1)
                dve.wait_ge(S["bias_ready"], n + 1)
                for q in range(PAIR):
                    v.scalar_tensor_tensor(lm[:, q * TJ:(q + 1) * TJ, :], pover[:, q, :].unsqueeze(1).broadcast_to([P, TJ, POOL]), -4.0e9,
                                           bank[2][:, q * TJ * POOL:(q + 1) * TJ * POOL].rearrange("p (j c) -> p j c", j=TJ),
                                           ALU.mult, ALU.add).then_inc(S[("lm_step", "lm_ready")[q]], 1)
                dve.wait_ge(S["lm_step"], n + 1)
                dve.wait_ge(S["lm_ready"], n + 1)
                v.tensor_reduce(mx[:, :], lm[:, :, :], AX, ALU.max).then_inc(S["max_ready"], 1)
                dve.wait_ge(S["max_ready"], n + 1)
                dve.wait_ge(S["ex_ready"], n)
                v.tensor_tensor(ls[:, :, :], lm[:, :, :], mx[:, :].unsqueeze(2).broadcast_to([P, PAIR * TJ, POOL]), ALU.subtract).then_inc(S["ls_ready"], 1)

            def softmax_out(n):
                dve.wait_ge(S["ex_ready"], n + 1)
                v.tensor_reduce(sm[:, :], ex[:, :, :], AX, ALU.add).then_inc(S["sum_ready"], 1)
                dve.wait_ge(S["sum_ready"], n + 1)
                v.reciprocal(rec[:, :], sm[:, :]).then_inc(S["rec_ready"], 1)
                dve.wait_ge(S["rec_ready"], n + 1)
                dve.wait_ge(S["atT_done"], n)
                v.tensor_tensor(at[:, :, :], ex[:, :, :], rec[:, :].unsqueeze(2).broadcast_to([P, PAIR * TJ, POOL]), ALU.mult).then_inc(S["at_ready"], 1)

            def finish(b, par, half):
                pair = bass.ds(PAIR * b, PAIR)
                dve.wait_ge(S["base_step"], 3 * b + 3)
                for q in range(PAIR):
                    dve.wait_ge(S["gate_ready"], PAIR * b + q + 1)
                    v.scalar_tensor_tensor(fin[:, 0, q, :, :], gate[:, q, :, :], 1.0,
                                           bank[4 + 2 * par + q][:, :].rearrange("p (j c) -> p j c", j=TJ)[:, :, 0:D],
                                           ALU.add, ALU.mult).then_inc(S["fin_step"], 1)
                for q in range(PAIR):
                    dve.wait_ge(S["fin_step"], FIN * b + PAIR + q)
                    v.scalar_tensor_tensor(fin[:, 1, q, :, :], fin[:, 0, q, :, :], cnt_rm[:, 1, bass.ds(PAIR * b + q, 1)],
                                           base[:, 2, q, :, :], ALU.mult, ALU.add).then_inc(S["fin_step"], 1)
                dve.wait_ge(S["fin_step"], FIN * b + 2 * PAIR)
                v.tensor_tensor(fin[:, 2, :, :, :].rearrange("p q j c -> p (q j c)"), fin[:, 1, :, :, :].rearrange("p q j c -> p (q j c)"),
                                gall[:, pair, :, :].rearrange("p q j c -> p (q j c)"), ALU.mult).then_inc(S["fin_step"], 1)
                dve.wait_ge(S["fin_step"], FIN * b + 2 * PAIR + 1)
                dve.wait_ge(out_done[par], 16 * half)
                v.tensor_tensor(obuf[:, par, :, :, :].rearrange("p q j c -> p (q j c)"), fin[:, 2, :, :, :].rearrange("p q j c -> p (q j c)"),
                                xall[:, pair, :, :].rearrange("p q j c -> p (q j c)"), ALU.add).then_inc(S["out_ready"], 1)

            choose(0)
            softmax_in(0)
            softmax_out(0)

            def step2(b, par, half):
                if has(b, 1, NG):
                    choose(b + 1)
                    softmax_in(b + 1)
                finish(b, par, half)
                if has(b, 1, NG):
                    softmax_out(b + 1)

            steps(dve, step2, NG)

        @block.gpsimd
        def _(pool):
            g = nc.gpsimd
            g.memset(ident[:, :], 0.0).then_inc(S["ln_step"], 1)
            pool.wait_ge(S["ln_step"], 1)
            g.affine_select(out=ident[:, :], in_=ident[:, :], compare_op=ALU.not_equal, fill=1.0, base=0,
                            pattern=[[-1, P]], channel_multiplier=1).then_inc(S["consts"], 1)
            pool.wait_ge(S["consts"], 1)
            g.tensor_copy(ident_bf[:, :], ident[:, :]).then_inc(S["consts"], 1)
            g.memset(ones32[:, :], 1.0).then_inc(S["consts"], 1)
            g.memset(ones3[:, :], 1.0).then_inc(S["consts"], 1)
            g.memset(upto[:, :], 1.0).then_inc(S["ln_step"], 1)
            g.memset(mask[:, :, :], 0.0).then_inc(S["ln_step"], 1)
            g.memset(minus_head[:, :, :], 0.0).then_inc(S["ln_step"], 1)
            pool.wait_ge(S["ln_step"], 4)
            g.affine_select(out=upto[:, 0:P], in_=upto[:, 0:P], compare_op=ALU.is_ge, fill=0.0, base=0,
                            pattern=[[1, P]], channel_multiplier=-1).then_inc(S["consts"], 1)
            g.affine_select(out=mask[:, :, :], in_=mask[:, :, :], compare_op=ALU.is_ge, fill=NEG, base=0,
                            pattern=[[0, HEADS], [1, P]], channel_multiplier=-1).then_inc(S["consts"], 1)
            for q in range(3):
                ins = g.affine_select(out=minus_head[:, :, :], in_=minus_head[:, :, :], compare_op=ALU.not_equal, fill=-1.0,
                                      base=-HEADS * q, pattern=[[-1, HEADS], [0, P]], channel_multiplier=1)
                ins.then_inc(S["ln_step"], 1)
                pool.wait_ge(S["ln_step"], 5 + q)
            g.iota(slots[:, :], pattern=[[1, POOL]], base=1, channel_multiplier=0,
                   allow_small_or_imprecise_dtypes=True).then_inc(S["consts"], 1)
            for c, value in enumerate(NUMS.values()):
                g.memset(nums[:, c:c + 1], value).then_inc(S["ln_step"], 1)
            SETUP = 7 + len(NUMS)
            pool.wait_ge(S["ln_step"], SETUP)
            pool.wait_ge(S["w_small"], 10)

            def norm(n):
                k = 0

                def link(ins):
                    nonlocal k
                    k += 1
                    ins.then_inc(S["ln_step"], 1)
                    pool.wait_ge(S["ln_step"], LN_STEPS * n + (SETUP + k))

                pool.wait_ge(S["mv_ready"], TJ * (n + 1))
                pool.wait_ge(S["xn_ready"], TJ * n)
                mean, var = mv[:, :, 0], mv[:, :, 1]
                link(g.tensor_tensor(lt[:, 0, :], var, num("eps", P, TJ), ALU.add))
                link(g.tensor_tensor(lnw[:, 0, :], lt[:, 0, :], num("-1/2", P, TJ), ALU.pow))
                link(g.tensor_tensor(lt[:, 1, :], var, lnw[:, 0, :], ALU.mult))
                link(g.tensor_tensor(lt[:, 2, :], lt[:, 1, :], lnw[:, 0, :], ALU.mult))
                link(g.tensor_tensor(lt[:, 2, :], lt[:, 2, :], num("eps", P, TJ), ALU.add))
                link(g.tensor_tensor(lt[:, 3, :], lt[:, 2, :], num("-1/2", P, TJ), ALU.pow))
                link(g.tensor_tensor(lt[:, 5, :], lnw[:, 0, :], lt[:, 3, :], ALU.mult))
                link(g.tensor_tensor(lt[:, 7, :], mean, num("-1", P, TJ), ALU.mult))
                link(g.tensor_tensor(lnw[:, 1, :], lt[:, 7, :], lnw[:, 0, :], ALU.mult))
                g.tensor_tensor(lt[:, 6, :], lnw[:, 1, :], lt[:, 3, :], ALU.mult).then_inc(S["norm_ready"], 1)
                link(g.tensor_tensor(lt[:, 4, :], lt[:, 2, :], num("1/2", P, TJ), ALU.pow))
                g.tensor_tensor(lnw[:, 2, :], lt[:, 4, :], fhalf[:, :], ALU.mult).then_inc(S["norm_kept"], 1)
                pool.wait_ge(S["norm_kept"], 2 * n + 1)
                g.tensor_tensor(norms[:, :, bass.ds(n, 1), :].squeeze(2), lnw[:, :, :], num("1", P, 3, TJ), ALU.mult).then_inc(S["norm_kept"], 1)
                assert k == LN_STEPS

            def scale_x(b):
                pool.wait_ge(S["xtok_ready"], b + 1)
                pool.wait_ge(S["y_done"], b)
                g.tensor_tensor(dtx[:, :, :].rearrange("p j (h d) -> p (j h) d", h=HEADS),
                                xtok[:, :, :].rearrange("p j (h d) -> p (j h) d", h=HEADS),
                                dt8[:, :].unsqueeze(2).broadcast_to([P, TJ * HEADS, HD]), ALU.mult).then_inc(S["x_scaled"], 1)
                pool.wait_ge(S["ysum_ready"], b)
                g.tensor_tensor(xD[:, :, :], xtok[:, :, :], dhalf[:, :].unsqueeze(1).broadcast_to([P, TJ, DI]), ALU.mult).then_inc(S["x_scaled"], 1)

            def softplus(n):
                k = 0

                def link(ins):
                    nonlocal k
                    k += 1
                    ins.then_inc(S["sp_step"], 1)
                    pool.wait_ge(S["sp_step"], SP_STEPS * n + k)

                W = TJ * HEADS
                pool.wait_ge(S["u_ready"], n + 1)
                g.tensor_tensor(sp[:, 3, :], sp[:, 2, :], num("2", P, W), ALU.add).then_inc(S["den_ready"], 1)
                pool.wait_ge(S["rden_ready"], n + 1)
                link(g.tensor_tensor(sp[:, 5, :], sp[:, 2, :], sp[:, 4, :], ALU.mult))
                link(g.tensor_tensor(sp[:, 6, :], sp[:, 5, :], sp[:, 5, :], ALU.mult))
                link(g.tensor_tensor(sp[:, 7, :], sp[:, 6, :], num(f"atanh{ATANH_TERMS - 1}", P, W), ALU.mult))
                for t in range(ATANH_TERMS - 2, -1, -1):
                    link(g.tensor_tensor(sp[:, 7, :], sp[:, 7, :], num(f"atanh{t}", P, W), ALU.add))
                    link(g.tensor_tensor(sp[:, 7, :], sp[:, 7, :], sp[:, 6 if t else 5, :], ALU.mult))
                link(g.tensor_tensor(sp[:, 8, :], sp[:, 0, :], sp[:, 7, :], ALU.add))
                pool.wait_ge(S["cum_done"], n)
                g.tensor_tensor(a_sb[:, :].rearrange("p (j h) -> p j h", j=TJ), sp[:, 8, :].rearrange("p (j h) -> p j h", j=TJ),
                                negA[:, :].unsqueeze(1).broadcast_to([P, TJ, HEADS]), ALU.mult).then_inc(S["a_ready"], 1)
                g.tensor_tensor(dt8[:, :], sp[:, 8, :], num("1/8", P, W), ALU.mult).then_inc(S["dt8_ready"], 1)
                assert k == SP_STEPS

            def split_cum(n):
                pool.wait_ge(S["craw_ready"], 2 * n + 2)
                pool.wait_ge(S["rows_in"], 96 * n)
                g.tensor_tensor(cres[:, :], craw[:, :], parts[:, 0, :], ALU.subtract).then_inc(S["parts_step"], 1)
                pool.wait_ge(S["parts_step"], PART_STEPS * n + 1)
                g.tensor_tensor(parts[:, 1, :], cres[:, :], num("1", HEADS, T), ALU.mult).then_inc(S["parts_step"], 1)
                pool.wait_ge(S["seg_done"], 3 * n)
                pool.wait_ge(S["parts_step"], PART_STEPS * n + 2)
                g.tensor_tensor(parts[:, 2, :], cres[:, :], parts[:, 1, :], ALU.subtract).then_inc(S["parts_ready"], 1)

            def rms(b):
                pool.wait_ge(S["ss_ready"], 2 * b + 2)
                g.tensor_tensor(rt[:, :], ss[:, :], num("1/DI", P, TJ), ALU.mult).then_inc(S["rstd_step"], 1)
                pool.wait_ge(S["rstd_step"], 2 * b + 1)
                g.tensor_tensor(rt[:, :], rt[:, :], num("rms eps", P, TJ), ALU.add).then_inc(S["rstd_step"], 1)
                pool.wait_ge(S["rstd_step"], 2 * b + 2)
                pool.wait_ge(S["y_ready"], 2 * b)
                g.tensor_tensor(rstd[:, :], rt[:, :], num("-1/2", P, TJ), ALU.pow).then_inc(S["rstd_ready"], 1)

            norm(0)
            softplus(0)
            norm(1)
            split_cum(0)

            def step(b, par, half):
                pool.wait_ge(S["dt8_ready"], b + 1)
                scale_x(b)
                if has(b, -1):
                    rms(b - 1)
                if has(b, 1):
                    softplus(b + 1)
                if has(b, 2):
                    norm(b + 2)
                if has(b, 1):
                    split_cum(b + 1)

            steps(pool, step)
            rms(NB - 1)

            def base_sum(b, par, half):
                pair = bass.ds(PAIR * b, PAIR)
                pool.wait_ge(y_in[par], 16 * (half + 1))
                pool.wait_ge(S["out_ready"], b)
                flat = "p q j d -> p (q j) d"
                k = PAIR * TJ
                g.tensor_tensor(base[:, 0, :, :, :].rearrange(flat), xall[:, pair, :, :].rearrange(flat),
                                norms[:, 0, pair, :].rearrange("p q j -> p (q j)").unsqueeze(2).broadcast_to([P, k, D]), ALU.mult).then_inc(S["base_step"], 1)
                pool.wait_ge(S["base_step"], 3 * b + 1)
                g.tensor_tensor(base[:, 1, :, :, :].rearrange(flat), base[:, 0, :, :, :].rearrange(flat),
                                norms[:, 1, pair, :].rearrange("p q j -> p (q j)").unsqueeze(2).broadcast_to([P, k, D]), ALU.add).then_inc(S["base_step"], 1)
                pool.wait_ge(S["base_step"], 3 * b + 2)
                g.tensor_tensor(base[:, 2, :, :, :], base[:, 1, :, :, :], yin[:, par, :, :, :], ALU.add).then_inc(S["base_step"], 1)

            steps(pool, base_sum, NG)


_INS = ['x', 'norm_w', 'in_w', 'conv_w', 'conv_b', 'dt_bias', 'A_log', 'D_param', 'gnorm_w', 'out_w',
        'scorer_w1', 'scorer_w2', 'summ_w', 'q_w', 'k_w', 'v_w', 'gate_w']
_FFN = ['k0', 'k1', 'k2', 's0', 's1', 's2']


def kernel(**inputs):
    import numpy as _np
    import concourse.bacc as _bacc
    from concourse import mybir as _mybir
    from concourse.bass_utils import run_bass_kernel_spmd as _run

    nc = _bacc.Bacc("TRN2", target_bir_lowering=False, num_devices=1)
    arrays, args = {}, []
    for name in [f"L0_attn_{n}" for n in _INS] + [f"L0_ffn_{n}" for n in _FFN]:
        a = _np.ascontiguousarray(inputs[name])
        if a.ndim == 0:
            a = a.reshape(1)
        arrays[f"in_{name}"] = a
        args.append(nc.dram_tensor(f"in_{name}", a.shape, _mybir.dt.from_np(a.dtype), kind="ExternalInput").ap())
    args.append(nc.dram_tensor("out_0", (NB, T, D), _mybir.dt.float32, kind="ExternalOutput").ap())
    layer_kernel(nc, *args)
    r = _run(nc, [arrays], core_ids=[0])
    return r.results[0]["out_0"]
```

```python
import concourse.bass as bass
from concourse import mybir
from contextlib import ExitStack

P = 128
NB, T, D = 16, 256, 128
TJ = T // P
HEADS, HD, NSTATE = 4, 64, 128
DI = HEADS * HD
CONV = DI + 2 * NSTATE
CB = CONV // P
TAPS = 4
PAD = TAPS - 1
NIN = 2 * DI + 2 * NSTATE + HEADS
POOL, SDIM, HID = 50, 64, 32
PAIR = 2
NG = NB // PAIR
FIN = 2 * PAIR + 1
FF = 512
FB = FF // P
EPS = 1e-5
WS = 64.0
H2S = 16.0
SATURATED = 16.635532
ATANH_TERMS = 8
NEG = -1.0e30
NUMS = {"-1/2": -0.5, "1/2": 0.5, "eps": EPS, "-1": -1.0, "1": 1.0, "2": 2.0, "1/8": 0.125, "1/DI": 1.0 / DI,
        "rms eps": EPS * (2 * WS) ** 2, **{f"atanh{i}": 2.0 / (2 * i + 1) for i in range(ATANH_TERMS)}}


def layer_kernel(nc, x, norm_w, in_w, conv_w, conv_b, dt_bias, A_log, D_param, gnorm_w, out_w,
                 scorer_w1, scorer_w2, summ_w, q_w, k_w, v_w, gate_w, k0, k1, k2, s0, s1, s2, out):
    f32, f16, bf16, u8 = mybir.dt.float32, mybir.dt.float16, mybir.dt.bfloat16, mybir.dt.uint8
    ALU = mybir.AluOpType
    ACT = mybir.ActivationFunctionType
    AX = mybir.AxisListType.X

    x_v = x.rearrange("b (j p) d -> b p j d", p=P)
    out_v = out.rearrange("b (j p) d -> b p j d", p=P)

    importance = nc.dram_tensor("importance", (NB, T), f32, kind="Internal").ap()

    ctx = ExitStack()
    with ctx:
        def sb(name, shape, dt=f32):
            return ctx.enter_context(nc.sbuf_tensor(name, shape, dt))

        def sem(name):
            return ctx.enter_context(nc.semaphore(name))

        inw_ld = sb("inw_ld", [P, 6, D])
        dtw_ld = sb("dtw_ld", [HEADS, D])
        outw_ld = sb("outw_ld", [P, DI])
        sw1_ld = sb("sw1_ld", [HID, D])
        gatew_ld = sb("gatew_ld", [P, 2 * D])
        kw_ld = sb("kw_ld", [SDIM, SDIM])
        vw_ld = sb("vw_ld", [P, SDIM])
        summ_sb = sb("summ_sb", [SDIM, D])
        qw_sb = sb("qw_sb", [SDIM, D])
        sw2_ld = sb("sw2_ld", [HID, 1])
        sw2_bc = sb("sw2_bc", [HID, P])
        k0_ld = sb("k0_ld", [P, 2, FF], u8)
        k1_ld = sb("k1_ld", [P, FB, FF], u8)
        k2_ld = sb("k2_ld", [P, FB, D], u8)
        nw_col = sb("nw_col", [P, 1])
        gw_col = sb("gw_col", [P, TJ])
        cw_ld = sb("cw_ld", [P, CB, TAPS])
        cb_sb = sb("cb_sb", [P, CB])
        dtb_bc = sb("dtb_bc", [P, HEADS])
        alog_bc = sb("alog_bc", [P, HEADS])
        dpar_bc = sb("dpar_bc", [P, HEADS])
        s_bc = sb("s_bc", [P, 3])
        ident = sb("ident", [P, P])
        ident_bf = sb("ident_bf", [P, P], bf16)
        ones32 = sb("ones32", [P, P])
        ones3 = sb("ones3", [3, P], bf16)
        upto = sb("upto", [P, T])
        mask = sb("mask", [P, HEADS, P], bf16)
        minus_head = sb("minus_head", [3 * HEADS, HEADS, P], bf16)
        slots = sb("slots", [P, POOL])
        nums = sb("nums", [P, len(NUMS)])
        wt32 = sb("wt32", [P, NIN])
        wt_hi = sb("wt_hi", [P, NIN], f16)
        wt_lo = sb("wt_lo", [P, NIN], f16)
        out_wT = sb("out_wT", [P, TJ, D])
        sw1T = sb("sw1T", [P, HID])
        gate1T = sb("gate1T", [P, D])
        gate2T = sb("gate2T", [P, D])
        kwT = sb("kwT", [SDIM, SDIM])
        vwT = sb("vwT", [SDIM, D])
        kp_sb = sb("kp_sb", [SDIM, D])
        wv_sb = sb("wv_sb", [P, D])
        wmT = sb("wmT", [P, D])
        wvv = sb("wvv", [P, 2 * D])
        k0_16 = sb("k0_16", [P, FF], f16)
        k0_d = sb("k0_d", [P, FF])
        k1_16 = sb("k1_16", [P, FB, FF], f16)
        k2_16 = sb("k2_16", [P, FB, D], f16)
        cw = sb("cw", [P, CB, TAPS])
        negA = sb("negA", [P, HEADS])
        aexp = sb("aexp", [P, HEADS])
        dhalf = sb("dhalf", [P, DI])
        sgn = sb("sgn", [P, 3])
        sneg = sb("sneg", [P, 3])
        sabs = sb("sabs", [P, 3])
        sprod = sb("sprod", [P, 1])
        fhalf = sb("fhalf", [P, 2])
        c1 = sb("c1", [P, 1])
        c2 = sb("c2", [P, 1])
        xall = sb("xall", [P, NB, TJ, D])
        yall = sb("yall", [P, NB, TJ, D])
        yTall = sb("yTall", [P, NB, T])
        gall = sb("gall", [P, NB, TJ, D])
        norms = sb("norms", [P, 3, NB, TJ])
        row = sb("row", [1, T])
        st6 = sb("st6", [P, TJ, 6])
        mv = sb("mv", [P, TJ, 2])
        lt = sb("lt", [P, 8, TJ])
        lnw = sb("lnw", [P, 3, TJ])
        xn = sb("xn", [P, TJ, D])
        xT_hi = sb("xT_hi", [P, 2, T], f16)
        xT_lo = sb("xT_lo", [P, 2, T], f16)
        raw = sb("raw", [P, TJ, HEADS])
        sp = sb("sp", [P, 9, TJ * HEADS])
        dt8 = sb("dt8", [P, TJ * HEADS])
        a_sb = sb("a_sb", [P, TJ * HEADS])
        craw = sb("craw", [HEADS, T])
        cres = sb("cres", [HEADS, T])
        parts = sb("parts", [HEADS, 3, T], bf16)
        cum_t = sb("cum_t", [3, HEADS, T], bf16)
        cum_s = sb("cum_s", [3 * HEADS, T], bf16)
        pre = sb("pre", [P, CB, PAD + T])
        acc = sb("acc", [P, CB, T])
        cth = sb("cth", [P, CB, T])
        xbc = sb("xbc", [P, CB, T])
        zth = sb("zth", [P, TJ, DI])
        zg = sb("zg", [P, TJ, DI])
        xtok = sb("xtok", [P, TJ, DI])
        dtx = sb("dtx", [P, TJ, DI])
        xD = sb("xD", [P, TJ, DI])
        decay = sb("decay", [P, 3, HEADS, P])
        mix = sb("mix", [P, 3, HEADS, P])
        ysum = sb("ysum", [P, TJ, DI])
        yg = sb("yg", [P, TJ, DI])
        ysq = sb("ysq", [P, TJ, DI], bf16)
        ss = sb("ss", [P, 2])
        rt = sb("rt", [P, 2])
        rstd = sb("rstd", [P, 2])
        ygT = sb("ygT", [P, TJ, T])
        ybuf = sb("ybuf", [P, TJ, D])
        yTbuf = sb("yTbuf", [P, T])
        hsc = sb("hsc", [HID, T])
        h1_hi = sb("h1_hi", [P, FB, T], f16)
        h1_lo = sb("h1_lo", [P, FB, T], f16)
        h2_hi = sb("h2_hi", [P, FB, T], f16)
        h2_lo = sb("h2_lo", [P, FB, T], f16)
        gth = sb("gth", [P, TJ, D])
        gth1 = sb("gth1", [P, TJ, D])
        keys = sb("keys", [NB, T])
        logit = sb("logit", [NB, T])
        work = sb("work", [NB, 2, T])
        top8 = sb("top8", [NB, 7, 8])
        gt = sb("gt", [NB, T])
        eq = sb("eq", [NB, T])
        eqc = sb("eqc", [NB, T])
        ok = sb("ok", [NB, T])
        sel = sb("sel", [NB, T])
        selc = sb("selc", [NB, T])
        slot = sb("slot", [NB, T])
        zero16 = sb("zero16", [NB, T])
        th16 = sb("th16", [NB, T])
        col = sb("col", [NB, 8])
        diag2 = sb("diag2", [NB, 2, NB])
        slotT = sb("slotT", [P, TJ, NB])
        cnt_rm = sb("cnt_rm", [P, 2, NB])
        yin = decay[:, 0:2, :, :].rearrange("p s (q j) d -> p s q j d", q=PAIR)
        yTin = mix[:, 0:2, :, :].rearrange("p s (q j) d -> p s q (j d)", q=PAIR)
        onehot = sb("onehot", [P, TJ, PAIR, POOL])
        pover = sb("pover", [P, PAIR, POOL])
        sT = sb("sT", [P, PAIR, POOL])
        m_sb = sb("m_sb", [P, PAIR, POOL])
        vv = zth[0:POOL, :, :]
        lm = sb("lm", [P, PAIR * TJ, POOL])
        ls = sb("ls", [P, PAIR * TJ, POOL])
        ex = sb("ex", [P, PAIR * TJ, POOL])
        at = sb("at", [P, PAIR * TJ, POOL])
        mx = sb("mx", [P, PAIR * TJ])
        sm = sb("sm", [P, PAIR * TJ])
        rec = sb("rec", [P, PAIR * TJ])
        atT = zg[0:POOL, :, :].rearrange("p j c -> p (j c)")
        gate = ysum[:, :, :].rearrange("p q (j d) -> p q j d", j=TJ)
        base = sb("base", [P, 2, PAIR, TJ, D])
        fin = sb("fin", [P, 3, PAIR, TJ, D])
        obuf = xbc[:, :, :].rearrange("p (s q) (j d) -> p s q j d", s=2, j=TJ)

        bank = [ctx.enter_context(nc.psum_tensor(f"bank{i}", [P, 512], f32)) for i in range(8)]
        F = [bank[0], bank[1]]
        pA = bank[2]
        pB = bank[3]
        pG = bank[4]
        pDT = pA[:, 0:TJ * HEADS]
        pY = bank[6]
        pS = [bank[5], pY, bank[5]]
        pC = bank[7][0:HEADS, 0:T]
        pO, pYT = bank[7][:, 0:256], bank[7][:, 256:512]

        S = {n: sem(n) for n in (
            "in_w_in", "weights_in", "small_in", "mlp_in", "w_factor", "setup_step", "consts", "w_T", "w_ev", "w_split", "w_mlp", "w_small", "w_dve",
            "w_exp", "pads",
            "stats", "mv_ready", "ln_step", "norm_ready", "norm_kept", "dt8_ready", "xn_ready", "xT_done", "xT_hi_ready",
            "xT_lo_ready", "dt_done", "raw_ready", "sp_step", "abs_ready", "u_ready", "den_ready",
            "rden_ready", "a_ready", "cum_done", "craw_ready", "parts_step", "parts_ready",
            "rows_in", "proj_done", "pre_ready", "conv_step", "cth_ready", "xbc_ready", "z_done",
            "zth_ready", "zg_ready", "xtok_done", "xtok_ready", "x_scaled", "g_done", "seg_done",
            "decay_ready", "mix_ready", "y_done", "ysum_ready", "yg_ready", "ss_ready",
            "rstd_step", "rstd_ready", "ygT_done", "ygT_ready", "yo_done", "y_ready", "yT_done",
            "yT_ready", "h_done", "h_ready", "row_done", "row_ready", "y_saved", "yT_saved",
            "l1_done", "h1_hi_ready", "h1_lo_ready", "l2_done", "h2_hi_ready", "h2_lo_ready",
            "l3_done", "gth_ready", "gth1_ready", "g_ready",
            "keys_in", "row_saved", "sel_step", "slots_done", "th16_ready", "slotT_done", "slotT_ready",
            "onehot_ready", "choose_step", "lm_step", "bias_ready", "s_done", "sT_ready", "m_done", "m_ready", "vv_done",
            "vv_ready", "lg_done", "lm_ready", "max_ready", "ls_ready", "ex_ready", "sum_ready",
            "rec_ready", "at_ready", "atT_done", "atT_ready", "rg_done", "gate_ready",
            "base_step", "fin_step", "out_ready")}
        x_in = [sem("x_in0"), sem("x_in1")]
        y_in = [sem("y_in0"), sem("y_in1")]
        yT_in = [sem("yT_in0"), sem("yT_in1")]
        out_done = [sem("out_done0"), sem("out_done1")]

        ctx.enter_context(nc.allow_non_contiguous_dma(reason="columns of small weights"))
        block = ctx.enter_context(nc.Block())

        def num(name, p, *free):
            c = list(NUMS).index(name)
            a = nums[0:p, c:c + 1]
            for _ in free[1:]:
                a = a.unsqueeze(2)
            return a.broadcast_to([p, *free])

        def steps(eng, step, count=NB, last=None):
            step(0, 0, 0)
            step(1, 1, 0)
            with eng.Fori(1, count // 2 - 1) as i:
                step(2 * i, 0, i)
                step(2 * i + 1, 1, i)
            step(count - 2, 0, count // 2 - 1)
            (last or step)(count - 1, 1, count // 2 - 1)

        def has(b, ahead, count=NB):
            return not isinstance(b, int) or 0 <= b + ahead < count

        N_IN, N_W, N_SMALL, N_MLP = 3, 9, 8, 3
        N_JOBS = 14

        def w_bank(t):
            return bank[t if t < 7 else (7, 0, 1, 4, 5, 6)[(t - 7) % 6]]
        LN_STEPS, SP_STEPS, PART_STEPS = 10, 2 + 1 + 2 * (ATANH_TERMS - 1) + 1, 2

        @block.sync
        def _(sp_eng):
            def w(dst, src, name="weights_in"):
                sp_eng.dma_start(dst, src).then_inc(S[name], 16)

            def load_x(n, par):
                sp_eng.dma_start(xall[:, bass.ds(n, 1), :, :], x_v[bass.ds(n, 1)].rearrange("b p j d -> p b j d")).then_inc(x_in[par], 16)

            sp_eng.dma_start(xall[:, 0:1, :, :], x_v[0:1].rearrange("b p j d -> p b j d")).then_inc(x_in[0], 16)
            w(inw_ld[:, :, :], in_w[0:6 * P, :].rearrange("(c p) d -> p c d", p=P), "in_w_in")
            w(dtw_ld[:, :], in_w[6 * P:NIN, :], "in_w_in")
            w(nw_col[:, :], norm_w.rearrange("(p a) -> p a", a=1), "in_w_in")
            sp_eng.dma_start(xall[:, 1:2, :, :], x_v[1:2].rearrange("b p j d -> p b j d")).then_inc(x_in[1], 16)
            w(outw_ld[:, :], out_w[:, :])
            w(gw_col[:, :], gnorm_w.rearrange("(a p) -> p a", p=P))
            w(sw1_ld[:, :], scorer_w1[:, :])
            w(sw2_ld[:, :], scorer_w2.rearrange("a h -> h a"))
            w(gatew_ld[:, :], gate_w[:, :])
            w(kw_ld[:, :], k_w[:, :])
            w(vw_ld[:, :], v_w[:, :])
            w(summ_sb[:, :], summ_w[:, :])
            w(qw_sb[:, :], q_w[:, :])
            w(k0_ld[:, :, :], k0.rearrange("(a p) n -> p a n", p=P), "mlp_in")
            w(k1_ld[:, :, :], k1.rearrange("(a p) n -> p a n", p=P), "mlp_in")
            w(k2_ld[:, :, :], k2.rearrange("(a p) n -> p a n", p=P), "mlp_in")

            def relayout(n):
                sp_eng.wait_ge(S["parts_ready"], n + 1)
                for q in range(3):
                    sp_eng.dma_start(cum_t[q:q + 1, :, :], parts[:, q, :]).then_inc(S["rows_in"], 16)
                sp_eng.dma_start(cum_s[:, :], parts[:, :, :]).then_inc(S["rows_in"], 16)

            def save_y(b):
                sp_eng.wait_ge(S["y_ready"], 2 * b + 2)
                sp_eng.dma_start(yall[:, bass.ds(b, 1), :, :], ybuf[:, :, :].unsqueeze(1)).then_inc(S["y_saved"], 16)

            def save_row(b):
                sp_eng.wait_ge(S["row_ready"], b + 1)
                sp_eng.dma_start(importance[bass.ds(b, 1), :], row[:, :]).then_inc(S["row_saved"], 16)
                sp_eng.dma_start(yTall[:, bass.ds(b, 1), :], yTbuf[:, :].unsqueeze(1)).then_inc(S["yT_saved"], 16)

            for n in range(2, 4):
                sp_eng.wait_ge(x_in[n % 2], 16)
                load_x(n, n % 2)
            relayout(0)

            def step(b, par, half):
                if has(b, 4):
                    sp_eng.wait_ge(x_in[par], 16 * (half + 2))
                    load_x(b + 4, par)
                if has(b, -1):
                    save_y(b - 1)
                if has(b, 1):
                    relayout(b + 1)
                if has(b, -1):
                    save_row(b - 1)

            step(0, 0, 0)
            step(1, 1, 0)
            with sp_eng.Fori(1, NB // 2 - 2) as i:
                step(2 * i, 0, i)
                step(2 * i + 1, 1, i)
            for b in range(NB - 4, NB):
                step(b, b % 2, b // 2)
            save_y(NB - 1)
            save_row(NB - 1)

            sp_eng.wait_ge(S["row_saved"], 16 * NB)
            sp_eng.dma_start(logit[:, :], importance[:, :]).then_inc(S["keys_in"], 16)

            def load_y(n, par):
                sp_eng.dma_start(yin[:, par, :, :, :], yall[:, bass.ds(PAIR * n, PAIR), :, :]).then_inc(y_in[par], 16)

            sp_eng.wait_ge(S["y_saved"], 16 * NB)
            sp_eng.wait_ge(S["yT_saved"], 16 * NB)
            for n in range(2):
                load_y(n, n)
                sp_eng.dma_start(yTin[:, n, :, :], yTall[:, PAIR * n:PAIR * (n + 1), :]).then_inc(yT_in[n], 16)

            def step2(b, par, half):
                if has(b, 2, NG):
                    sp_eng.wait_ge(S["base_step"], 3 * b + 3)
                    load_y(b + 2, par)
                sp_eng.wait_ge(S["out_ready"], b + 1)
                sp_eng.dma_start(out_v[bass.ds(PAIR * b, PAIR)].rearrange("b p j d -> p b j d"), obuf[:, par, :, :, :]).then_inc(out_done[par], 16)

            steps(sp_eng, step2, NG)
            for par in range(2):
                sp_eng.wait_ge(out_done[par], 16 * NG // 2)

        @block.tensor
        def _(pe):
            mm = nc.tensor.matmul

            jobs = [(inw_ld[:, c, :], P) for c in range(6)] + [(dtw_ld[:, :], HEADS)] \
                + [(outw_ld[:, k * P:(k + 1) * P], P) for k in range(2)] + [(sw1_ld[:, :], HID)] \
                + [(gatew_ld[:, k * D:(k + 1) * D], P) for k in range(2)] + [(kw_ld[:, :], SDIM), (vw_ld[:, :], P)]
            pe.wait_ge(S["consts"], 1)
            pe.wait_ge(S["in_w_in"], 16 * N_IN)

            def transpose_weights(first, count):
                for t in range(first, first + count):
                    if t > 7:
                        pe.wait_ge(S["w_ev"], t - 5)
                    src, rows = jobs[t]
                    nc.tensor.transpose(w_bank(t)[0:src.shape[1], 0:rows], src, ident[0:rows, 0:rows]).then_inc(S["w_T"], 1)

            transpose_weights(0, 7)

            def weight_products():
                pe.wait_ge(S["w_ev"], N_JOBS)
                mm(w_bank(14)[0:SDIM, 0:D], kwT[:, :], summ_sb[:, :], start=True, stop=True).then_inc(S["w_T"], 1)
                mm(w_bank(15)[:, 0:D], summ_sb[:, :], vwT[:, :], start=True, stop=True).then_inc(S["w_T"], 1)
                mm(w_bank(16)[:, 0:D], vwT[:, :], summ_sb[:, :], start=True, stop=True).then_inc(S["w_T"], 1)
                pe.wait_ge(S["w_ev"], N_JOBS + 3)
                mm(w_bank(17)[:, 0:D], kp_sb[:, :], qw_sb[:, :], start=True, stop=True).then_inc(S["w_T"], 1)
                mm(w_bank(18)[:, 0:D], wv_sb[:, :], gate2T[:, :], start=True, stop=True).then_inc(S["w_T"], 1)

            def norm_T(n):
                pe.wait_ge(S["xn_ready"], TJ * (n + 1))
                pe.wait_ge(S["zg_ready"], n)
                for j in range(TJ):
                    nc.tensor.transpose(pA[:, j * P:(j + 1) * P], xn[:, j, :], ident[:, :]).then_inc(S["xT_done"], 1)

            def dt_proj(n, par):
                pe.wait_ge(S["xT_hi_ready"], n + 1)
                pe.wait_ge(S["xT_lo_ready"], n + 1)
                for j in range(TJ):
                    o = pDT[:, j * HEADS:(j + 1) * HEADS]
                    t = slice(j * P, (j + 1) * P)
                    mm(o, xT_hi[:, par, t], wt_hi[:, 6 * P:NIN], start=True, stop=False)
                    mm(o, xT_hi[:, par, t], wt_lo[:, 6 * P:NIN], start=False, stop=False)
                    mm(o, xT_lo[:, par, t], wt_hi[:, 6 * P:NIN], start=False, stop=True).then_inc(S["dt_done"], 1)

            def conv_proj(n, par, half):
                dst = pB if half else pA
                if half == 0:
                    pe.wait_ge(S["raw_ready"], n + 1)
                elif has(n, -1):
                    pe.wait_ge(S["xtok_ready"], n)
                    if has(n, -2):
                        pe.wait_ge(S["ygT_ready"], n - 1)
                for i in range(2):
                    c = DI + (2 * half + i) * P
                    o = dst[:, i * T:(i + 1) * T]
                    mm(o, wt_hi[:, c:c + P], xT_hi[:, par, :], start=True, stop=False)
                    mm(o, wt_hi[:, c:c + P], xT_lo[:, par, :], start=False, stop=False)
                    mm(o, wt_lo[:, c:c + P], xT_hi[:, par, :], start=False, stop=True).then_inc(S["proj_done"], 1)

            def z_proj(n, par):
                pe.wait_ge(S["pre_ready"], 6 * n + 3)
                for j in range(TJ):
                    o = pA[:, j * DI:(j + 1) * DI]
                    t = slice(j * P, (j + 1) * P)
                    mm(o, xT_hi[:, par, t], wt_hi[:, 0:DI], start=True, stop=False)
                    mm(o, xT_hi[:, par, t], wt_lo[:, 0:DI], start=False, stop=False)
                    mm(o, xT_lo[:, par, t], wt_hi[:, 0:DI], start=False, stop=True).then_inc(S["z_done"], 1)

            def cum(n):
                pe.wait_ge(S["a_ready"], n + 1)
                if has(n, -2):
                    pe.wait_ge(S["yT_ready"], n - 1)
                mm(pC[:, :], a_sb[:, 0:HEADS], upto[:, :], start=True, stop=False)
                mm(pC[:, P:T], a_sb[:, HEADS:2 * HEADS], upto[:, 0:P], start=False, stop=True).then_inc(S["cum_done"], 1)

            def x_by_token(b):
                pe.wait_ge(S["xbc_ready"], 2 * b + 1)
                pe.wait_ge(S["pre_ready"], 6 * b + 6)
                for j in range(TJ):
                    for k in range(2):
                        nc.tensor.transpose(pB[:, j * DI + k * P:j * DI + (k + 1) * P], xbc[:, k, j * P:(j + 1) * P],
                                            ident[:, :]).then_inc(S["xtok_done"], 1)

            def scores(b):
                pe.wait_ge(S["xbc_ready"], 2 * b + 2)
                if has(b, -2):
                    pe.wait_ge(S["row_ready"], b - 1)
                elif has(b, -1):
                    pe.wait_ge(S["mix_ready"], 3 * b)
                mm(pG[:, 0:T], xbc[:, 2, 0:P], xbc[:, 3, :], start=True, stop=True).then_inc(S["g_done"], 1)
                mm(pG[:, T:T + P], xbc[:, 2, P:T], xbc[:, 3, P:T], start=True, stop=True).then_inc(S["g_done"], 1)

            def segment(b, k):
                s, t = ((0, 0), (0, 1), (1, 1))[k]
                if k == 0:
                    pe.wait_ge(S["rows_in"], 64 * (b + 1))
                if k == 1:
                    pe.wait_ge(S["ysum_ready"], b)
                elif k == 2 or has(b, -1):
                    pe.wait_ge(S["decay_ready"], 3 * b + (1 if k else 0))
                o = pS[k][:, :].rearrange("p (h t) -> p h t", h=HEADS)
                mm(o, ones3[:, :], cum_t[:, :, t * P:(t + 1) * P], start=True, stop=False)
                last = mm(o, cum_s[:, s * P:(s + 1) * P], minus_head[:, :, :], start=False, stop=s != t)
                if s == t:
                    last = mm(o, ident_bf[:, :], mask[:, :, :], start=False, stop=True)
                last.then_inc(S["seg_done"], 1)

            def recur(b):
                pe.wait_ge(S["mix_ready"], 3 * b + 3)
                pe.wait_ge(S["x_scaled"], 2 * b + 1)
                for h in range(HEADS):
                    c = slice(h * HD, (h + 1) * HD)
                    mm(pY[:, c], mix[:, 0, h, :], dtx[:, 0, c], start=True, stop=True)
                for h in range(HEADS):
                    c = slice(h * HD, (h + 1) * HD)
                    o = pY[:, DI + h * HD:DI + (h + 1) * HD]
                    mm(o, mix[:, 1, h, :], dtx[:, 0, c], start=True, stop=False)
                    last = mm(o, mix[:, 2, h, :], dtx[:, 1, c], start=False, stop=True)
                last.then_inc(S["y_done"], 1)

            def gated_T(b):
                pe.wait_ge(S["yg_ready"], b + 1)
                if has(b, 1):
                    pe.wait_ge(S["xtok_ready"], b + 2)
                for k in range(2):
                    for j in range(TJ):
                        nc.tensor.transpose(pB[:, k * T + j * P:k * T + (j + 1) * P], yg[:, j, k * P:(k + 1) * P],
                                            ident[:, :]).then_inc(S["ygT_done"], 1)

            def out_proj(b):
                pe.wait_ge(S["ygT_ready"], b + 1)
                if has(b, 1):
                    pe.wait_ge(S["craw_ready"], 2 * b + 4)
                else:
                    pe.wait_ge(S["yT_ready"], b)
                for j in range(TJ):
                    o = pO[:, j * D:(j + 1) * D]
                    mm(o, ygT[:, 0, j * P:(j + 1) * P], out_wT[:, 0, :], start=True, stop=False)
                    mm(o, ygT[:, 1, j * P:(j + 1) * P], out_wT[:, 1, :], start=False, stop=True).then_inc(S["yo_done"], 1)

            def y_T(b):
                pe.wait_ge(S["y_ready"], 2 * b + 2)
                for j in range(TJ):
                    nc.tensor.transpose(pYT[:, j * P:(j + 1) * P], ybuf[:, j, :], ident[:, :]).then_inc(S["yT_done"], 1)

            def scorer(b):
                pe.wait_ge(S["yT_ready"], b + 1)
                pe.wait_ge(S["mix_ready"], 3 * b + (6 if has(b, 1) else 3))
                mm(pG[0:HID, 0:T], sw1T[:, :], yTbuf[:, :], start=True, stop=True).then_inc(S["h_done"], 1)

            def scorer_row(b):
                pe.wait_ge(S["h_ready"], b + 1)
                mm(pG[:, T:2 * T], sw2_bc[:, :], hsc[:, :], start=True, stop=True).then_inc(S["row_done"], 1)

            def layer1(b, par, half):
                if half == 0:
                    pe.wait_ge(S["xT_hi_ready"], b + 1)
                    pe.wait_ge(S["xT_lo_ready"], b + 1)
                    pe.wait_ge(S["g_ready"], 2 * b)
                else:
                    pe.wait_ge(S["h2_hi_ready"], 2 * b)
                    pe.wait_ge(S["h2_lo_ready"], 2 * b)
                for i in range(2):
                    m = 2 * half + i
                    o = F[half][:, i * T:(i + 1) * T]
                    mm(o, k0_16[:, m * P:(m + 1) * P], xT_hi[:, par, :], start=True, stop=False)
                    last = mm(o, k0_16[:, m * P:(m + 1) * P], xT_lo[:, par, :], start=False, stop=True)
                last.then_inc(S["l1_done"], 1)

            def layer2(b, half, quarters=(0, 1)):
                if half == 0 and 0 in quarters:
                    pe.wait_ge(S["h1_hi_ready"], 2 * b + 2)
                    pe.wait_ge(S["h1_lo_ready"], 2 * b + 2)
                for i in quarters:
                    m = 2 * half + i
                    o = F[half][:, i * T:(i + 1) * T]
                    for k in range(FB):
                        mm(o, k1_16[:, k, m * P:(m + 1) * P], h1_hi[:, k, :], start=k == 0, stop=False)
                        last = mm(o, k1_16[:, k, m * P:(m + 1) * P], h1_lo[:, k, :], start=False, stop=k == FB - 1)
                if 1 in quarters:
                    last.then_inc(S["l2_done"], 1)

            def layer3(b):
                pe.wait_ge(S["h2_hi_ready"], 2 * b + 2)
                pe.wait_ge(S["h2_lo_ready"], 2 * b + 2)
                for j in range(TJ):
                    o = F[0][:, j * D:(j + 1) * D]
                    t = slice(j * P, (j + 1) * P)
                    for k in range(FB):
                        mm(o, h2_hi[:, k, t], k2_16[:, k, :], start=k == 0, stop=False)
                        last = mm(o, h2_lo[:, k, t], k2_16[:, k, :], start=False, stop=k == FB - 1)
                last.then_inc(S["l3_done"], 1)

            pe.wait_ge(S["w_ev"], 7)
            norm_T(0)
            pe.wait_ge(S["w_split"], 2)
            dt_proj(0, 0)
            conv_proj(0, 0, 0)
            conv_proj(0, 0, 1)
            z_proj(0, 0)
            pe.wait_ge(S["weights_in"], 16 * N_W)
            transpose_weights(7, N_JOBS - 7)
            pe.wait_ge(S["w_ev"], N_JOBS)
            pe.wait_ge(S["consts"], 7)
            cum(0)
            weight_products()
            pe.wait_ge(S["w_ev"], N_JOBS + 5)
            pe.wait_ge(S["w_mlp"], 4)

            def step(b, par, half):
                x_by_token(b)
                layer1(b, par, 0)
                layer1(b, par, 1)
                if has(b, -1):
                    gated_T(b - 1)
                if has(b, 1):
                    norm_T(b + 1)
                if has(b, -1):
                    out_proj(b - 1)
                scores(b)
                if has(b, 1):
                    dt_proj(b + 1, 1 - par)
                segment(b, 0)
                if has(b, -1):
                    y_T(b - 1)
                if has(b, 1):
                    conv_proj(b + 1, 1 - par, 0)
                    conv_proj(b + 1, 1 - par, 1)
                segment(b, 1)
                segment(b, 2)
                layer2(b, 0, (0,))
                layer2(b, 0, (1,))
                layer2(b, 1, (0,))
                layer2(b, 1, (1,))
                if has(b, 1):
                    z_proj(b + 1, 1 - par)
                    cum(b + 1)
                if has(b, -1):
                    scorer(b - 1)
                layer3(b)
                recur(b)
                if has(b, -1):
                    scorer_row(b - 1)

            def last_step(b, par, half):
                x_by_token(b)
                gated_T(b - 1)
                scores(b)
                segment(b, 0)
                out_proj(b - 1)
                layer1(b, par, 0)
                segment(b, 1)
                layer1(b, par, 1)
                segment(b, 2)
                y_T(b - 1)
                layer2(b, 0, (0,))
                recur(b)
                scorer(b - 1)
                layer2(b, 0, (1,))
                gated_T(b)
                scorer_row(b - 1)
                layer2(b, 1, (0,))
                out_proj(b)
                layer2(b, 1, (1,))
                y_T(b)
                scorer(b)
                scorer_row(b)
                layer3(b)

            steps(pe, step, last=last_step)

            def gather(n, par, half):
                pe.wait_ge(S["onehot_ready"], n + 1)
                pe.wait_ge(y_in[par], 16 * (half + 1))
                pe.wait_ge(S["m_ready"], n)
                for q in range(PAIR):
                    for j in range(TJ):
                        last = mm(bank[0][:, q * POOL:(q + 1) * POOL], yin[:, par, q, j, :], onehot[:, j, q, :],
                                  start=j == 0, stop=j == TJ - 1)
                last.then_inc(S["s_done"], 1)

            def pool_vectors(n):
                pe.wait_ge(S["sT_ready"], n + 1)
                mm(bank[0][:, 256:256 + PAIR * POOL], wmT[:, :], sT[:, :, :], start=True, stop=True).then_inc(S["m_done"], 1)

            def value_vectors(n):
                pe.wait_ge(S["vv_ready"], n)
                for q in range(PAIR):
                    last = mm(bank[1][0:POOL, q * 2 * D:(q + 1) * 2 * D], sT[:, q, :], wvv[:, :], start=True, stop=True)
                last.then_inc(S["vv_done"], 1)

            def logits(n, par, half):
                pe.wait_ge(S["m_ready"], n + 1)
                pe.wait_ge(yT_in[par], 16 * (half + 1))
                pe.wait_ge(S["lm_ready"], n)
                for q in range(PAIR):
                    for j in range(TJ):
                        c = (q * TJ + j) * POOL
                        last = mm(bank[2][:, c:c + POOL], yTin[:, par, q, j * P:(j + 1) * P], m_sb[:, q, :], start=True, stop=True)
                last.then_inc(S["lg_done"], 1)

            def attention_T(b):
                pe.wait_ge(S["at_ready"], b + 1)
                pe.wait_ge(S["atT_ready"], b)
                for q in range(PAIR):
                    for j in range(TJ):
                        c = (q * TJ + j) * P
                        last = mm(bank[3][0:POOL, c:c + P], at[:, q * TJ + j, :], ident[:, :], start=True, stop=True)
                last.then_inc(S["atT_done"], 1)

            def gate_y(n, par, half):
                pe.wait_ge(yT_in[par], 16 * (half + 1))
                if has(n, -2, NG):
                    pe.wait_ge(S["fin_step"], FIN * (n - 1))
                for q in range(PAIR):
                    for j in range(TJ):
                        mm(bank[4 + 2 * par + q][:, (2 * j + 1) * D:(2 * j + 2) * D], yTin[:, par, q, j * P:(j + 1) * P], gate1T[:, :],
                           start=j == 0, stop=False)

            def retrieve(b, par):
                pe.wait_ge(S["atT_ready"], b + 1)
                pe.wait_ge(S["vv_ready"], b + 1)
                for q in range(PAIR):
                    for j in range(TJ):
                        o = bank[4 + 2 * par + q][:, j * 2 * D:(j + 1) * 2 * D]
                        a = atT[:, (q * TJ + j) * P:(q * TJ + j + 1) * P]
                        mm(o[:, 0:D], a, vv[:, q, 0:D], start=False, stop=False)
                        last = mm(o[:, D:2 * D], a, vv[:, q, D:2 * D], start=False, stop=j == TJ - 1)
                    last.then_inc(S["rg_done"], 1)

            pe.wait_ge(S["slots_done"], 1)
            for j in range(TJ):
                nc.tensor.transpose(bank[0][:, j * NB:(j + 1) * NB], slot[:, j * P:(j + 1) * P], ident[0:NB, 0:NB]).then_inc(S["slotT_done"], 1)
            mm(bank[1][:, 0:2 * NB], ones32[0:NB, :], diag2[:, :, :], start=True, stop=True).then_inc(S["slotT_done"], 1)
            gate_y(0, 0, 0)
            pe.wait_ge(S["slotT_ready"], 2)

            gather(0, 0, 0)
            pool_vectors(0)
            logits(0, 0, 0)
            gate_y(1, 1, 0)
            value_vectors(0)

            def step2(b, par, half):
                if has(b, 1, NG):
                    gather(b + 1, 1 - par, half + par)
                    pool_vectors(b + 1)
                attention_T(b)
                if has(b, 1, NG):
                    logits(b + 1, 1 - par, half + par)
                    if has(b, -1, NG):
                        gate_y(b + 1, 1 - par, half + par)
                retrieve(b, par)
                if has(b, 1, NG):
                    value_vectors(b + 1)

            steps(pe, step2, NG)

        @block.scalar
        def _(act):
            go = nc.scalar.activation

            def w(dst, src):
                act.dma_start(dst, src).then_inc(S["small_in"], 16)

            w(dtb_bc[:, :], dt_bias.partition_broadcast(P))
            w(alog_bc[:, :], A_log.partition_broadcast(P))
            w(s_bc[:, 0:1], s0.partition_broadcast(P))
            w(s_bc[:, 1:2], s1.partition_broadcast(P))
            w(s_bc[:, 2:3], s2.partition_broadcast(P))
            w(cw_ld[:, :, :], conv_w.rearrange("(a p) k -> p a k", p=P))
            w(cb_sb[:, :], conv_b.rearrange("(a p) -> p a", p=P))
            w(dpar_bc[:, :], D_param.partition_broadcast(P))
            act.wait_ge(S["w_ev"], 7)
            go(wt_hi[:, :], wt32[:, :], ACT.Copy).then_inc(S["w_split"], 1)

            def xT_high(n, par):
                act.wait_ge(S["xT_done"], TJ * (n + 1))
                if has(n, -2):
                    act.wait_ge(S["l1_done"], 2 * (n - 1))
                go(xT_hi[:, par, :], pA[:, 0:T], ACT.Copy).then_inc(S["xT_hi_ready"], 1)

            def exp_dt(n):
                act.wait_ge(S["abs_ready"], 2 * n + 2)
                go(sp[:, 2, :], sp[:, 1, :], ACT.Exp).then_inc(S["u_ready"], 1)

            def conv_start(n, half):
                src = pB if half else pA
                act.wait_ge(S["proj_done"], 4 * n + 2 * half + 2)
                act.wait_ge(S["xbc_ready"], 2 * n)
                go(pre[:, 2 * half:2 * half + 2, PAD:], src[:, :].rearrange("p (c t) -> p c t", c=2), ACT.Copy).then_inc(S["pre_ready"], 1)
                for i in range(2):
                    c = 2 * half + i
                    go(acc[:, c, :], src[:, i * T:(i + 1) * T], ACT.Identity, bias=cb_sb[:, c:c + 1],
                       scale=cw[:, c, TAPS - 1:TAPS]).then_inc(S["pre_ready"], 1)

            def conv_tanh(n, half):
                act.wait_ge(S["conv_step"], 12 * n + 6 * half + 6)
                act.wait_ge(S["xbc_ready"], 2 * n)
                go(cth[:, 2 * half:2 * half + 2, :], acc[:, 2 * half:2 * half + 2, :], ACT.Tanh, scale=0.5).then_inc(S["cth_ready"], 1)

            def z_tanh(n):
                act.wait_ge(S["z_done"], TJ * (n + 1))
                act.wait_ge(S["zg_ready"], n)
                go(zth[:, :, :], pA[:, :].rearrange("p (j c) -> p j c", j=TJ), ACT.Tanh, scale=0.5 / WS).then_inc(S["zth_ready"], 1)

            def cum_out(n):
                act.wait_ge(S["cum_done"], n + 1)
                act.wait_ge(S["rows_in"], 64 * n)
                act.wait_ge(S["parts_ready"], n)
                go(parts[:, 0, :], pC, ACT.Copy).then_inc(S["craw_ready"], 1)
                go(craw[:, :], pC, ACT.Copy).then_inc(S["craw_ready"], 1)

            def hidden_high(b, layer, half):
                done, ready = (("l1_done", "h1_hi_ready"), ("l2_done", "h2_hi_ready"))[layer]
                act.wait_ge(S[done], 2 * b + half + 1)
                if half == 0:
                    if layer == 0:
                        act.wait_ge(S["l2_done"], 2 * b)
                    else:
                        act.wait_ge(S["l3_done"], b)
                dst = (h1_hi, h2_hi)[layer]
                go(dst[:, 2 * half:2 * half + 2, :], F[half][:, :].rearrange("p (c t) -> p c t", c=2), ACT.Relu).then_inc(S[ready], 1)

            def decay_exp(b, k):
                act.wait_ge(S["seg_done"], 3 * b + k + 1)
                if k == 0:
                    act.wait_ge(S["mix_ready"], 3 * b)
                go(decay[:, k, :, :], pS[k][:, :].rearrange("p (h t) -> p h t", h=HEADS), ACT.Exp).then_inc(S["decay_ready"], 1)

            def x_out(b):
                act.wait_ge(S["xtok_done"], 4 * b + 4)
                act.wait_ge(S["x_scaled"], 2 * b)
                go(xtok[:, :, :], pB[:, :].rearrange("p (j c) -> p j c", j=TJ), ACT.Copy).then_inc(S["xtok_ready"], 1)

            def mlp_tanh(b):
                act.wait_ge(S["l3_done"], b + 1)
                act.wait_ge(S["gth1_ready"], b)
                for j in range(TJ):
                    go(gth[:, j, :], F[0][:, j * D:(j + 1) * D], ACT.Tanh,
                       scale=norms[:, 2, bass.ds(b, 1), j:j + 1].squeeze(1)).then_inc(S["gth_ready"], 1)

            def squares(b):
                act.wait_ge(S["yg_ready"], b + 1)
                act.wait_ge(S["rstd_step"], 2 * b)
                for j in range(TJ):
                    go(ysq[:, j, :], yg[:, j, :], ACT.Square, accum_out=ss[:, j:j + 1]).then_inc(S["ss_ready"], 1)

            def gated_T_out(b):
                act.wait_ge(S["ygT_done"], 4 * b + 4)
                act.wait_ge(S["yo_done"], 2 * b)
                go(ygT[:, :, :], pB[:, :].rearrange("p (k t) -> p k t", k=2), ACT.Copy).then_inc(S["ygT_ready"], 1)

            def y_out(b):
                act.wait_ge(S["yo_done"], 2 * b + 2)
                act.wait_ge(S["rstd_ready"], b + 1)
                act.wait_ge(S["y_saved"], 16 * b)
                act.wait_ge(S["yT_done"], 2 * b)
                for j in range(TJ):
                    go(ybuf[:, j, :], pO[:, j * D:(j + 1) * D], ACT.Copy, scale=rstd[:, j:j + 1]).then_inc(S["y_ready"], 1)

            def y_T_out(b):
                act.wait_ge(S["yT_done"], 2 * b + 2)
                act.wait_ge(S["yT_saved"], 16 * b)
                act.wait_ge(S["h_done"], b)
                go(yTbuf[:, :], pYT, ACT.Copy).then_inc(S["yT_ready"], 1)

            def scorer_out(b):
                act.wait_ge(S["h_done"], b + 1)
                act.wait_ge(S["row_done"], b)
                go(hsc[:, :], pG[0:HID, 0:T], ACT.Relu).then_inc(S["h_ready"], 1)

            def row_out(b):
                act.wait_ge(S["row_done"], b + 1)
                act.wait_ge(S["row_saved"], 16 * b)
                go(row[:, :], pG[0:1, T:2 * T], ACT.Copy).then_inc(S["row_ready"], 1)

            xT_high(0, 0)
            act.wait_ge(S["small_in"], 16 * N_SMALL)
            go(aexp[:, :], alog_bc[:, :], ACT.Exp).then_inc(S["w_exp"], 1)
            act.wait_ge(S["pads"], 1)
            act.wait_ge(S["w_dve"], 1)
            exp_dt(0)
            conv_start(0, 0)
            conv_start(0, 1)
            conv_tanh(0, 0)
            z_tanh(0)
            cum_out(0)
            conv_tanh(0, 1)

            def step(b, par, half):
                x_out(b)
                if has(b, -1):
                    squares(b - 1)
                    gated_T_out(b - 1)
                hidden_high(b, 0, 0)
                if has(b, 1):
                    xT_high(b + 1, 1 - par)
                if has(b, -1):
                    y_out(b - 1)
                hidden_high(b, 0, 1)
                if has(b, 1):
                    exp_dt(b + 1)
                decay_exp(b, 0)
                if has(b, 1):
                    conv_start(b + 1, 0)
                    conv_start(b + 1, 1)
                decay_exp(b, 1)
                hidden_high(b, 1, 0)
                decay_exp(b, 2)
                if has(b, -1):
                    y_T_out(b - 1)
                hidden_high(b, 1, 1)
                if has(b, 1):
                    conv_tanh(b + 1, 0)
                    cum_out(b + 1)
                mlp_tanh(b)
                if has(b, 1):
                    z_tanh(b + 1)
                if has(b, -1):
                    scorer_out(b - 1)
                if has(b, 1):
                    conv_tanh(b + 1, 1)
                if has(b, -1):
                    row_out(b - 1)

            def last_step(b, par, half):
                x_out(b)
                squares(b - 1)
                gated_T_out(b - 1)
                decay_exp(b, 0)
                y_out(b - 1)
                hidden_high(b, 0, 0)
                decay_exp(b, 1)
                hidden_high(b, 0, 1)
                decay_exp(b, 2)
                y_T_out(b - 1)
                scorer_out(b - 1)
                squares(b)
                gated_T_out(b)
                row_out(b - 1)
                hidden_high(b, 1, 0)
                y_out(b)
                hidden_high(b, 1, 1)
                y_T_out(b)
                scorer_out(b)
                row_out(b)
                mlp_tanh(b)

            steps(act, step, last=last_step)

            act.wait_ge(S["keys_in"], 16)
            go(th16[:, :], logit[:, :], ACT.Tanh, scale=0.5, accum_out=col[:, 4:5]).then_inc(S["th16_ready"], 1)

            def chosen_out(n):
                act.wait_ge(S["s_done"], n + 1)
                act.wait_ge(S["vv_done"], n)
                go(sT[:, :, :], bank[0][:, 0:PAIR * POOL].rearrange("p (q c) -> p q c", q=PAIR), ACT.Copy).then_inc(S["sT_ready"], 1)

            def vectors_out(n):
                act.wait_ge(S["m_done"], n + 1)
                act.wait_ge(S["lg_done"], n)
                go(m_sb[:, :, :], bank[0][:, 256:256 + PAIR * POOL].rearrange("p (q c) -> p q c", q=PAIR), ACT.Copy).then_inc(S["m_ready"], 1)

            def values_out(n):
                act.wait_ge(S["vv_done"], n + 1)
                act.wait_ge(S["rg_done"], PAIR * n)
                go(vv[:, :, :], bank[1][0:POOL, :].rearrange("p (q c) -> p q c", q=PAIR), ACT.Copy).then_inc(S["vv_ready"], 1)

            def soft_exp(n):
                act.wait_ge(S["ls_ready"], n + 1)
                act.wait_ge(S["at_ready"], n)
                go(ex[:, :, :], ls[:, :, :], ACT.Exp, scale=0.25).then_inc(S["ex_ready"], 1)

            def attention_out(b):
                act.wait_ge(S["atT_done"], b + 1)
                act.wait_ge(S["rg_done"], PAIR * b)
                go(atT[:, :], bank[3][0:POOL, :], ACT.Copy).then_inc(S["atT_ready"], 1)

            def gate_tanh(b, par):
                for q in range(PAIR):
                    act.wait_ge(S["rg_done"], PAIR * b + q + 1)
                    if q == 0:
                        act.wait_ge(S["fin_step"], FIN * b)
                    go(gate[:, q, :, :], bank[4 + 2 * par + q][:, :].rearrange("p (j c) -> p j c", j=TJ)[:, :, D:2 * D],
                       ACT.Tanh, scale=0.5).then_inc(S["gate_ready"], 1)

            chosen_out(0)
            vectors_out(0)
            values_out(0)
            soft_exp(0)

            def step2(b, par, half):
                if has(b, 1, NG):
                    chosen_out(b + 1)
                    vectors_out(b + 1)
                attention_out(b)
                if has(b, 1, NG):
                    soft_exp(b + 1)
                gate_tanh(b, par)
                if has(b, 2, NG):
                    act.dma_start(yTin[:, par, :, :], yTall[:, bass.ds(PAIR * (b + 2), PAIR), :]).then_inc(yT_in[par], 16)
                if has(b, 1, NG):
                    values_out(b + 1)

            steps(act, step2, NG)

        @block.vector
        def _(dve):
            v = nc.vector
            def stats(n, par, half):
                dve.wait_ge(x_in[par], 16 * (half + 1))
                for j in range(TJ):
                    v.bn_stats(st6[:, j, :], xall[:, bass.ds(n, 1), j, :].squeeze(1)).then_inc(S["stats"], 1)

            def mean_var(n):
                for j in range(TJ):
                    v.bn_aggr(mv[:, j, :], st6[:, j, :]).then_inc(S["mv_ready"], 1)

            stats(0, 0, 0)
            dve.wait_ge(S["stats"], TJ)
            mean_var(0)
            def out_of(t, dst, src, *scale):
                dve.wait_ge(S["w_T"], t + 1)
                if scale:
                    v.tensor_scalar(dst, src, scale[0], scale[1], ALU.mult, ALU.mult).then_inc(S["w_ev"], 1)
                else:
                    v.tensor_copy(dst, src).then_inc(S["w_ev"], 1)

            dve.wait_ge(S["in_w_in"], 16 * N_IN)
            for t in range(6):
                out_of(t, wt32[:, t * P:(t + 1) * P], w_bank(t)[:, 0:P], nw_col[:, :], WS)
            out_of(6, wt32[:, 6 * P:NIN], w_bank(6)[:, 0:HEADS], nw_col[:, :], WS)

            def small_weights():
                dve.wait_ge(S["small_in"], 16 * N_SMALL)
                v.tensor_scalar(cw[:, :, :], cw_ld[:, :, :], 1.0 / WS, None, ALU.mult).then_inc(S["w_dve"], 1)
                v.tensor_scalar(dhalf[:, :].rearrange("p (h d) -> p h d", h=HEADS),
                                dpar_bc[:, :].unsqueeze(2).broadcast_to([P, HEADS, HD]), 0.5, None, ALU.mult).then_inc(S["w_dve"], 1)
                v.memset(pre[:, :, 0:PAD], 0.0).then_inc(S["pads"], 1)
                v.tensor_scalar(sgn[:, :], s_bc[:, :], 0.0, None, ALU.is_gt).then_inc(S["w_small"], 1)
                v.tensor_scalar(sneg[:, :], s_bc[:, :], 0.0, None, ALU.is_lt).then_inc(S["w_small"], 1)
                dve.wait_ge(S["w_small"], 2)
                v.tensor_tensor(sgn[:, :], sgn[:, :], sneg[:, :], ALU.subtract).then_inc(S["w_small"], 1)
                dve.wait_ge(S["w_small"], 3)
                v.tensor_tensor(sabs[:, :], sgn[:, :], s_bc[:, :], ALU.mult).then_inc(S["w_small"], 1)
                v.tensor_scalar(c1[:, :], sgn[:, 1:2], 2.0 / H2S, None, ALU.mult).then_inc(S["w_small"], 1)
                v.tensor_scalar(c2[:, :], sgn[:, 1:2], -1.0 / H2S, None, ALU.mult).then_inc(S["w_small"], 1)
                dve.wait_ge(S["w_small"], 6)
                v.tensor_scalar(sprod[:, :], sabs[:, 0:1], sabs[:, 1:2], 4.0 * H2S, ALU.mult, ALU.mult).then_inc(S["w_small"], 1)
                dve.wait_ge(S["w_small"], 7)
                v.tensor_scalar(fhalf[:, :], s_bc[:, 2:3].broadcast_to([P, 2]), sprod[:, :], None, ALU.mult).then_inc(S["w_factor"], 1)
                dve.wait_ge(S["w_exp"], 1)
                v.tensor_scalar(negA[:, :], aexp[:, :], -1.0, None, ALU.mult).then_inc(S["w_small"], 1)

            def weights_out():
                dve.wait_ge(S["weights_in"], 16 * N_W)
                v.tensor_copy(sw2_bc[:, :], sw2_ld[:, :].broadcast_to([HID, P])).then_inc(S["w_mlp"], 1)
                out_of(7, out_wT[:, 0, :], w_bank(7)[:, 0:P], gw_col[:, 0:1], 1.0)
                out_of(8, out_wT[:, 1, :], w_bank(8)[:, 0:P], gw_col[:, 1:2], 1.0)
                out_of(9, sw1T[:, :], w_bank(9)[:, 0:HID])
                out_of(10, gate1T[:, :], w_bank(10)[:, 0:D])
                out_of(11, gate2T[:, :], w_bank(11)[:, 0:D])
                out_of(12, kwT[:, :], w_bank(12)[0:SDIM, 0:SDIM])
                out_of(13, vwT[:, :], w_bank(13)[0:SDIM, 0:D])

            def products_out():
                out_of(14, kp_sb[:, :], w_bank(14)[0:SDIM, 0:D])
                out_of(15, wvv[:, 0:D], w_bank(15)[:, 0:D])
                out_of(16, wv_sb[:, :], w_bank(16)[:, 0:D])
                out_of(17, wmT[:, :], w_bank(17)[:, 0:D])
                out_of(18, wvv[:, D:2 * D], w_bank(18)[:, 0:D])

            def mlp_weights():
                dve.wait_ge(S["mlp_in"], 16 * N_MLP)
                v.tensor_tensor(k0_d[:, :], k0_ld[:, 0, :], k0_ld[:, 1, :], ALU.subtract).then_inc(S["w_small"], 1)
                dve.wait_ge(S["w_small"], 9)
                v.tensor_scalar(k0_16[:, :], k0_d[:, :], sgn[:, 0:1], None, ALU.mult).then_inc(S["w_mlp"], 1)
                v.tensor_scalar(k1_16[:, :, :], k1_ld[:, :, :], c1[:, :], c2[:, :], ALU.mult, ALU.add).then_inc(S["w_mlp"], 1)
                v.tensor_scalar(k2_16[:, :, :], k2_ld[:, :, :], 2.0, -1.0, ALU.mult, ALU.add).then_inc(S["w_mlp"], 1)

            def normed(n):
                dve.wait_ge(S["norm_ready"], n + 1)
                dve.wait_ge(S["xT_done"], TJ * n)
                for j in range(TJ):
                    v.tensor_scalar(xn[:, j, :], xall[:, bass.ds(n, 1), j, :].squeeze(1), lt[:, 5, j:j + 1],
                                    lt[:, 6, j:j + 1], ALU.mult, ALU.add).then_inc(S["xn_ready"], 1)

            def xT_low(n, par):
                dve.wait_ge(S["xT_hi_ready"], n + 1)
                v.tensor_tensor(xT_lo[:, par, :], pA[:, 0:T], xT_hi[:, par, :], ALU.subtract).then_inc(S["xT_lo_ready"], 1)

            def dt_raw(n):
                dve.wait_ge(S["dt_done"], TJ * (n + 1))
                dve.wait_ge(S["sp_step"], SP_STEPS * n)
                dve.wait_ge(S["u_ready"], n)
                v.scalar_tensor_tensor(raw[:, :, :], pDT.rearrange("p (j h) -> p j h", j=TJ), 1.0 / WS,
                                       dtb_bc[:, :].unsqueeze(1).broadcast_to([P, TJ, HEADS]), ALU.mult, ALU.add).then_inc(S["raw_ready"], 1)
                r = raw[:, :, :].rearrange("p j h -> p (j h)")
                dve.wait_ge(S["raw_ready"], n + 1)
                v.tensor_scalar(sp[:, 0, :], r, 0.0, None, ALU.max).then_inc(S["abs_ready"], 1)
                v.scalar_tensor_tensor(sp[:, 1, :], r, -1.0, r, ALU.mult, ALU.min).then_inc(S["abs_ready"], 1)

            def dt_recip(n):
                dve.wait_ge(S["den_ready"], n + 1)
                v.reciprocal(sp[:, 4, :], sp[:, 3, :]).then_inc(S["rden_ready"], 1)

            def conv(n, half):
                dve.wait_ge(S["pre_ready"], 6 * n + 3 * half + 3)
                for k in range(PAD):
                    for i in range(2):
                        c = 2 * half + i
                        if k:
                            dve.wait_ge(S["conv_step"], 12 * n + 6 * half + 2 * k + i - 1)
                        v.scalar_tensor_tensor(acc[:, c, :], pre[:, c, k:k + T], cw[:, c, k:k + 1], acc[:, c, :],
                                               ALU.mult, ALU.add).then_inc(S["conv_step"], 1)

            def conv_silu(n, half):
                dve.wait_ge(S["cth_ready"], 2 * n + half + 1)
                dve.wait_ge(S[("xtok_done", "g_done")[half]], (4, 2)[half] * n)
                c = slice(2 * half, 2 * half + 2)
                v.scalar_tensor_tensor(xbc[:, c, :], cth[:, c, :], 1.0, acc[:, c, :], ALU.add, ALU.mult).then_inc(S["xbc_ready"], 1)

            def z_gate(n):
                dve.wait_ge(S["zth_ready"], n + 1)
                dve.wait_ge(S["yg_ready"], n)
                v.scalar_tensor_tensor(zg[:, :, :], zth[:, :, :], 1.0, pA[:, :].rearrange("p (j c) -> p j c", j=TJ),
                                       ALU.add, ALU.mult).then_inc(S["zg_ready"], 1)

            def hidden_low(b, layer, half):
                hi, lo = ((h1_hi, h1_lo), (h2_hi, h2_lo))[layer]
                dve.wait_ge(S[("h1_hi_ready", "h2_hi_ready")[layer]], 2 * b + half + 1)
                c = slice(2 * half, 2 * half + 2)
                v.scalar_tensor_tensor(lo[:, c, :], F[half][:, :].rearrange("p (c t) -> p c t", c=2), 0.0, hi[:, c, :],
                                       ALU.max, ALU.subtract).then_inc(S[("h1_lo_ready", "h2_lo_ready")[layer]], 1)

            def mixing(b, k):
                dve.wait_ge(S["decay_ready"], 3 * b + k + 1)
                dve.wait_ge(S["g_done"], 2 * b + 2)
                if k == 0:
                    dve.wait_ge(S["y_done"], b)
                v.tensor_tensor(mix[:, k, :, :], decay[:, k, :, :],
                                pG[:, k * P:(k + 1) * P].unsqueeze(1).broadcast_to([P, HEADS, P]), ALU.mult).then_inc(S["mix_ready"], 1)

            def gated(b):
                dve.wait_ge(S["y_done"], b + 1)
                dve.wait_ge(S["x_scaled"], 2 * b + 2)
                v.tensor_tensor(ysum[:, :, :], pY[:, :].rearrange("p (j c) -> p j c", j=TJ), xD[:, :, :], ALU.add).then_inc(S["ysum_ready"], 1)
                dve.wait_ge(S["ysum_ready"], b + 1)
                dve.wait_ge(S["zg_ready"], b + 1)
                dve.wait_ge(S["ygT_done"], 4 * b)
                dve.wait_ge(S["ss_ready"], 2 * b)
                v.tensor_tensor(yg[:, :, :], ysum[:, :, :], zg[:, :, :], ALU.mult).then_inc(S["yg_ready"], 1)

            def mlp_out(b):
                dve.wait_ge(S["gth_ready"], 2 * b + 2)
                dve.wait_ge(S["g_ready"], 2 * b)
                v.tensor_scalar(gth1[:, :, :], gth[:, :, :], 1.0, None, ALU.add).then_inc(S["gth1_ready"], 1)
                dve.wait_ge(S["gth1_ready"], b + 1)
                for j in range(TJ):
                    v.scalar_tensor_tensor(gall[:, bass.ds(b, 1), j, :].squeeze(1), F[0][:, j * D:(j + 1) * D],
                                           norms[:, 2, bass.ds(b, 1), j:j + 1].squeeze(1), gth1[:, j, :],
                                           ALU.mult, ALU.mult).then_inc(S["g_ready"], 1)

            normed(0)
            dve.wait_ge(S["w_split"], 1)
            v.tensor_tensor(wt_lo[:, :], wt32[:, :], wt_hi[:, :], ALU.subtract).then_inc(S["w_split"], 1)
            xT_low(0, 0)
            small_weights()
            dt_raw(0)
            stats(1, 1, 0)
            dve.wait_ge(S["stats"], 2 * TJ)
            dve.wait_ge(S["norm_kept"], 2)
            mean_var(1)
            dt_recip(0)
            mlp_weights()
            conv(0, 0)
            weights_out()
            conv_silu(0, 0)
            conv(0, 1)
            z_gate(0)
            products_out()
            conv_silu(0, 1)
            normed(1)

            def step(b, par, half):
                hidden_low(b, 0, 0)
                if has(b, 1):
                    xT_low(b + 1, 1 - par)
                if has(b, 2):
                    stats(b + 2, par, half + 1)
                if has(b, 1):
                    dt_raw(b + 1)
                if has(b, 2):
                    dve.wait_ge(S["stats"], TJ * (b + 3))
                    dve.wait_ge(S["norm_kept"], 2 * b + 4)
                if has(b, 1):
                    dt_recip(b + 1)
                if has(b, 2):
                    mean_var(b + 2)
                mixing(b, 0)
                hidden_low(b, 0, 1)
                if has(b, 1):
                    conv(b + 1, 0)
                hidden_low(b, 1, 0)
                mixing(b, 1)
                mixing(b, 2)
                hidden_low(b, 1, 1)
                if has(b, 1):
                    conv(b + 1, 1)
                    conv_silu(b + 1, 0)
                mlp_out(b)
                gated(b)
                if has(b, 1):
                    z_gate(b + 1)
                if has(b, 2):
                    normed(b + 2)
                if has(b, 1):
                    conv_silu(b + 1, 1)

            def last_step(b, par, half):
                mixing(b, 0)
                hidden_low(b, 0, 0)
                mixing(b, 1)
                hidden_low(b, 0, 1)
                mixing(b, 2)
                gated(b)
                hidden_low(b, 1, 0)
                hidden_low(b, 1, 1)
                mlp_out(b)

            steps(dve, step, last=last_step)

            k = 0

            def link(ins):
                nonlocal k
                k += 1
                ins.then_inc(S["sel_step"], 1)
                dve.wait_ge(S["sel_step"], k)

            link(v.memset(zero16[:, :], 0.0))
            dve.wait_ge(S["keys_in"], 16)
            link(v.tensor_scalar(keys[:, :], logit[:, :], SATURATED, None, ALU.min))
            cur = keys[:, :]
            for r in range(7):
                link(v.max(top8[:, r, :], cur))
                if r < 6:
                    link(v.match_replace(work[:, r % 2, :], top8[:, r, :], cur, -3.0e38))
                    cur = work[:, r % 2, :]
            kth = top8[:, 6, 1:2]
            link(v.tensor_scalar(gt[:, :], keys[:, :], kth, None, ALU.is_gt))
            link(v.tensor_scalar(eq[:, :], keys[:, :], kth, None, ALU.is_equal))
            link(v.tensor_reduce(col[:, 0:1], gt[:, :], AX, ALU.add))
            link(v.tensor_scalar(col[:, 1:2], col[:, 0:1], -1.0, float(POOL), ALU.mult, ALU.add))
            link(v.tensor_tensor_scan(eqc[:, :], eq[:, :], zero16[:, :], 0.0, ALU.add, ALU.add))
            link(v.tensor_scalar(ok[:, :], eqc[:, :], col[:, 1:2], None, ALU.is_le))
            link(v.tensor_tensor(ok[:, :], ok[:, :], eq[:, :], ALU.mult))
            link(v.tensor_tensor(sel[:, :], ok[:, :], gt[:, :], ALU.add))
            link(v.scalar_tensor_tensor(sel[:, :], keys[:, :], 0.0, sel[:, :], ALU.is_gt, ALU.mult))
            link(v.tensor_tensor_scan(selc[:, :], sel[:, :], zero16[:, :], 0.0, ALU.add, ALU.add))
            link(v.tensor_tensor(slot[:, :], selc[:, :], sel[:, :], ALU.mult))
            dve.wait_ge(S["th16_ready"], 1)
            link(v.tensor_scalar(col[:, 2:3], col[:, 4:5], 0.5 / T, 0.5, ALU.mult, ALU.add))
            link(v.tensor_scalar(col[:, 3:4], col[:, 2:3], 0.3, 0.5, ALU.is_gt, ALU.mult))
            link(v.scalar_tensor_tensor(col[:, 5:6], selc[:, T - 1:T], 0.0, col[:, 3:4], ALU.is_gt, ALU.mult))
            link(v.tensor_scalar(diag2[:, 0, :], ident[0:NB, 0:NB], selc[:, T - 1:T], None, ALU.mult))
            v.tensor_scalar(diag2[:, 1, :], ident[0:NB, 0:NB], col[:, 5:6], None, ALU.mult).then_inc(S["slots_done"], 1)
            dve.wait_ge(S["slotT_done"], 3)
            v.tensor_copy(slotT[:, :, :], bank[0][:, 0:TJ * NB].rearrange("p (j b) -> p j b", j=TJ)).then_inc(S["slotT_ready"], 1)
            v.tensor_copy(cnt_rm[:, :, :], bank[1][:, 0:2 * NB].rearrange("p (a b) -> p a b", a=2)).then_inc(S["slotT_ready"], 1)
            dve.wait_ge(S["slotT_ready"], 2)

            def choose(n):
                c = bass.ds(PAIR * n, PAIR)
                dve.wait_ge(S["s_done"], n)
                for j in range(TJ):
                    v.tensor_tensor(onehot[:, j, :, :], slots[:, :].unsqueeze(1).broadcast_to([P, PAIR, POOL]),
                                    slotT[:, j, c].unsqueeze(2).broadcast_to([P, PAIR, POOL]), ALU.is_equal)\
                        .then_inc(S[("choose_step", "onehot_ready")[j]], 1)
                v.tensor_tensor(pover[:, :, :], slots[:, :].unsqueeze(1).broadcast_to([P, PAIR, POOL]),
                                cnt_rm[:, 0, c].unsqueeze(2).broadcast_to([P, PAIR, POOL]), ALU.is_gt).then_inc(S["bias_ready"], 1)

            def softmax_in(n):
                dve.wait_ge(S["lg_done"], n + 1)
                dve.wait_ge(S["bias_ready"], n + 1)
                for q in range(PAIR):
                    v.scalar_tensor_tensor(lm[:, q * TJ:(q + 1) * TJ, :], pover[:, q, :].unsqueeze(1).broadcast_to([P, TJ, POOL]), -4.0e9,
                                           bank[2][:, q * TJ * POOL:(q + 1) * TJ * POOL].rearrange("p (j c) -> p j c", j=TJ),
                                           ALU.mult, ALU.add).then_inc(S[("lm_step", "lm_ready")[q]], 1)
                dve.wait_ge(S["lm_step"], n + 1)
                dve.wait_ge(S["lm_ready"], n + 1)
                v.tensor_reduce(mx[:, :], lm[:, :, :], AX, ALU.max).then_inc(S["max_ready"], 1)
                dve.wait_ge(S["max_ready"], n + 1)
                dve.wait_ge(S["ex_ready"], n)
                v.tensor_tensor(ls[:, :, :], lm[:, :, :], mx[:, :].unsqueeze(2).broadcast_to([P, PAIR * TJ, POOL]), ALU.subtract).then_inc(S["ls_ready"], 1)

            def softmax_out(n):
                dve.wait_ge(S["ex_ready"], n + 1)
                v.tensor_reduce(sm[:, :], ex[:, :, :], AX, ALU.add).then_inc(S["sum_ready"], 1)
                dve.wait_ge(S["sum_ready"], n + 1)
                v.reciprocal(rec[:, :], sm[:, :]).then_inc(S["rec_ready"], 1)
                dve.wait_ge(S["rec_ready"], n + 1)
                dve.wait_ge(S["atT_done"], n)
                v.tensor_tensor(at[:, :, :], ex[:, :, :], rec[:, :].unsqueeze(2).broadcast_to([P, PAIR * TJ, POOL]), ALU.mult).then_inc(S["at_ready"], 1)

            def finish(b, par, half):
                pair = bass.ds(PAIR * b, PAIR)
                dve.wait_ge(S["base_step"], 3 * b + 3)
                for q in range(PAIR):
                    dve.wait_ge(S["gate_ready"], PAIR * b + q + 1)
                    v.scalar_tensor_tensor(fin[:, 0, q, :, :], gate[:, q, :, :], 1.0,
                                           bank[4 + 2 * par + q][:, :].rearrange("p (j c) -> p j c", j=TJ)[:, :, 0:D],
                                           ALU.add, ALU.mult).then_inc(S["fin_step"], 1)
                dve.wait_ge(S["fin_step"], FIN * b + PAIR)
                for q in range(PAIR):
                    v.scalar_tensor_tensor(fin[:, 1, q, :, :], fin[:, 0, q, :, :], cnt_rm[:, 1, bass.ds(PAIR * b + q, 1)],
                                           base[:, par, q, :, :], ALU.mult, ALU.add).then_inc(S["fin_step"], 1)
                dve.wait_ge(S["fin_step"], FIN * b + 2 * PAIR)
                v.tensor_tensor(fin[:, 2, :, :, :].rearrange("p q j c -> p (q j c)"), fin[:, 1, :, :, :].rearrange("p q j c -> p (q j c)"),
                                gall[:, pair, :, :].rearrange("p q j c -> p (q j c)"), ALU.mult).then_inc(S["fin_step"], 1)
                dve.wait_ge(S["fin_step"], FIN * b + 2 * PAIR + 1)
                dve.wait_ge(out_done[par], 16 * half)
                v.tensor_tensor(obuf[:, par, :, :, :].rearrange("p q j c -> p (q j c)"), fin[:, 2, :, :, :].rearrange("p q j c -> p (q j c)"),
                                xall[:, pair, :, :].rearrange("p q j c -> p (q j c)"), ALU.add).then_inc(S["out_ready"], 1)

            choose(0)
            softmax_in(0)
            choose(1)
            softmax_out(0)

            def step2(b, par, half):
                if has(b, 1, NG):
                    softmax_in(b + 1)
                if has(b, 2, NG):
                    choose(b + 2)
                if has(b, 1, NG):
                    softmax_out(b + 1)
                finish(b, par, half)

            steps(dve, step2, NG)

        @block.gpsimd
        def _(pool):
            g = nc.gpsimd
            g.memset(ident[:, :], 0.0).then_inc(S["setup_step"], 1)
            pool.wait_ge(S["setup_step"], 1)
            g.affine_select(out=ident[:, :], in_=ident[:, :], compare_op=ALU.not_equal, fill=1.0, base=0,
                            pattern=[[-1, P]], channel_multiplier=1).then_inc(S["consts"], 1)
            for c, value in enumerate(NUMS.values()):
                g.memset(nums[:, c:c + 1], value).then_inc(S["setup_step"], 1)
            pool.wait_ge(S["consts"], 1)
            pool.wait_ge(S["setup_step"], 1 + len(NUMS))

            def constants():
                k = 1 + len(NUMS)
                g.memset(upto[:, :], 1.0).then_inc(S["setup_step"], 1)
                g.memset(mask[:, :, :], 0.0).then_inc(S["setup_step"], 1)
                g.memset(minus_head[:, :, :], -1.0).then_inc(S["setup_step"], 1)
                g.tensor_copy(ident_bf[:, :], ident[:, :]).then_inc(S["consts"], 1)
                g.memset(ones32[:, :], 1.0).then_inc(S["consts"], 1)
                g.memset(ones3[:, :], 1.0).then_inc(S["consts"], 1)
                pool.wait_ge(S["setup_step"], k + 3)
                g.affine_select(out=upto[:, 0:P], in_=upto[:, 0:P], compare_op=ALU.is_ge, fill=0.0, base=0,
                                pattern=[[1, P]], channel_multiplier=-1).then_inc(S["consts"], 1)
                g.affine_select(out=mask[:, :, :], in_=mask[:, :, :], compare_op=ALU.is_ge, fill=NEG, base=0,
                                pattern=[[0, HEADS], [1, P]], channel_multiplier=-1).then_inc(S["consts"], 1)
                g.affine_select(out=minus_head[:, :, :], in_=minus_head[:, :, :], compare_op=ALU.is_ge, fill=0.0,
                                base=0, pattern=[[-3, HEADS], [0, P]], channel_multiplier=1).then_inc(S["setup_step"], 1)
                pool.wait_ge(S["setup_step"], k + 4)
                g.affine_select(out=minus_head[:, :, :], in_=minus_head[:, :, :], compare_op=ALU.is_ge, fill=0.0,
                                base=2, pattern=[[3, HEADS], [0, P]], channel_multiplier=-1).then_inc(S["setup_step"], 1)
                pool.wait_ge(S["setup_step"], k + 5)
                g.iota(slots[:, :], pattern=[[1, POOL]], base=1, channel_multiplier=0,
                       allow_small_or_imprecise_dtypes=True).then_inc(S["consts"], 1)

            def norm(n):
                k = 0

                def link(ins):
                    nonlocal k
                    k += 1
                    ins.then_inc(S["ln_step"], 1)
                    pool.wait_ge(S["ln_step"], LN_STEPS * n + k)

                pool.wait_ge(S["mv_ready"], TJ * (n + 1))
                pool.wait_ge(S["xn_ready"], TJ * n)
                mean, var = mv[:, :, 0], mv[:, :, 1]
                link(g.tensor_tensor(lt[:, 0, :], var, num("eps", P, TJ), ALU.add))
                link(g.tensor_tensor(lnw[:, 0, :], lt[:, 0, :], num("-1/2", P, TJ), ALU.pow))
                link(g.tensor_tensor(lt[:, 1, :], var, lnw[:, 0, :], ALU.mult))
                link(g.tensor_tensor(lt[:, 2, :], lt[:, 1, :], lnw[:, 0, :], ALU.mult))
                link(g.tensor_tensor(lt[:, 2, :], lt[:, 2, :], num("eps", P, TJ), ALU.add))
                link(g.tensor_tensor(lt[:, 3, :], lt[:, 2, :], num("-1/2", P, TJ), ALU.pow))
                link(g.tensor_tensor(lt[:, 5, :], lnw[:, 0, :], lt[:, 3, :], ALU.mult))
                link(g.tensor_tensor(lt[:, 7, :], mean, num("-1", P, TJ), ALU.mult))
                link(g.tensor_tensor(lnw[:, 1, :], lt[:, 7, :], lnw[:, 0, :], ALU.mult))
                g.tensor_tensor(lt[:, 6, :], lnw[:, 1, :], lt[:, 3, :], ALU.mult).then_inc(S["norm_ready"], 1)
                link(g.tensor_tensor(lt[:, 4, :], lt[:, 2, :], num("1/2", P, TJ), ALU.pow))
                if not has(n, -1):
                    constants()
                    pool.wait_ge(S["w_factor"], 1)
                g.tensor_tensor(lnw[:, 2, :], lt[:, 4, :], fhalf[:, :], ALU.mult).then_inc(S["norm_kept"], 1)
                pool.wait_ge(S["norm_kept"], 2 * n + 1)
                g.tensor_tensor(norms[:, :, bass.ds(n, 1), :].squeeze(2), lnw[:, :, :], num("1", P, 3, TJ), ALU.mult).then_inc(S["norm_kept"], 1)
                assert k == LN_STEPS

            def scale_x(b):
                pool.wait_ge(S["xtok_ready"], b + 1)
                pool.wait_ge(S["y_done"], b)
                g.tensor_tensor(dtx[:, :, :].rearrange("p j (h d) -> p (j h) d", h=HEADS),
                                xtok[:, :, :].rearrange("p j (h d) -> p (j h) d", h=HEADS),
                                dt8[:, :].unsqueeze(2).broadcast_to([P, TJ * HEADS, HD]), ALU.mult).then_inc(S["x_scaled"], 1)

            def skip_x(b):
                pool.wait_ge(S["ysum_ready"], b)
                g.tensor_tensor(xD[:, :, :], xtok[:, :, :], dhalf[:, :].unsqueeze(1).broadcast_to([P, TJ, DI]), ALU.mult).then_inc(S["x_scaled"], 1)

            def softplus(n):
                k = 0

                def link(ins):
                    nonlocal k
                    k += 1
                    ins.then_inc(S["sp_step"], 1)
                    pool.wait_ge(S["sp_step"], SP_STEPS * n + k)

                W = TJ * HEADS
                pool.wait_ge(S["u_ready"], n + 1)
                g.tensor_tensor(sp[:, 3, :], sp[:, 2, :], num("2", P, W), ALU.add).then_inc(S["den_ready"], 1)
                pool.wait_ge(S["rden_ready"], n + 1)
                link(g.tensor_tensor(sp[:, 5, :], sp[:, 2, :], sp[:, 4, :], ALU.mult))
                link(g.tensor_tensor(sp[:, 6, :], sp[:, 5, :], sp[:, 5, :], ALU.mult))
                link(g.tensor_tensor(sp[:, 7, :], sp[:, 6, :], num(f"atanh{ATANH_TERMS - 1}", P, W), ALU.mult))
                for t in range(ATANH_TERMS - 2, -1, -1):
                    link(g.tensor_tensor(sp[:, 7, :], sp[:, 7, :], num(f"atanh{t}", P, W), ALU.add))
                    link(g.tensor_tensor(sp[:, 7, :], sp[:, 7, :], sp[:, 6 if t else 5, :], ALU.mult))
                link(g.tensor_tensor(sp[:, 8, :], sp[:, 0, :], sp[:, 7, :], ALU.add))
                pool.wait_ge(S["cum_done"], n)
                g.tensor_tensor(a_sb[:, :].rearrange("p (j h) -> p j h", j=TJ), sp[:, 8, :].rearrange("p (j h) -> p j h", j=TJ),
                                negA[:, :].unsqueeze(1).broadcast_to([P, TJ, HEADS]), ALU.mult).then_inc(S["a_ready"], 1)
                g.tensor_tensor(dt8[:, :], sp[:, 8, :], num("1/8", P, W), ALU.mult).then_inc(S["dt8_ready"], 1)
                assert k == SP_STEPS

            def split_cum(n):
                pool.wait_ge(S["craw_ready"], 2 * n + 2)
                pool.wait_ge(S["rows_in"], 64 * n)
                g.tensor_tensor(cres[:, :], craw[:, :], parts[:, 0, :], ALU.subtract).then_inc(S["parts_step"], 1)
                pool.wait_ge(S["parts_step"], PART_STEPS * n + 1)
                g.tensor_tensor(parts[:, 1, :], cres[:, :], num("1", HEADS, T), ALU.mult).then_inc(S["parts_step"], 1)
                pool.wait_ge(S["seg_done"], 3 * n)
                pool.wait_ge(S["parts_step"], PART_STEPS * n + 2)
                g.tensor_tensor(parts[:, 2, :], cres[:, :], parts[:, 1, :], ALU.subtract).then_inc(S["parts_ready"], 1)

            def rms(b):
                pool.wait_ge(S["ss_ready"], 2 * b + 2)
                g.tensor_tensor(rt[:, :], ss[:, :], num("1/DI", P, TJ), ALU.mult).then_inc(S["rstd_step"], 1)
                pool.wait_ge(S["rstd_step"], 2 * b + 1)
                g.tensor_tensor(rt[:, :], rt[:, :], num("rms eps", P, TJ), ALU.add).then_inc(S["rstd_step"], 1)
                pool.wait_ge(S["rstd_step"], 2 * b + 2)
                pool.wait_ge(S["y_ready"], 2 * b)
                g.tensor_tensor(rstd[:, :], rt[:, :], num("-1/2", P, TJ), ALU.pow).then_inc(S["rstd_ready"], 1)

            norm(0)
            pool.wait_ge(S["w_dve"], 2)
            pool.wait_ge(S["w_small"], 8)
            softplus(0)
            norm(1)
            split_cum(0)

            def step(b, par, half):
                pool.wait_ge(S["dt8_ready"], b + 1)
                scale_x(b)
                if has(b, -1):
                    rms(b - 1)
                skip_x(b)
                if has(b, 1):
                    softplus(b + 1)
                if has(b, 2):
                    norm(b + 2)
                if has(b, 1):
                    split_cum(b + 1)

            steps(pool, step)
            rms(NB - 1)

            def base_sum(b, par, half):
                pair = bass.ds(PAIR * b, PAIR)
                pool.wait_ge(y_in[par], 16 * (half + 1))
                if has(b, -1, NG):
                    pool.wait_ge(S["fin_step"], FIN * (b - 1))
                flat = "p q j d -> p (q j) d"
                k = PAIR * TJ
                g.tensor_tensor(base[:, par, :, :, :].rearrange(flat), xall[:, pair, :, :].rearrange(flat),
                                norms[:, 0, pair, :].rearrange("p q j -> p (q j)").unsqueeze(2).broadcast_to([P, k, D]), ALU.mult).then_inc(S["base_step"], 1)
                pool.wait_ge(S["base_step"], 3 * b + 1)
                g.tensor_tensor(base[:, par, :, :, :].rearrange(flat), base[:, par, :, :, :].rearrange(flat),
                                norms[:, 1, pair, :].rearrange("p q j -> p (q j)").unsqueeze(2).broadcast_to([P, k, D]), ALU.add).then_inc(S["base_step"], 1)
                pool.wait_ge(S["base_step"], 3 * b + 2)
                pool.wait_ge(S["s_done"], b + 1)
                g.tensor_tensor(base[:, par, :, :, :], base[:, par, :, :, :], yin[:, par, :, :, :], ALU.add).then_inc(S["base_step"], 1)

            steps(pool, base_sum, NG)


_INS = ['x', 'norm_w', 'in_w', 'conv_w', 'conv_b', 'dt_bias', 'A_log', 'D_param', 'gnorm_w', 'out_w',
        'scorer_w1', 'scorer_w2', 'summ_w', 'q_w', 'k_w', 'v_w', 'gate_w']
_FFN = ['k0', 'k1', 'k2', 's0', 's1', 's2']


def kernel(**inputs):
    import numpy as _np
    import concourse.bacc as _bacc
    from concourse import mybir as _mybir
    from concourse.bass_utils import run_bass_kernel_spmd as _run

    nc = _bacc.Bacc("TRN2", target_bir_lowering=False, num_devices=1)
    arrays, args = {}, []
    for name in [f"L0_attn_{n}" for n in _INS] + [f"L0_ffn_{n}" for n in _FFN]:
        a = _np.ascontiguousarray(inputs[name])
        if a.ndim == 0:
            a = a.reshape(1)
        arrays[f"in_{name}"] = a
        args.append(nc.dram_tensor(f"in_{name}", a.shape, _mybir.dt.from_np(a.dtype), kind="ExternalInput").ap())
    args.append(nc.dram_tensor("out_0", (NB, T, D), _mybir.dt.float32, kind="ExternalOutput").ap())
    layer_kernel(nc, *args)
    r = _run(nc, [arrays], core_ids=[0])
    return r.results[0]["out_0"]
```
